# Optimizing a Trainium2 kernel written in Bass

```python
import numpy as np
import jax
import jax.numpy as jnp

def _softmax(x, axis=-1):
    return jax.nn.softmax(x, axis=axis)

def _gelu(x):
    return jax.nn.gelu(x, approximate=True)

def _silu(x):
    return jax.nn.silu(x)

def _sigmoid(x):
    return jax.nn.sigmoid(x)

def _layernorm(x, axis=-1, eps=1e-05):
    m = jnp.mean(x, axis=axis, keepdims=True)
    v = jnp.var(x, axis=axis, keepdims=True)
    return (x - m) / jnp.sqrt(v + eps)

def _scatter_add(tgt, idx, src, axis=0):
    return tgt.at[idx].add(src)

def _segment_sum(src, seg, n):
    return jax.ops.segment_sum(src, seg, n)
kernel_name = 'mk_seq_preln_d1_jaxref_r4_90b7c3'

def setup_inputs(seed: int=0):
    np.random.seed(seed)
    _w = jnp.asarray

    def _L0_attn_setup():
        import jax, jax.numpy as jnp
        import numpy as np
        EPS = 1e-06

        def layernorm(x, alpha, bias):
            mean = x.mean(axis=-1, keepdims=True)
            std = jnp.std(x, axis=-1, keepdims=True, ddof=1)
            return alpha * (x - mean) / (std + EPS) + bias
        key = jax.random.key(seed)
        B, L, d_model = (2, 256, 256)
        d_state, d_conv, expand = (16, 4, 2)
        d_inner = expand * d_model
        ks = jax.random.split(key, 8)
        std = 0.02
        x = jax.random.normal(ks[0], (B, L, d_model), dtype=jnp.float32)
        in_proj_w = jax.random.normal(ks[1], (2 * d_inner, d_model), dtype=jnp.float32) * std
        in_proj_b = jnp.zeros((2 * d_inner,), jnp.float32)
        conv_w = jax.random.normal(ks[2], (d_inner, 1, d_conv), dtype=jnp.float32) * std
        conv_b = jnp.zeros((d_inner,), jnp.float32)
        x_proj_w = jax.random.normal(ks[3], (2 * d_state, d_inner), dtype=jnp.float32) * std
        x_proj_b = jnp.zeros((2 * d_state,), jnp.float32)
        dt_proj_w = jax.random.normal(ks[4], (d_inner, d_inner), dtype=jnp.float32) * std
        dt_proj_b = jnp.zeros((d_inner,), jnp.float32)
        A_log = jnp.log(jnp.tile(jnp.arange(1, d_state + 1, dtype=jnp.float32), (d_inner, 1)))
        D = jnp.ones((d_inner,), jnp.float32)
        out_proj_w = jax.random.normal(ks[5], (d_model, d_inner), dtype=jnp.float32) * std
        out_proj_b = jnp.zeros((d_model,), jnp.float32)
        in_norm_alpha = jnp.ones((d_model,), jnp.float32)
        in_norm_bias = jnp.zeros((d_model,), jnp.float32)
        norm_alpha = jnp.ones((d_model,), jnp.float32)
        norm_bias = jnp.zeros((d_model,), jnp.float32)
        return {'x': x, 'in_proj_w': in_proj_w, 'in_proj_b': in_proj_b, 'conv_w': conv_w, 'conv_b': conv_b, 'x_proj_w': x_proj_w, 'x_proj_b': x_proj_b, 'dt_proj_w': dt_proj_w, 'dt_proj_b': dt_proj_b, 'A_log': A_log, 'D': D, 'out_proj_w': out_proj_w, 'out_proj_b': out_proj_b, 'in_norm_alpha': in_norm_alpha, 'in_norm_bias': in_norm_bias, 'norm_alpha': norm_alpha, 'norm_bias': norm_bias}
    _L0_attn_in = _L0_attn_setup()

    def _L0_ffn_setup():
        import jax, jax.numpy as jnp
        import numpy as np
        D_MODEL = 256
        N_HEADS = 16
        HEAD_DIM = D_MODEL // N_HEADS
        KV_LATENT = 128
        N_EXPERTS = 4
        D_HIDDEN = 4 * D_MODEL
        B, T = (2, 256)

        def rmsnorm(x, w, eps=1e-06):
            return w * (x * jax.lax.rsqrt(jnp.mean(x * x, axis=-1, keepdims=True) + eps))

        def layernorm(x, g, b, eps=1e-05):
            mu = jnp.mean(x, axis=-1, keepdims=True)
            var = jnp.mean((x - mu) ** 2, axis=-1, keepdims=True)
            return (x - mu) * jax.lax.rsqrt(var + eps) * g + b

        def apply_rope(x):
            t, d = (x.shape[2], x.shape[3])
            half = d // 2
            pos = jnp.arange(t, dtype=x.dtype)[:, None]
            inv_freq = 1.0 / 10000.0 ** (jnp.arange(half, dtype=x.dtype) / half)
            ang = pos * inv_freq[None, :]
            sin, cos = (jnp.sin(ang), jnp.cos(ang))
            x1, x2 = (x[..., :half], x[..., half:])
            return jnp.concatenate([x1 * cos - x2 * sin, x1 * sin + x2 * cos], axis=-1)

        def mla_attention(x, Wq, Wdkv, Wuk, Wuv, Wo, ln_g, ln_b):
            b, t, _ = x.shape
            q = (x @ Wq.T).reshape(b, t, N_HEADS, HEAD_DIM).transpose(0, 2, 1, 3)
            latent = layernorm(x @ Wdkv.T, ln_g, ln_b)
            k = (latent @ Wuk.T).reshape(b, t, N_HEADS, HEAD_DIM).transpose(0, 2, 1, 3)
            v = (latent @ Wuv.T).reshape(b, t, N_HEADS, HEAD_DIM).transpose(0, 2, 1, 3)
            q = apply_rope(q)
            k = apply_rope(k)
            scores = jnp.einsum('bhqd,bhkd->bhqk', q, k) / np.sqrt(HEAD_DIM)
            causal = jnp.tril(jnp.ones((t, t), dtype=bool))
            scores = jnp.where(causal, scores, -jnp.inf)
            attn = jax.nn.softmax(scores, axis=-1)
            out = jnp.einsum('bhqk,bhkd->bhqd', attn, v).transpose(0, 2, 1, 3).reshape(b, t, D_MODEL)
            return out @ Wo.T

        def moe(x, gate_w, gate_b, W1, b1, W2, b2):
            logits = x @ gate_w.T + gate_b
            top = jnp.argmax(logits, axis=-1)
            onehot = jax.nn.one_hot(top, N_EXPERTS, dtype=x.dtype)
            h = jax.nn.relu(jnp.einsum('btd,ehd->bteh', x, W1) + b1)
            y = jnp.einsum('bteh,edh->bted', h, W2) + b2
            return jnp.einsum('bted,bte->btd', y, onehot)
        key = jax.random.key(seed)
        ks = jax.random.split(key, 16)
        s = lambda fan_in: 1.0 / np.sqrt(fan_in)
        return {'x': jax.random.normal(ks[0], (B, T, D_MODEL), jnp.float32), 'norm1_w': jnp.ones((D_MODEL,), jnp.float32), 'norm2_w': jnp.ones((D_MODEL,), jnp.float32), 'Wq': jax.random.normal(ks[1], (D_MODEL, D_MODEL), jnp.float32) * s(D_MODEL), 'Wdkv': jax.random.normal(ks[2], (KV_LATENT, D_MODEL), jnp.float32) * s(D_MODEL), 'Wuk': jax.random.normal(ks[3], (D_MODEL, KV_LATENT), jnp.float32) * s(KV_LATENT), 'Wuv': jax.random.normal(ks[4], (D_MODEL, KV_LATENT), jnp.float32) * s(KV_LATENT), 'Wo': jax.random.normal(ks[5], (D_MODEL, D_MODEL), jnp.float32) * s(D_MODEL), 'ln_g': jnp.ones((KV_LATENT,), jnp.float32), 'ln_b': jnp.zeros((KV_LATENT,), jnp.float32), 'gate_w': jax.random.normal(ks[6], (N_EXPERTS, D_MODEL), jnp.float32) * s(D_MODEL), 'gate_b': jnp.zeros((N_EXPERTS,), jnp.float32), 'W1': jax.random.normal(ks[7], (N_EXPERTS, D_HIDDEN, D_MODEL), jnp.float32) * s(D_MODEL), 'b1': jnp.zeros((N_EXPERTS, D_HIDDEN), jnp.float32), 'W2': jax.random.normal(ks[8], (N_EXPERTS, D_MODEL, D_HIDDEN), jnp.float32) * s(D_HIDDEN), 'b2': jnp.zeros((N_EXPERTS, D_MODEL), jnp.float32)}
    _L0_ffn_in = _L0_ffn_setup()
    _d = {'L0_attn_x': _L0_attn_in['x'], 'L0_attn_in_proj_w': _L0_attn_in['in_proj_w'], 'L0_attn_in_proj_b': _L0_attn_in['in_proj_b'], 'L0_attn_conv_w': _L0_attn_in['conv_w'], 'L0_attn_conv_b': _L0_attn_in['conv_b'], 'L0_attn_x_proj_w': _L0_attn_in['x_proj_w'], 'L0_attn_x_proj_b': _L0_attn_in['x_proj_b'], 'L0_attn_dt_proj_w': _L0_attn_in['dt_proj_w'], 'L0_attn_dt_proj_b': _L0_attn_in['dt_proj_b'], 'L0_attn_A_log': _L0_attn_in['A_log'], 'L0_attn_D': _L0_attn_in['D'], 'L0_attn_out_proj_w': _L0_attn_in['out_proj_w'], 'L0_attn_out_proj_b': _L0_attn_in['out_proj_b'], 'L0_attn_in_norm_alpha': _L0_attn_in['in_norm_alpha'], 'L0_attn_in_norm_bias': _L0_attn_in['in_norm_bias'], 'L0_attn_norm_alpha': _L0_attn_in['norm_alpha'], 'L0_attn_norm_bias': _L0_attn_in['norm_bias'], 'L0_ffn_norm1_w': _L0_ffn_in['norm1_w'], 'L0_ffn_norm2_w': _L0_ffn_in['norm2_w'], 'L0_ffn_Wq': _L0_ffn_in['Wq'], 'L0_ffn_Wdkv': _L0_ffn_in['Wdkv'], 'L0_ffn_Wuk': _L0_ffn_in['Wuk'], 'L0_ffn_Wuv': _L0_ffn_in['Wuv'], 'L0_ffn_Wo': _L0_ffn_in['Wo'], 'L0_ffn_ln_g': _L0_ffn_in['ln_g'], 'L0_ffn_ln_b': _L0_ffn_in['ln_b'], 'L0_ffn_gate_w': _L0_ffn_in['gate_w'], 'L0_ffn_gate_b': _L0_ffn_in['gate_b'], 'L0_ffn_W1': _L0_ffn_in['W1'], 'L0_ffn_b1': _L0_ffn_in['b1'], 'L0_ffn_W2': _L0_ffn_in['W2'], 'L0_ffn_b2': _L0_ffn_in['b2']}
    _x0 = _d['L0_attn_x']
    _d['L0_attn_x'] = jax.random.normal(jax.random.fold_in(jax.random.key(seed), 1), (2, 2048, 256), dtype=_x0.dtype)
    del _x0
    return _d

def reference(L0_attn_x, L0_attn_in_proj_w, L0_attn_in_proj_b, L0_attn_conv_w, L0_attn_conv_b, L0_attn_x_proj_w, L0_attn_x_proj_b, L0_attn_dt_proj_w, L0_attn_dt_proj_b, L0_attn_A_log, L0_attn_D, L0_attn_out_proj_w, L0_attn_out_proj_b, L0_attn_in_norm_alpha, L0_attn_in_norm_bias, L0_attn_norm_alpha, L0_attn_norm_bias, L0_ffn_norm1_w, L0_ffn_norm2_w, L0_ffn_Wq, L0_ffn_Wdkv, L0_ffn_Wuk, L0_ffn_Wuv, L0_ffn_Wo, L0_ffn_ln_g, L0_ffn_ln_b, L0_ffn_gate_w, L0_ffn_gate_b, L0_ffn_W1, L0_ffn_b1, L0_ffn_W2, L0_ffn_b2):

    def _L0_attn_ref(x, in_proj_w, in_proj_b, conv_w, conv_b, x_proj_w, x_proj_b, dt_proj_w, dt_proj_b, A_log, D, out_proj_w, out_proj_b, in_norm_alpha, in_norm_bias, norm_alpha, norm_bias):
        import jax, jax.numpy as jnp
        import numpy as np
        EPS = 1e-06

        def layernorm(x, alpha, bias):
            mean = x.mean(axis=-1, keepdims=True)
            std = jnp.std(x, axis=-1, keepdims=True, ddof=1)
            return alpha * (x - mean) / (std + EPS) + bias
        batch, L, d_model = x.shape
        d_inner = D.shape[0]
        d_state = A_log.shape[1]
        d_conv = conv_w.shape[-1]
        residual = x
        xn = layernorm(x, in_norm_alpha, in_norm_bias)
        xz = xn @ in_proj_w.T + in_proj_b
        x_in, z = jnp.split(xz, 2, axis=-1)
        xc = jnp.swapaxes(x_in, 1, 2)
        xc = jax.lax.conv_general_dilated(xc, conv_w, window_strides=(1,), padding=[(d_conv - 1, 0)], dimension_numbers=('NCH', 'OIH', 'NCH'), feature_group_count=d_inner) + conv_b[None, :, None]
        xc = jax.nn.silu(jnp.swapaxes(xc, 1, 2))
        Bmat, Cmat = jnp.split(xc @ x_proj_w.T + x_proj_b, 2, axis=-1)
        delta = jnp.clip(jax.nn.softplus(xc @ dt_proj_w.T + dt_proj_b), 0.0001, 10.0)
        A = -jnp.exp(A_log)
        flags = jnp.arange(L) % 16 == 15

        def step(h, inp):
            d_t, B_t, C_t, x_t, flag = inp
            dA = jnp.exp(jnp.clip(d_t[..., None] * A, -10.0, 0.0))
            dBx = d_t[..., None] * B_t[:, None, :] * x_t[..., None]
            h = dA * h + dBx
            hn = jnp.maximum(jnp.linalg.norm(h, axis=-1, keepdims=True), 1e-06)
            scale = jnp.where(hn > 10.0, 10.0 / hn, 1.0)
            h = jnp.where(flag, h * scale, h)
            y_t = jnp.sum(C_t[:, None, :] * h, axis=-1) + D * x_t
            return (h, y_t)
        h0 = jnp.zeros((batch, d_inner, d_state), dtype=x.dtype)
        xs = (jnp.swapaxes(delta, 0, 1), jnp.swapaxes(Bmat, 0, 1), jnp.swapaxes(Cmat, 0, 1), jnp.swapaxes(xc, 0, 1), flags)
        _, ys = jax.lax.scan(step, h0, xs)
        y = jnp.swapaxes(ys, 0, 1)
        y = y * jax.nn.silu(z)
        out = y @ out_proj_w.T + out_proj_b
        return layernorm(residual + out, norm_alpha, norm_bias)

    def _L0_ffn_ref(x, norm1_w, norm2_w, Wq, Wdkv, Wuk, Wuv, Wo, ln_g, ln_b, gate_w, gate_b, W1, b1, W2, b2):
        import jax, jax.numpy as jnp
        import numpy as np
        D_MODEL = 256
        N_HEADS = 16
        HEAD_DIM = D_MODEL // N_HEADS
        KV_LATENT = 128
        N_EXPERTS = 4
        D_HIDDEN = 4 * D_MODEL
        B, T = (2, 256)

        def rmsnorm(x, w, eps=1e-06):
            return w * (x * jax.lax.rsqrt(jnp.mean(x * x, axis=-1, keepdims=True) + eps))

        def layernorm(x, g, b, eps=1e-05):
            mu = jnp.mean(x, axis=-1, keepdims=True)
            var = jnp.mean((x - mu) ** 2, axis=-1, keepdims=True)
            return (x - mu) * jax.lax.rsqrt(var + eps) * g + b

        def apply_rope(x):
            t, d = (x.shape[2], x.shape[3])
            half = d // 2
            pos = jnp.arange(t, dtype=x.dtype)[:, None]
            inv_freq = 1.0 / 10000.0 ** (jnp.arange(half, dtype=x.dtype) / half)
            ang = pos * inv_freq[None, :]
            sin, cos = (jnp.sin(ang), jnp.cos(ang))
            x1, x2 = (x[..., :half], x[..., half:])
            return jnp.concatenate([x1 * cos - x2 * sin, x1 * sin + x2 * cos], axis=-1)

        def mla_attention(x, Wq, Wdkv, Wuk, Wuv, Wo, ln_g, ln_b):
            b, t, _ = x.shape
            q = (x @ Wq.T).reshape(b, t, N_HEADS, HEAD_DIM).transpose(0, 2, 1, 3)
            latent = layernorm(x @ Wdkv.T, ln_g, ln_b)
            k = (latent @ Wuk.T).reshape(b, t, N_HEADS, HEAD_DIM).transpose(0, 2, 1, 3)
            v = (latent @ Wuv.T).reshape(b, t, N_HEADS, HEAD_DIM).transpose(0, 2, 1, 3)
            q = apply_rope(q)
            k = apply_rope(k)
            scores = jnp.einsum('bhqd,bhkd->bhqk', q, k) / np.sqrt(HEAD_DIM)
            causal = jnp.tril(jnp.ones((t, t), dtype=bool))
            scores = jnp.where(causal, scores, -jnp.inf)
            attn = jax.nn.softmax(scores, axis=-1)
            out = jnp.einsum('bhqk,bhkd->bhqd', attn, v).transpose(0, 2, 1, 3).reshape(b, t, D_MODEL)
            return out @ Wo.T

        def moe(x, gate_w, gate_b, W1, b1, W2, b2):
            logits = x @ gate_w.T + gate_b
            top = jnp.argmax(logits, axis=-1)
            onehot = jax.nn.one_hot(top, N_EXPERTS, dtype=x.dtype)
            h = jax.nn.relu(jnp.einsum('btd,ehd->bteh', x, W1) + b1)
            y = jnp.einsum('bteh,edh->bted', h, W2) + b2
            return jnp.einsum('bted,bte->btd', y, onehot)
        x = x + mla_attention(rmsnorm(x, norm1_w), Wq, Wdkv, Wuk, Wuv, Wo, ln_g, ln_b)
        x = x + moe(rmsnorm(x, norm2_w), gate_w, gate_b, W1, b1, W2, b2)
        return x
    x = L0_attn_x
    x = x + _L0_attn_ref(_layernorm(x, axis=-1), L0_attn_in_proj_w, L0_attn_in_proj_b, L0_attn_conv_w, L0_attn_conv_b, L0_attn_x_proj_w, L0_attn_x_proj_b, L0_attn_dt_proj_w, L0_attn_dt_proj_b, L0_attn_A_log, L0_attn_D, L0_attn_out_proj_w, L0_attn_out_proj_b, L0_attn_in_norm_alpha, L0_attn_in_norm_bias, L0_attn_norm_alpha, L0_attn_norm_bias)
    x = x + _L0_ffn_ref(_layernorm(x, axis=-1), L0_ffn_norm1_w, L0_ffn_norm2_w, L0_ffn_Wq, L0_ffn_Wdkv, L0_ffn_Wuk, L0_ffn_Wuv, L0_ffn_Wo, L0_ffn_ln_g, L0_ffn_ln_b, L0_ffn_gate_w, L0_ffn_gate_b, L0_ffn_W1, L0_ffn_b1, L0_ffn_W2, L0_ffn_b2)
    return x

_drawn_inputs = setup_inputs


def setup_inputs(seed=0):
    import zlib

    import numpy as np

    out = dict(_drawn_inputs(seed))
    spreads = {'L0_attn_in_proj_b': (0.0, 0.634),
     'L0_attn_conv_b': (0.0, 0.575),
     'L0_attn_x_proj_b': (0.0, 0.8),
     'L0_attn_dt_proj_b': (0.0, 0.8),
     'L0_attn_D': (1.0, 0.6),
     'L0_attn_out_proj_b': (0.0, 0.346),
     'L0_attn_in_norm_alpha': (1.0, 0.6),
     'L0_attn_in_norm_bias': (0.0, 0.8),
     'L0_attn_norm_alpha': (1.0, 0.2),
     'L0_attn_norm_bias': (0.0, 0.1),
     'L0_ffn_norm1_w': (1.0, 0.2),
     'L0_ffn_norm2_w': (1.0, 0.2),
     'L0_ffn_ln_g': (1.0, 0.2),
     'L0_ffn_ln_b': (0.0, 0.1),
     'L0_ffn_gate_b': (0.0, 0.1),
     'L0_ffn_b1': (0.0, 0.359),
     'L0_ffn_b2': (0.0, 0.1)}
    factors = {'L0_attn_in_proj_w': 5.046,
     'L0_attn_conv_w': 8.0,
     'L0_attn_x_proj_w': 8.0,
     'L0_attn_dt_proj_w': 8.0,
     'L0_attn_A_log': 8.0,
     'L0_attn_out_proj_w': 4.768}
    for name, (base, spread) in spreads.items():
        noise = np.random.default_rng([zlib.crc32(name.encode()), seed]).standard_normal(out[name].shape)
        drawn = base * np.exp(spread * noise) if base else spread * noise
        out[name] = jnp.asarray(drawn.astype(out[name].dtype))
    for name, factor in factors.items():
        out[name] = (out[name] * factor).astype(out[name].dtype)
    return out
```

```python
from contextlib import ExitStack

import numpy as np

import concourse.bass as bass
from concourse import mybir

F32 = mybir.dt.float32
BF16 = mybir.dt.bfloat16
ALU = mybir.AluOpType
ACT = mybir.ActivationFunctionType
AX = mybir.AxisListType

P = 128
B, L, D = 2, 2048, 256
DI, NS, KC = 512, 16, 4
TOK = B * L
NT = TOK // P
KD = D // P
MI = DI // P
BLK = 512
NB = L // BLK
HP = 2
DH = MI // HP
TB = 128
SB_ = L // TB
SUB = BLK // TB
CH = 16
NC_ = TB // CH
GD = P // NS
TL = DH * P // GD
ST = TL * B
W1 = CH + 1
IT = 8
TI = TL // IT
NH, HD, LAT = 16, 16, 128
VW = 32
NE, DHID = 4, 1024
H_MAX = 10.0
INP_AT = [(), (), (0,), (1,), (2,), (3,), (4, 5), (6, 7)]
DA_MIN = float(np.exp(np.float32(-10.0)))
LN_EPS = 1e-5
STD_EPS = 1e-6
BESSEL = D / (D - 1)
DT_MIN, DT_MAX = 1e-4, 10.0
LN_EXP, SQRT_SET = "natural_log_exp_and_others", "sqrt_and_others"


def sliced(ap, start, size):
    return ap[bass.ds(start, size)]


def token_rows(t, j, n, per=1):
    return t[:, bass.ds(j, n)]


def input_stats(nc, alloc, x, xs, mean, rstd, scale):
    sb, ps, sem = alloc
    raw = sb("in_bn_raw", [P, NT, 6])
    mv = sb("in_mean_var", [P, NT, 2])
    tmp = sb("in_tmp", [P, 4, NT])
    LOADS = 4
    per = NT // LOADS
    x_in = [sem(f"in_x_in{j}") for j in range(LOADS)]
    raw_done, mv_done, var_eps, roots, step = (sem(f"in_{n}") for n in ("raw", "mv", "var_eps", "roots", "step"))
    xt = x.rearrange("b (t p) d -> p (b t) d", p=P)
    with nc.Block() as block:

        @block.sync
        def _(sp):
            for j in range(LOADS):
                sp.dma_start(xs[:, j * per:(j + 1) * per, :], xt[:, j * per:(j + 1) * per, :]).then_inc(x_in[j], 16)

        @block.vector
        def _(dve):
            for j in range(LOADS):
                dve.wait_ge(x_in[j], 16)
                for t in range(j * per, (j + 1) * per):
                    dve.bn_stats(raw[:, t, :], xs[:, t, :]).then_inc(raw_done, 1)
            for t in range(NT):
                dve.wait_ge(raw_done, t + 1)
                dve.bn_aggr(mv[:, t, :], raw[:, t, :]).then_inc(mv_done, 1)
            dve.wait_ge(mv_done, NT)
            dve.tensor_scalar(tmp[:, 0, :], mv[:, :, 1], LN_EPS, None, ALU.add).then_inc(var_eps, 1)
            dve.tensor_copy(mean[:], mv[:, :, 0]).then_inc(step, 1)
            dve.wait_ge(roots, 2)
            dve.reciprocal(rstd[:], tmp[:, 1, :]).then_inc(step, 1)
            dve.wait_ge(step, 2)
            dve.tensor_tensor(tmp[:, 3, :], tmp[:, 2, :], rstd[:], ALU.mult).then_inc(step, 1)
            dve.wait_ge(step, 3)
            dve.tensor_scalar(scale[:], tmp[:, 3, :], STD_EPS, None, ALU.add).then_inc(step, 1)
            dve.wait_ge(step, 4)
            dve.reciprocal(tmp[:, 3, :], scale[:]).then_inc(step, 1)
            dve.wait_ge(step, 5)
            dve.tensor_tensor(scale[:], tmp[:, 3, :], rstd[:], ALU.mult).then_inc(step, 1)

        @block.scalar
        def _(act):
            act.wait_ge(var_eps, 1)
            act.activation(tmp[:, 1, :], tmp[:, 0, :], ACT.Sqrt).then_inc(roots, 1)
            act.activation(tmp[:, 2, :], mv[:, :, 1], ACT.Sqrt, scale=BESSEL).then_inc(roots, 1)


def to_features(nc, alloc, tag, xs, mean, scale, alpha, beta, ident, out):
    sb, ps, sem = alloc
    centred = [sb(f"{tag}_centred{u}", [P, 4, D]) for u in range(2)]
    weight, bias = sb(f"{tag}_weight", [P, KD]), sb(f"{tag}_bias", [P, KD])
    tr = [[ps(f"{tag}_tr{u}{k}", [P, BLK]) for k in range(KD)] for u in range(2)]
    w_in, scaled, turned, stored = (sem(f"{tag}_{n}") for n in ("w_in", "scaled", "turned", "stored"))
    loads = [(weight, alpha)] + ([(bias, beta)] if beta is not None else [])
    with nc.Block() as block:

        @block.sync
        def _(sp):
            for tile, src in loads:
                sp.dma_start(tile[:], src).then_inc(w_in, 16)

        @block.vector
        def _(dve):
            for g in range(NT // 4):
                if g >= 2:
                    dve.wait_ge(turned, 2 * (g - 1))
                for a in range(4):
                    t = 4 * g + a
                    if mean is None:
                        dve.tensor_scalar(centred[g % 2][:, a, :], xs[:, t, :], scale[:, t:t + 1], None,
                                          ALU.mult).then_inc(scaled, 1)
                    else:
                        dve.tensor_scalar(centred[g % 2][:, a, :], xs[:, t, :], mean[:, t:t + 1], scale[:, t:t + 1],
                                          ALU.subtract, ALU.mult).then_inc(scaled, 1)

        @block.scalar
        def _(act):
            act.wait_ge(w_in, 16 * len(loads))
            for g in range(NT // 4):
                for k in range(KD):
                    act.wait_ge(turned, KD * g + k + 1)
                    act.activation(out[:, k, g * BLK:(g + 1) * BLK], tr[g % 2][k][:], ACT.Identity,
                                   bias=bias[:, k:k + 1] if beta is not None else 0.0,
                                   scale=weight[:, k:k + 1]).then_inc(stored, 1)

        @block.tensor
        def _(pe):
            for g in range(NT // 4):
                pe.wait_ge(scaled, 4 * g + 4)
                for k in range(KD):
                    if g >= 2:
                        pe.wait_ge(stored, KD * (g - 2) + k + 1)
                    for a in range(4):
                        last = pe.transpose(tr[g % 2][k][:, a * P:(a + 1) * P],
                                            centred[g % 2][:, a, k * P:(k + 1) * P], ident[:])
                    last.then_inc(turned, 1)


def projections(nc, alloc, w, xn_t, scr):
    sb, ps, sem = alloc
    w_in = sb("pj_w_in", [P, KD, 2 * DI])
    b_in = sb("pj_b_in", [P, 2 * MI])
    w_cv = sb("pj_w_cv", [P, MI, KC])
    b_cv = sb("pj_b_cv", [P, MI])
    w_dt = sb("pj_w_dt", [P, MI, DI])
    b_dt = sb("pj_b_dt", [P, MI])
    w_bc = sb("pj_w_bc", [P, MI, 2, P])
    b_bc = sb("pj_b_bc", [P, 2])
    halo = KC - 1
    xin = [sb(f"pj_xin{b}", [P, MI, halo + BLK]) for b in range(B)]
    cv = [sb(f"pj_cv{b}", [P, MI, BLK]) for b in range(B)]
    xc = [sb(f"pj_xc{b}", [P, MI, BLK]) for b in range(B)]
    zs = [sb(f"pj_zs{b}", [P, MI, BLK]) for b in range(B)]
    dl = [sb(f"pj_dl{b}", [P, MI, BLK]) for b in range(B)]
    ux = [sb(f"pj_ux{b}", [P, MI, BLK]) for b in range(B)]
    bc = [sb(f"pj_bc{b}", [P, 2, BLK]) for b in range(B)]
    ps_x = [ps(f"pj_ps_x{j}", [P, BLK]) for j in range(2)]
    ps_z = [ps(f"pj_ps_z{j}", [P, BLK]) for j in range(2)]
    ps_d = [ps(f"pj_ps_d{j}", [P, BLK]) for j in range(2)]
    ps_b = [ps(f"pj_ps_b{j}", [P, BLK]) for j in range(2)]
    weights = sem("pj_weights")
    x_mm, z_mm, d_mm, b_mm = (sem(f"pj_{n}_mm") for n in "xzdb")
    x_out, z_out, d_out, b_out = (sem(f"pj_{n}_out") for n in "xzdb")
    zeroed, halo_ok, tap, conv_done = sem("pj_zeroed"), sem("pj_halo"), sem("pj_tap"), sem("pj_conv")
    xc_done, exp_done, ln_done = sem("pj_xc"), sem("pj_exp"), sem("pj_ln")
    dl_done, ux_done = sem("pj_dl"), sem("pj_ux")
    act_stored = [sem(f"pj_act_stored{b}") for b in range(B)]
    dve_stored = [sem(f"pj_dve_stored{b}") for b in range(B)]
    ACT_ST, DVE_ST = 3 * HP * 16, 2 * HP * 16
    M2 = B * MI
    loads = [(w_in, w["in_w"]), (b_in, w["in_b"]), (w_cv, w["cv_w"]), (b_cv, w["cv_b"]), (w_dt, w["dt_w"]),
             (b_dt, w["dt_b"]), (w_bc, w["bc_w"]), (b_bc, w["bc_b"])]
    with nc.Block() as block:

        @block.gpsimd
        def _(pool):
            for tile, src in loads:
                pool.dma_start(tile[:], src).then_inc(weights, 16)

        @block.sync
        def _(sp):
            def store(name, tile, i, b, done):
                n = tile.shape[1] // (HP if name != "bc" else 1)
                for h in range(HP):
                    own = tile[:, h * n:(h + 1) * n, :] if name != "bc" else tile[:]
                    sp.dma_start(scr[name][h, bass.ds(i * SUB, SUB), :, :, b, :].rearrange("n p d t -> p d n t"),
                                 own.rearrange("p d (n t) -> p d n t", t=TB)).then_inc(done, 16)

            with sp.Fori(0, NB) as i:
                for b in range(B):
                    sp.wait_ge(z_out, i * M2 + MI * (b + 1) + 2)
                    store("zs", zs[b], i, b, act_stored[b])
                    sp.wait_ge(xc_done, i * M2 + MI * (b + 1))
                    store("xc", xc[b], i, b, act_stored[b])
                for b in range(B):
                    sp.wait_ge(b_out, i * 2 * B + 2 * (b + 1) + 2)
                    store("bc", bc[b], i, b, act_stored[b])
                    sp.wait_ge(dl_done, i * M2 + MI * (b + 1))
                    store("dl", dl[b], i, b, dve_stored[b])
                    sp.wait_ge(ux_done, i * M2 + MI * (b + 1))
                    store("ux", ux[b], i, b, dve_stored[b])
            for b in range(B):
                sp.wait_ge(act_stored[b], NB * ACT_ST)
                sp.wait_ge(dve_stored[b], NB * DVE_ST)

        @block.tensor
        def _(pe):
            pe.wait_ge(weights, 16 * len(loads))
            with pe.Fori(0, NB) as i:
                for b in range(B):
                    rhs = [xn_t[:, k, bass.ds(b * L + i * BLK, BLK)] for k in range(KD)]
                    for m in range(MI):
                        pe.wait_ge(x_out, i * M2 + MI * b + m + 1)
                        for k in range(KD):
                            mm = pe.matmul(ps_x[m % 2][:], w_in[:, k, m * P:(m + 1) * P], rhs[k],
                                           start=k == 0, stop=k == KD - 1)
                        mm.then_inc(x_mm, 1)
                        pe.wait_ge(z_out, i * M2 + MI * b + m + 1)
                        for k in range(KD):
                            mm = pe.matmul(ps_z[m % 2][:], w_in[:, k, DI + m * P:DI + (m + 1) * P], rhs[k],
                                           start=k == 0, stop=k == KD - 1)
                        mm.then_inc(z_mm, 1)
                for b in range(B):
                    pe.wait_ge(xc_done, i * M2 + MI * (b + 1))
                    for c in range(2):
                        pe.wait_ge(b_out, i * 2 * B + 2 * b + c + 1)
                        for k in range(MI):
                            mm = pe.matmul(ps_b[c][:], w_bc[:, k, c, :], xc[b][:, k, :], start=k == 0, stop=k == MI - 1)
                        mm.then_inc(b_mm, 1)
                    for m in range(MI):
                        pe.wait_ge(d_out, i * M2 + MI * b + m + 1)
                        for k in range(MI):
                            mm = pe.matmul(ps_d[m % 2][:], w_dt[:, k, m * P:(m + 1) * P], xc[b][:, k, :],
                                           start=k == 0, stop=k == MI - 1)
                        mm.then_inc(d_mm, 1)

        @block.vector
        def _(dve):
            for b in range(B):
                dve.memset(xin[b][:], 0.0).then_inc(zeroed, 1)
            dve.sem_inc(x_out, 2)
            dve.sem_inc(d_out, 2)
            dve.wait_ge(weights, 16 * len(loads))
            dve.wait_ge(zeroed, B)
            with dve.Fori(0, NB) as i:
                for b in range(B):
                    dve.wait_ge(conv_done, i * M2)
                    dve.tensor_copy(xin[b][:, :, 0:halo], xin[b][:, :, BLK:BLK + halo]).then_inc(halo_ok, 1)
                    dve.wait_ge(halo_ok, i * B + b + 1)
                    dve.wait_ge(xc_done, i * M2)
                    for m in range(MI):
                        n = i * M2 + MI * b + m
                        dve.wait_ge(x_mm, n + 1)
                        dve.tensor_scalar(xin[b][:, m, halo:], ps_x[m % 2][:], b_in[:, m:m + 1], None,
                                          ALU.add).then_inc(x_out, 1)
                        dve.wait_ge(x_out, n + 3)
                        dve.tensor_scalar(cv[b][:, m, :], xin[b][:, m, 0:BLK], w_cv[:, m, 0:1], b_cv[:, m:m + 1],
                                          ALU.mult, ALU.add).then_inc(tap, 1)
                        for j in range(1, KC):
                            dve.wait_ge(tap, n * (KC - 1) + j)
                            dve.scalar_tensor_tensor(cv[b][:, m, :], xin[b][:, m, j:j + BLK], w_cv[:, m, j:j + 1],
                                                     cv[b][:, m, :], ALU.mult, ALU.add)\
                               .then_inc(tap if j < KC - 1 else conv_done, 1)
                for b in range(B):
                    dve.wait_ge(dve_stored[b], i * DVE_ST)
                    for m in range(MI):
                        n = i * M2 + MI * b + m
                        dve.wait_ge(d_mm, n + 1)
                        dve.tensor_scalar(dl[b][:, m, :], ps_d[m % 2][:], b_dt[:, m:m + 1], 20.0,
                                          ALU.add, ALU.min).then_inc(d_out, 1)
                    for m in range(MI):
                        n = i * M2 + MI * b + m
                        dve.wait_ge(ln_done, n + 1)
                        dve.tensor_scalar(dl[b][:, m, :], dl[b][:, m, :], DT_MIN, DT_MAX,
                                          ALU.max, ALU.min).then_inc(dl_done, 1)
                        dve.wait_ge(dl_done, n + 1)
                        dve.tensor_tensor(ux[b][:, m, :], dl[b][:, m, :], xc[b][:, m, :], ALU.mult).then_inc(ux_done, 1)

        @block.scalar
        def _(act):
            act.sem_inc(z_out, 2)
            act.sem_inc(b_out, 2)
            act.wait_ge(weights, 16 * len(loads))
            with act.Fori(0, NB) as i:
                for b in range(B):
                    act.wait_ge(act_stored[b], i * ACT_ST)
                    for m in range(MI):
                        n = i * M2 + MI * b + m
                        act.wait_ge(z_mm, n + 1)
                        act.activation(zs[b][:, m, :], ps_z[m % 2][:], ACT.Silu,
                                       bias=b_in[:, MI + m:MI + m + 1]).then_inc(z_out, 1)
                        act.wait_ge(conv_done, n + 1)
                        act.activation(xc[b][:, m, :], cv[b][:, m, :], ACT.Silu).then_inc(xc_done, 1)
                for b in range(B):
                    for c in range(2):
                        act.wait_ge(b_mm, i * 2 * B + 2 * b + c + 1)
                        act.activation(bc[b][:, c, :], ps_b[c][:], ACT.Identity, bias=b_bc[:, c:c + 1])\
                           .then_inc(b_out, 1)
                    for m in range(MI):
                        n = i * M2 + MI * b + m
                        act.wait_ge(d_out, n + 3)
                        act.activation(dl[b][:, m, :], dl[b][:, m, :], ACT.Exp).then_inc(exp_done, 1)
                        act.wait_ge(exp_done, n + 1)
                        act.activation(dl[b][:, m, :], dl[b][:, m, :], ACT.Ln, bias=1.0).then_inc(ln_done, 1)



def tile_place(st):
    item, jr, e = st // TI, (st % TI) // 2, st % 2
    d, q, r = item // 4, item // 2 % 2, item % 2
    return d, 2 * r + jr, 2 * q + e


def selective_scan(nc, alloc, w, scr):
    sb, ps, sem = alloc
    NJ = HP * SB_
    sel = sb("sc_sel", [P, 4, P])
    ysel = sb("sc_ysel", [P, 4, 32])
    pool16 = sb("sc_pool16", [P, P])
    par = sb("sc_par", [P, NJ, TL + DH + 1])
    dA = [sb(f"sc_dA{q}", [P, NC_, ST, W1]) for q in range(2)]
    hb = [sb(f"sc_h{q}", [P, NC_, ST, W1]) for q in range(2)]
    dl = [sb(f"sc_dl{q}", [P, DH, B, TB]) for q in range(2)]
    ux = [sb(f"sc_ux{q}", [P, DH, B, TB]) for q in range(2)]
    bt = [sb(f"sc_b{q}", [P, B, TB]) for q in range(2)]
    ct = [sb(f"sc_c{q}", [P, B, TB]) for q in range(2)]
    xc = [sb(f"sc_xc{q}", [P, DH, B, TB]) for q in range(2)]
    zs = [sb(f"sc_zs{q}", [P, DH, B, TB]) for q in range(2)]
    yv = [sb(f"sc_yv{q}", [P, DH, B, TB]) for q in range(2)]
    yg = [sb(f"sc_yg{q}", [P, DH, B, TB]) for q in range(2)]
    sq = sb("sc_sq", [P, ST])
    mx = sb("sc_mx", [P, ST])
    lg = sb("sc_lg", [P, ST])
    scl = [sb(f"sc_scl{q}", [P, ST]) for q in range(2)]
    ps_d = [ps(f"sc_ps_d{q}", [P, 2, 2, B * TB]) for q in range(2)]
    ps_u = ps("sc_ps_u", [P, 2, 2, B * TB])
    ps_y = ps("sc_ps_y", [P, DH, B * TB])
    ps_n = ps("sc_ps_n", [P, BLK])

    consts, decay = sem("sc_consts"), sem("sc_decay")
    cleared = sem("sc_cleared")
    in_a = [sem(f"sc_in_a{q}") for q in range(2)]
    in_c = [sem(f"sc_in_c{q}") for q in range(2)]
    in_x = [sem(f"sc_in_x{q}") for q in range(2)]
    stored = [sem(f"sc_stored{q}") for q in range(2)]
    d_mm, u_mm, n_mm, y_mm = (sem(f"sc_{n}_mm") for n in "duny")
    exp_done, clip_done, inp_done = sem("sc_exp"), sem("sc_clip"), sem("sc_inp")
    scan_done, sq_done, mx_done, lg_done, scl_done, head_done = (
        sem(f"sc_{n}") for n in ("scan", "sq", "mx", "lg", "scl", "head"))
    last_done, c_done = sem("sc_last"), sem("sc_cmul")
    y_done, gate_done = sem("sc_y"), sem("sc_gate")
    EXP_AHEAD, LAST_AHEAD, GATE_AHEAD = 2 * TI, 1, 2

    def turns(eng, turn):
        for u in range(2):
            turn(u, u, 0, u == 0, False)
        with eng.Fori(1, NJ // 2 - 1) as m:
            for u in range(2):
                turn(2 * m + u, u, m, False, False)
        for u in range(2):
            turn(NJ - 2 + u, u, NJ // 2 - 1, False, u == 1)

    blocks = {n: scr[n].rearrange("h n p d b t -> (h n) p d b t") for n in ("dl", "ux", "xc", "zs", "yg", "bc")}

    def block_of(name, j):
        return blocks[name][bass.ds(j, 1)].rearrange("n p d b t -> (n p) d b t")

    with nc.Block() as block:

        @block.sync
        def _(sp):
            def load_a(j, q):
                sp.dma_start(dl[q][:], block_of("dl", j)).then_inc(in_a[q], 16)
                sp.dma_start(ux[q][:], block_of("ux", j)).then_inc(in_a[q], 16)
                sp.dma_start(bt[q][:], block_of("bc", j)[:, 0]).then_inc(in_a[q], 16)

            def load_c(j, q):
                sp.dma_start(ct[q][:], block_of("bc", j)[:, 1]).then_inc(in_c[q], 16)

            def load_x(j, q):
                sp.dma_start(xc[q][:], block_of("xc", j)).then_inc(in_x[q], 16)
                sp.dma_start(zs[q][:], block_of("zs", j)).then_inc(in_x[q], 16)

            def turn(j, u, m, first, last):
                ahead = not (isinstance(j, int) and j + 2 >= NJ)
                if ahead:
                    sp.wait_ge(d_mm, (j + 1) * IT)
                    sp.wait_ge(inp_done, (j + 1) * 2 * IT)
                    load_a(j + 2, u)
                if not first:
                    sp.wait_ge(gate_done, j + GATE_AHEAD)
                    sp.dma_start(block_of("yg", j - 1), yg[1 - u][:]).then_inc(stored[1 - u], 16)
                if not last:
                    load_x(j + 1, 1 - u)
                if ahead:
                    sp.wait_ge(c_done, (j + 1) * NC_)
                    load_c(j + 2, u)

            for name, tile in (("sel", sel), ("ysel", ysel), ("pool16", pool16), ("par", par)):
                sp.dma_start(tile[:], w[name]).then_inc(consts, 16)
            for q in range(2):
                load_a(q, q)
                load_c(q, q)
            load_x(0, 0)
            turns(sp, turn)
            sp.wait_ge(gate_done, NJ + GATE_AHEAD)
            sp.dma_start(block_of("yg", NJ - 1), yg[1][:]).then_inc(stored[1], 16)
            for q in range(2):
                sp.wait_ge(stored[q], 16 * NJ // 2)

        @block.tensor
        def _(pe):
            def spread(out, src, item, jr_e):
                jr, e = jr_e
                d, quad, i = tile_place(item * TI + 2 * jr + e)
                rows = slice(32 * quad, 32 * quad + 32)
                return pe.matmul(out[:, jr, e, :], sel[rows, i, :], src[rows, d].rearrange("p b t -> p (b t)"),
                                 start=True, stop=True)

            def decays(jj, q, item):
                pe.wait_ge(exp_done, (jj * IT + item) * TI + TI)
                for e in range(2):
                    for jr in range(2):
                        mm = spread(ps_d[item % 2], dl[q], item, (jr, e))
                mm.then_inc(d_mm, 1)

            def inputs(jj, q, item):
                pe.wait_ge(inp_done, (jj * IT + item) * 2)
                for e in range(2):
                    for jr in range(2):
                        mm = spread(ps_u, ux[q], item, (jr, e))
                mm.then_inc(u_mm, 1)

            def sums(j, q, part):
                for quad in range(4):
                    d, i = part // 4, part % 4
                    st = next(s for s in range(TL) if tile_place(s) == (d, quad, i))
                    h = hb[q][:, :, st * B:(st + 1) * B, 1:].rearrange("p c b t -> p b c t")
                    mm = pe.matmul(ps_y[32 * quad:32 * quad + 32, d, :].rearrange("p (b c t) -> p b c t", b=B, t=CH),
                                   ysel[:, i, :], h, start=i == 0, stop=i == 3)
                mm.then_inc(y_mm, 1)

            def turn(j, u, m, first, last):
                for c in range(NC_):
                    if not last:
                        if c == 0:
                            pe.wait_ge(in_a[1 - u], 48 * (m + 1 + u))
                        decays(j + 1, 1 - u, c)
                    pe.wait_ge(sq_done, j * NC_ + c + 1)
                    pe.matmul(ps_n[:, 0:ST], pool16[:], sq[:], start=True, stop=True).then_inc(n_mm, 1)
                    if c < 2 and not first:
                        if c == 0:
                            pe.wait_ge(c_done, j * NC_)
                            pe.wait_ge(y_done, (j - 1) * DH)
                        for part in range(4 * c, 4 * c + 4):
                            sums(j - 1, 1 - u, part)
                    if not last:
                        for item in INP_AT[c]:
                            inputs(j + 1, 1 - u, item)

            pe.wait_ge(consts, 64)
            pe.wait_ge(in_a[0], 48)
            for item in range(IT):
                decays(0, 0, item)
                inputs(0, 0, item)
            turns(pe, turn)
            pe.wait_ge(c_done, NJ * NC_)
            pe.wait_ge(y_done, (NJ - 1) * DH)
            for part in range(8):
                sums(NJ - 1, 1, part)

        @block.scalar
        def _(act):
            def decay_exps(jj, q, item, tiles):
                if 0 in tiles:
                    act.wait_ge(d_mm, jj * IT + item + 1)
                for n in tiles:
                    st = item * TI + n
                    out = dA[q][:, :, st * B:(st + 1) * B, 1:].rearrange("p c b t -> p b c t")
                    act.activation(out, ps_d[item % 2][:, n // 2, n % 2, :].rearrange("p (b c t) -> p b c t", b=B, t=CH),
                                   ACT.Exp, scale=par[:, jj, st:st + 1] if isinstance(jj, int)
                                   else par[:, bass.ds(jj, 1), st:st + 1].rearrange("p a b -> p (a b)"))\
                       .then_inc(exp_done, 1)

            def turn(j, u, m, first, last):
                for c in range(NC_):
                    s = j * NC_ + c
                    act.wait_ge(scan_done, s + 1)
                    act.activation(sq[:], hb[u][:, c, :, CH], ACT.Square).then_inc(sq_done, 1)
                    if not last:
                        decay_exps(j + 1, 1 - u, c, (0, 1))
                    act.wait_ge(mx_done, s + 1)
                    act.activation(lg[:], mx[:], ACT.Ln, scale=1.0 / (H_MAX * H_MAX)).then_inc(lg_done, 1)
                    act.wait_ge(lg_done, s + 1)
                    act.wait_ge(last_done, s)
                    act.activation(scl[c % 2][:], lg[:], ACT.Exp, scale=-0.5).then_inc(scl_done, 1)
                    if not last:
                        decay_exps(j + 1, 1 - u, c, (2, 3))

            act.preload_act_table_set(LN_EXP)
            act.sem_inc(exp_done, EXP_AHEAD)
            act.wait_ge(consts, 64)
            act.activation(par[:, :, 0:TL], par[:, :, 0:TL], ACT.Exp).then_inc(decay, 1)
            act.wait_ge(decay, 2)
            act.wait_ge(cleared, 2)
            for item in range(IT):
                decay_exps(0, 0, item, range(TI))
            turns(act, turn)

        @block.vector
        def _(dve):
            def clip(jj, q, item):
                dve.wait_ge(exp_done, (jj * IT + item) * TI + TI + EXP_AHEAD)
                own = dA[q][:, :, item * TI * B:(item + 1) * TI * B, 1:]
                dve.tensor_scalar(own, own, DA_MIN, None, ALU.max).then_inc(clip_done, 1)

            def inputs(jj, q, item):
                dve.wait_ge(u_mm, jj * IT + item + 1)
                for b in range(B):
                    streams = slice(item * TI * B + b, (item + 1) * TI * B, B)
                    out = hb[q][:, :, streams, 1:].rearrange("p c s t -> p s c t")
                    rep = bt[q][:, b, :].rearrange("p (c t) -> p c t", t=CH).unsqueeze(1).broadcast_to([P, TI, NC_, CH])
                    dve.tensor_tensor(out, ps_u[:, :, :, b * TB:(b + 1) * TB].rearrange("p k e (c t) -> p (k e) c t", t=CH),
                                      rep, ALU.mult).then_inc(inp_done, 1)

            def outputs(j, q, count):
                dve.wait_ge(y_mm, (j + 1) * 8)
                dve.wait_ge(in_x[q], count)
                dve.wait_ge(gate_done, j + 1)
                for d in range(DH):
                    dve.scalar_tensor_tensor(
                        yv[q][:, d].rearrange("p b t -> p (b t)"), xc[q][:, d].rearrange("p b t -> p (b t)"),
                        par[:, j, TL + d:TL + d + 1] if isinstance(j, int)
                        else par[:, bass.ds(j, 1), TL + d:TL + d + 1].rearrange("p a b -> p (a b)"),
                        ps_y[:, d, :], ALU.mult, ALU.add).then_inc(y_done, 1)

            def turn(j, u, m, first, last):
                for c in range(NC_):
                    s = j * NC_ + c
                    if c == 0:
                        dve.wait_ge(clip_done, (j + 1) * IT)
                        dve.wait_ge(inp_done, (j + 1) * 2 * IT)
                    dve.wait_ge(head_done, s + 1)
                    flat = lambda t: t[:, c].rearrange("p s w -> p (s w)")
                    dve.tensor_tensor_scan(flat(hb[u]), flat(dA[u]), flat(hb[u]), 0.0, ALU.mult, ALU.add)\
                       .then_inc(scan_done, 1)
                    if c >= 1 and not last:
                        clip(j + 1, 1 - u, c - 1)
                    dve.wait_ge(n_mm, s + 1)
                    dve.tensor_scalar(mx[:], ps_n[:, 0:ST], H_MAX * H_MAX, None, ALU.max).then_inc(mx_done, 1)
                    if c == 2:
                        if not first:
                            dve.wait_ge(y_mm, j * 8)
                    if c == 1 and not first:
                        outputs(j - 1, 1 - u, 32 * (m + u))
                    if not last:
                        for item in INP_AT[c][:1]:
                            inputs(j + 1, 1 - u, item)
                    dve.wait_ge(scl_done, s + 1)
                    if c < NC_ - 1:
                        dve.tensor_tensor(hb[u][:, c + 1, :, 0], hb[u][:, c, :, CH], scl[c % 2][:], ALU.mult)\
                           .then_inc(head_done, 1)
                    elif not last:
                        keep = par[:, j + 1, TL + DH:] if isinstance(j, int) else \
                            par[:, bass.ds(j + 1, 1), TL + DH:].rearrange("p a b -> p (a b)")
                        dve.scalar_tensor_tensor(hb[1 - u][:, 0, :, 0], hb[u][:, c, :, CH], keep, scl[c % 2][:],
                                                 ALU.mult, ALU.mult).then_inc(head_done, 1)
                    if not last:
                        for item in INP_AT[c][1:]:
                            inputs(j + 1, 1 - u, item)
                        if c == NC_ - 1:
                            clip(j + 1, 1 - u, c)

            for q in range(2):
                dve.memset(dA[q][:, :, :, 0], 0.0).then_inc(cleared, 1)
            dve.memset(hb[0][:, 0, :, 0], 0.0).then_inc(head_done, 1)
            dve.wait_ge(decay, 1)
            dve.tensor_scalar(par[:, :, 0:TL], par[:, :, 0:TL], -1.0, None, ALU.mult).then_inc(decay, 1)
            for item in range(IT):
                clip(0, 0, item)
                inputs(0, 0, item)
            turns(dve, turn)
            outputs(NJ - 1, 1, 32 * (NJ // 2))

        @block.gpsimd
        def _(pool):
            def gate(j, q, count):
                pool.wait_ge(y_done, (j + 1) * DH)
                pool.wait_ge(stored[q], count)
                pool.tensor_tensor(yg[q][:], yv[q][:], zs[q][:], ALU.mult).then_inc(gate_done, 1)

            def turn(j, u, m, first, last):
                for c in range(NC_):
                    s = j * NC_ + c
                    pool.wait_ge(scl_done, s + 1)
                    if not (last and c == NC_ - 1):
                        pool.wait_ge(head_done, s + 2)
                    pool.tensor_tensor(hb[u][:, c, :, CH], hb[u][:, c, :, CH], scl[c % 2][:], ALU.mult)\
                        .then_inc(last_done, 1)
                    pool.wait_ge(last_done, s + 1 + LAST_AHEAD)
                    if c == 0:
                        pool.wait_ge(in_c[u], 16 * (m + 1))
                    h = hb[u][:, c, :, 1:].rearrange("p (s b) t -> p s b t", b=B)
                    rep = ct[u][:, :, c * CH:(c + 1) * CH].unsqueeze(1).broadcast_to([P, TL, B, CH])
                    pool.tensor_tensor(h, h, rep, ALU.mult).then_inc(c_done, 1)
                    if c == 3 and not first:
                        gate(j - 1, 1 - u, 16 * (m + u - 1))

            pool.sem_inc(last_done, LAST_AHEAD)
            pool.sem_inc(gate_done, GATE_AHEAD)
            turns(pool, turn)
            gate(NJ - 1, 1, 16 * (NJ // 2 - 1))


def back_to_tokens(nc, alloc, w, scr, x, mean, rstd, out, mean3, scale3, rstd3):
    sb, ps, sem = alloc
    wo, wb = sb("bt_w", [P, MI, D]), sb("bt_b", [P, D])
    ga, be = sb("bt_gamma", [P, D]), sb("bt_beta", [P, D])
    xb = sb("bt_x_beta", [P, NT, D])
    yt = [sb(f"bt_y{b}", [P, MI, BLK]) for b in range(B)]
    xt = [sb(f"bt_x{b}", [P, SUB, D]) for b in range(B)]
    r1, r2 = sb("bt_r1", [P, 2, D]), sb("bt_r2", [P, 2, D])
    raw, mv = sb("bt_raw", [P, NT, 6]), sb("bt_mv", [P, NT, 2])
    tmp = sb("bt_tmp", [P, 4, NT])
    po = [ps(f"bt_ps{j}", [P, BLK])[:, 0:D] for j in range(2)]
    weights, mm, res, own, summed, raw_done, xb_done = (
        sem(f"bt_{n}") for n in ("weights", "mm", "res", "own", "summed", "raw", "xb"))
    y_in = [sem(f"bt_y_in{b}") for b in range(B)]
    x_in = [sem(f"bt_x_in{b}") for b in range(B)]
    mv_done, roots, root_in, step, normed, raw2, mv2 = (
        sem(f"bt_{n}") for n in ("mv", "roots", "root_in", "step", "normed", "raw2", "mv2"))
    M = B * SUB
    with nc.Block() as block:

        @block.sync
        def _(sp):
            for tile, name in ((wo, "out_w"), (wb, "out_b"), (ga, "gamma"), (be, "beta")):
                sp.dma_start(tile[:], w[name]).then_inc(weights, 16)
            with sp.Fori(0, NB) as i:
                for b in range(B):
                    sp.wait_ge(mm, i * M)
                    for h in range(HP):
                        sp.dma_start(yt[b][:, h * DH:(h + 1) * DH, :].rearrange("p d (n t) -> p d n t", t=TB),
                                     scr["yg"][h, bass.ds(i * SUB, SUB), :, :, b, :].rearrange("n p d t -> p d n t"))\
                          .then_inc(y_in[b], 16)
                    sp.wait_ge(res, i * M)
                    sp.dma_start(xt[b][:], x[b, bass.ds(i * BLK, BLK), :].rearrange("(a p) d -> p a d", p=P))\
                      .then_inc(x_in[b], 16)

        @block.tensor
        def _(pe):
            pe.wait_ge(weights, 64)
            with pe.Fori(0, NB) as i:
                for b in range(B):
                    pe.wait_ge(y_in[b], 32 * (i + 1))
                    for a in range(SUB):
                        pe.wait_ge(own, i * M + SUB * b + a + 1)
                        for k in range(MI):
                            last = pe.matmul(po[a % 2], yt[b][:, k, a * P:(a + 1) * P], wo[:, k, :],
                                             start=k == 0, stop=k == MI - 1)
                        last.then_inc(mm, 1)

        @block.gpsimd
        def _(pool):
            pool.wait_ge(weights, 64)
            with pool.Fori(0, NB) as i:
                for b in range(B):
                    pool.wait_ge(x_in[b], 16 * (i + 1))
                    pool.tensor_tensor(xb[:, bass.ds(b * (NT // B) + i * SUB, SUB), :], xt[b][:],
                                       be[:].unsqueeze(1).broadcast_to([P, SUB, D]), ALU.add).then_inc(xb_done, 1)

        @block.vector
        def _(dve):
            dve.sem_inc(own, 2)
            dve.wait_ge(weights, 64)
            with dve.Fori(0, NB) as i:
                for b in range(B):
                    dve.wait_ge(x_in[b], 16 * (i + 1))
                    for a in range(SUB):
                        n = i * M + SUB * b + a
                        t = b * (NT // B) + i * SUB + a
                        at = lambda v: v[:, bass.ds(t, 1)]
                        dve.wait_ge(summed, n)
                        if a == SUB - 1:
                            dve.wait_ge(xb_done, i * B + b + 1)
                        dve.tensor_scalar(r1[:, a % 2, :], xt[b][:, a, :], at(mean), at(rstd),
                                          ALU.subtract, ALU.mult).then_inc(res, 1)
                        dve.wait_ge(res, n + 1)
                        dve.wait_ge(mm, n + 1)
                        dve.tensor_tensor(r2[:, a % 2, :], po[a % 2], r1[:, a % 2, :], ALU.add).then_inc(own, 1)
                        dve.wait_ge(own, n + 3)
                        dve.tensor_tensor(out[:, bass.ds(t, 1), :].rearrange("p a d -> p (a d)"), r2[:, a % 2, :], wb[:],
                                          ALU.add).then_inc(summed, 1)
            dve.wait_ge(summed, NT)
            for t in range(NT):
                dve.bn_stats(raw[:, t, :], out[:, t, :]).then_inc(raw_done, 1)
            for t in range(NT):
                dve.wait_ge(raw_done, t + 1)
                dve.bn_aggr(mv[:, t, :], raw[:, t, :]).then_inc(mv_done, 1)
            dve.wait_ge(mv_done, NT)
            dve.wait_ge(roots, 1)
            dve.tensor_scalar(tmp[:, 1, :], tmp[:, 0, :], STD_EPS, None, ALU.add).then_inc(step, 1)
            dve.wait_ge(step, 1)
            dve.reciprocal(tmp[:, 2, :], tmp[:, 1, :]).then_inc(step, 1)
            dve.wait_ge(step, 2)
            dve.wait_ge(xb_done, NB * B)
            for t in range(NT):
                dve.tensor_scalar(r1[:, t % 2, :], out[:, t, :], mv[:, t, 0:1], tmp[:, 2, t:t + 1],
                                  ALU.subtract, ALU.mult).then_inc(normed, 1)
                dve.wait_ge(normed, 3 * t + 1)
                dve.tensor_tensor(r2[:, t % 2, :], r1[:, t % 2, :], ga[:], ALU.mult).then_inc(normed, 1)
                dve.wait_ge(normed, 3 * t + 2)
                dve.tensor_tensor(out[:, t, :], r2[:, t % 2, :], xb[:, t, :], ALU.add).then_inc(normed, 1)
                dve.wait_ge(normed, 3 * t + 3)
                dve.bn_stats(raw[:, t, :], out[:, t, :]).then_inc(raw2, 1)
            dve.wait_ge(raw2, NT)
            for t in range(NT):
                dve.bn_aggr(mv[:, t, :], raw[:, t, :]).then_inc(mv2, 1)
            dve.wait_ge(mv2, NT)
            dve.tensor_copy(mean3[:], mv[:, :, 0]).then_inc(step, 1)
            dve.tensor_scalar(tmp[:, 0, :], mv[:, :, 1], LN_EPS, None, ALU.add).then_inc(root_in, 1)
            dve.wait_ge(roots, 2)
            dve.reciprocal(rstd3[:], tmp[:, 1, :]).then_inc(step, 1)
            dve.wait_ge(root_in, 1)
            dve.reciprocal(tmp[:, 2, :], tmp[:, 0, :]).then_inc(step, 1)
            dve.wait_ge(step, 5)
            dve.tensor_tensor(tmp[:, 3, :], tmp[:, 2, :], mv[:, :, 1], ALU.mult).then_inc(step, 1)
            dve.wait_ge(step, 6)
            dve.tensor_scalar(tmp[:, 2, :], tmp[:, 3, :], STD_EPS, None, ALU.add).then_inc(root_in, 1)
            dve.wait_ge(roots, 3)
            dve.reciprocal(tmp[:, 1, :], tmp[:, 0, :]).then_inc(step, 1)
            dve.wait_ge(step, 7)
            dve.tensor_tensor(scale3[:], tmp[:, 1, :], rstd3[:], ALU.mult).then_inc(step, 1)

        @block.scalar
        def _(act):
            act.wait_ge(mv_done, NT)
            act.activation(tmp[:, 0, :], mv[:, :, 1], ACT.Sqrt, scale=BESSEL).then_inc(roots, 1)
            act.wait_ge(root_in, 1)
            act.activation(tmp[:, 1, :], tmp[:, 0, :], ACT.Sqrt).then_inc(roots, 1)
            act.wait_ge(root_in, 2)
            act.activation(tmp[:, 0, :], tmp[:, 2, :], ACT.Sqrt).then_inc(roots, 1)


def latents(nc, alloc, w, h_t, scr):
    sb, ps, sem = alloc
    wq, wk = sb("la_wq", [P, KD, 2 * D]), sb("la_wk", [P, 2 * D])
    wl, wv = sb("la_wl", [P, KD, P]), sb("la_wv", [P, D])
    lg, lb = sb("la_g", [P, 1]), sb("la_b", [P, 1])
    cos, sin = sb("la_cos", [P, L]), sb("la_sin", [P, L])
    avg = sb("la_avg", [P, P])
    eps = sb("la_eps", [P, 1])
    qa, qb = sb("la_qa", [P, 2, BLK]), sb("la_qb", [P, 2, BLK])
    qf, qr = sb("la_qf", [P, 2, BLK]), sb("la_qr", [P, 2, BLK])
    parts = sb("la_parts", [P, 2, 3, BLK], BF16)
    lat, cen, sq, sd, rec = (sb(f"la_{n}", [P, BLK]) for n in ("lat", "cen", "sq", "sd", "rec"))
    ln = sb("la_ln", [P, BLK])
    vt = sb("la_vt", [P, SUB, NH, VW])
    pq = [ps(f"la_pq{j}", [P, BLK]) for j in range(4)]
    pl, pm, pv = ps("la_pl", [P, BLK]), ps("la_pm", [P, BLK]), ps("la_pv", [P, BLK])
    po = ps("la_po", [P, BLK])[:, 0:D]
    (weights, ready, l_mm, m_mm, v_mm, q_mm, o_mm, lat_done, cen_done, sq_done, sd_done, rec_done, nrm_done,
     ln_done, turn1, turn2, q_done, cut, lo_done, v_out) = (
        sem(f"la_{n}") for n in ("weights ready l_mm m_mm v_mm q_mm o_mm lat cen sq sd rec nrm ln turn1 turn2 "
                                 "q cut lo v_out").split())
    q_st = [sem(f"la_q_st{j}") for j in range(2)]
    v_st = sem("la_v_st")
    loads = [(wq, "wq"), (wk, "wk"), (wl, "wl"), (wv, "wv"), (lg, "ln_g"), (lb, "ln_b"), (cos, "cos"), (sin, "sin"),
             (avg, "avg")]
    R = 2 * KD
    with nc.Block() as block:

        @block.gpsimd
        def _(pool):
            pool.memset(vt[:], 0.0).then_inc(ready, 1)
            pool.memset(eps[:], LN_EPS).then_inc(ready, 1)
            pool.wait_ge(ready, 2)
            pool.memset(vt[:, :, :, HD], 1.0).then_inc(ready, 1)

        @block.sync
        def _(sp):
            for tile, name in loads:
                sp.dma_start(tile[:], w[name]).then_inc(weights, 16)
            for b in range(B):
                with sp.Fori(0, NB) as i:
                    n = b * NB + i
                    col = bass.ds(b * L + i * BLK, BLK)
                    for r in range(R):
                        dst = scr["qs" if r < KD else "ks"]
                        sp.wait_ge(lo_done, n * R + r + 1)
                        sp.dma_start(dst[:, r % KD * P:(r % KD + 1) * P, col].rearrange("s p t -> p s t"),
                                     parts[:, r % 2]).then_inc(q_st[r % 2], 16)
                    sp.wait_ge(v_out, (n + 1) * SUB)
                    sp.dma_start(scr["v"][bass.ds(b * L + i * BLK, BLK)].rearrange("(a p) h c -> p a h c", p=P),
                                 vt[:]).then_inc(v_st, 16)
            for r in range(2):
                sp.wait_ge(q_st[r], B * NB * R // 2 * 16)
            sp.wait_ge(v_st, B * NB * 16)

        @block.tensor
        def _(pe):
            pe.wait_ge(weights, 16 * len(loads))
            for b in range(B):
                with pe.Fori(0, NB) as i:
                    n = b * NB + i
                    rhs = [h_t[:, k, bass.ds(b * L + i * BLK, BLK)] for k in range(KD)]
                    pe.wait_ge(lat_done, n)
                    for k in range(KD):
                        last = pe.matmul(pl[:], wl[:, k, :], rhs[k], start=k == 0, stop=k == KD - 1)
                    last.then_inc(l_mm, 1)
                    for m in range(KD):
                        pe.wait_ge(turn2, n * R + m)
                        for v in range(2):
                            for k in range(KD):
                                last = pe.matmul(pq[2 * (m % 2) + v][:], wq[:, k, v * D + m * P:v * D + (m + 1) * P],
                                                 rhs[k], start=k == 0, stop=k == KD - 1)
                        last.then_inc(q_mm, 1)
                    pe.wait_ge(lat_done, n + 1)
                    pe.matmul(pm[:], avg[:], lat[:], start=True, stop=True).then_inc(m_mm, 1)
                    pe.wait_ge(sq_done, n + 1)
                    pe.matmul(pv[:], avg[:], sq[:], start=True, stop=True).then_inc(v_mm, 1)
                    pe.wait_ge(ln_done, n + 1)
                    for m in range(KD):
                        pe.wait_ge(turn2, n * R + KD + m)
                        for v in range(2):
                            last = pe.matmul(pq[2 * (m % 2) + v][:], wk[:, v * D + m * P:v * D + (m + 1) * P], ln[:],
                                             start=True, stop=True)
                        last.then_inc(q_mm, 1)
                    for a in range(SUB):
                        pe.wait_ge(v_out, n * SUB + a)
                        pe.matmul(po, ln[:, a * P:(a + 1) * P], wv[:], start=True, stop=True)\
                          .then_inc(o_mm, 1)

        @block.scalar
        def _(act):
            act.preload_act_table_set(SQRT_SET)
            act.wait_ge(ready, 3)
            for b in range(B):
                with act.Fori(0, NB) as i:
                    n = b * NB + i
                    act.wait_ge(l_mm, n + 1)
                    act.wait_ge(cen_done, n)
                    act.activation(lat[:], pl[:], ACT.Copy).then_inc(lat_done, 1)
                    act.wait_ge(cen_done, n + 1)
                    act.activation(sq[:], cen[:], ACT.Square).then_inc(sq_done, 1)
                    act.wait_ge(v_mm, n + 1)
                    act.activation(sd[:], pv[:], ACT.Sqrt, bias=eps[:]).then_inc(sd_done, 1)
                    act.wait_ge(v_st, n * 16)
                    for a in range(SUB):
                        act.wait_ge(o_mm, n * SUB + a + 1)
                        act.activation(vt[:, a, :, 0:HD], po.rearrange("p (h c) -> p h c", c=HD), ACT.Copy)\
                           .then_inc(v_out, 1)

        @block.vector
        def _(dve):
            dve.sem_inc(turn2, 1)
            dve.wait_ge(weights, 16 * len(loads))
            for b in range(B):
                with dve.Fori(0, NB) as i:
                    n = b * NB + i

                    def rotate(r):
                        u = r % 2
                        k = n * R + r
                        col = bass.ds(i * BLK, BLK)
                        dve.wait_ge(q_mm, k + 1)
                        dve.wait_ge(q_done, k)
                        dve.tensor_tensor(qa[:, u], pq[2 * u][:], cos[:, col], ALU.mult).then_inc(turn1, 1)
                        dve.tensor_tensor(qb[:, u], pq[2 * u + 1][:], sin[:, col], ALU.mult).then_inc(turn2, 1)
                        dve.wait_ge(turn1, k + 1)
                        dve.wait_ge(turn2, k + 2)
                        dve.tensor_tensor(qf[:, u], qa[:, u], qb[:, u], ALU.add).then_inc(q_done, 1)
                        dve.wait_ge(q_done, k + 1)
                        dve.wait_ge(q_st[u], (n * (R // 2) + r // 2) * 16)
                        dve.tensor_copy(parts[:, u, 0], qf[:, u]).then_inc(cut, 1)
                        dve.wait_ge(cut, 3 * k + 1)
                        dve.tensor_tensor(qr[:, u], qf[:, u], parts[:, u, 0], ALU.subtract).then_inc(cut, 1)
                        dve.wait_ge(cut, 3 * k + 2)
                        dve.tensor_copy(parts[:, u, 1], qr[:, u]).then_inc(cut, 1)
                        dve.wait_ge(cut, 3 * k + 3)
                        dve.tensor_tensor(parts[:, u, 2], qr[:, u], parts[:, u, 1], ALU.subtract).then_inc(lo_done, 1)
                        dve.wait_ge(lo_done, k + 1)

                    dve.wait_ge(m_mm, n + 1)
                    dve.wait_ge(nrm_done, n)
                    dve.tensor_tensor(cen[:], lat[:], pm[:], ALU.subtract).then_inc(cen_done, 1)
                    for m in range(KD):
                        rotate(m)
                    dve.wait_ge(sd_done, n + 1)
                    dve.reciprocal(rec[:], sd[:]).then_inc(rec_done, 1)
                    dve.wait_ge(rec_done, n + 1)
                    dve.tensor_tensor(sq[:], cen[:], rec[:], ALU.mult).then_inc(nrm_done, 1)
                    dve.wait_ge(nrm_done, n + 1)
                    dve.wait_ge(o_mm, n * SUB)
                    dve.tensor_scalar(ln[:], sq[:], lg[:], lb[:], ALU.mult, ALU.add).then_inc(ln_done, 1)
                    for m in range(KD):
                        rotate(KD + m)


def attention(nc, alloc, w, scr):
    sb, ps, sem = alloc
    HQ, QB = 4, L // BLK
    ks = [sb(f"at_k{j}", [P, L], BF16) for j in range(HQ)]
    qs = [sb(f"at_q{j}", [P, L], BF16) for j in range(HQ)]
    vs = sb("at_v", [P, L // P, HQ, VW])
    idb, dsel = sb("at_idb", [P, P], BF16), sb("at_dsel", [P, P])
    later = sb("at_later", [P, 2, P], BF16)
    pmx = sb("at_pmx", [P, 2, SUB, HQ, QB])
    neg, res = sb("at_neg", [P, 2, SUB, HQ]), sb("at_res", [P, 2, SUB, HQ])
    msp = sb("at_msp", [P, 2, SUB, HQ, 3], BF16)
    pt = [sb(f"at_p{u}", [P, HQ, BLK]) for u in range(2)]
    ob, rec = sb("at_ob", [P, BLK]), sb("at_rec", [P, BLK])
    on = [sb(f"at_on{u}", [P, BLK]) for u in range(2)]
    p1 = [ps(f"at_p1{j}", [P, BLK]) for j in range(2)]
    p2 = [ps(f"at_p2{j}", [P, 2, BLK]) for j in range(2)]
    po = ps("at_po", [P, BLK])
    pr = ps("at_pr", [P, BLK])
    (consts, ready, q_in, s1_mm, mx_done, cut, s_lo, t_mm, t_out, s2_mm, e_done,
     pv_mm, ob_done, b_mm, rec_done, on_done) = (
        sem(f"at_{n}") for n in ("consts ready q_in s1 mx cut s_lo t_mm t_out s2 e pv "
                                 "ob b_mm rec on").split())
    on_st = [sem(f"at_on_st{u}") for u in range(2)]
    units = [(qb, kt) for qb in range(QB) for kt in range(SUB * (qb + 1))]
    NU = len(units)
    s1_of = [[(a, kc, j) for a in range(SUB) for kc in range(qb + 1) for j in range(HQ)] for qb in range(QB)]
    s1_before = [sum(len(x) for x in s1_of[:qb]) for qb in range(QB + 1)]
    G = B * (NH // HQ)
    E_AHEAD, PV_AHEAD, S1_AHEAD, LOADS_ = 2, 1, 2, HQ * 12 + 1
    last_of = {(qb, SUB * (qb + 1) - 1): qb for qb in range(QB)}

    def s1_at(n):
        qb, kt = units[n]
        if qb + 1 == QB or units[n] in last_of:
            return []
        todo, slots = s1_of[qb + 1], SUB * (qb + 1) - 1
        lo, hi = (len(todo) * x // slots for x in (kt, kt + 1))
        return list(enumerate(todo))[lo:hi]

    def groups(eng, body):
        for b in range(B):
            with eng.Fori(0, NH // HQ) as hq:
                body(b, hq, b * (NH // HQ) + hq)

    with nc.Block() as block:

        @block.sync
        def _(sp):
            for tile, name in ((idb, "idb"), (later, "later"), (dsel, "dsel")):
                sp.dma_start(tile[:], w[name]).then_inc(consts, 16)
            sp.wait_ge(ready, 2 * HQ)

            def body(b, hq, g):
                row, head = hq * (HQ * HD), hq * HQ
                sp.wait_ge(pv_mm, g * NU + PV_AHEAD)
                cols = slice(b * L, (b + 1) * L)
                for j in range(HQ):
                    rows = bass.ds(row + j * HD, HD)
                    part = lambda name, s: scr[name][s, rows, cols]
                    for r in range(3):
                        sp.dma_start(qs[j][r * HD:(r + 1) * HD, :], part("qs", 0)).then_inc(q_in, 16)
                    for r in range(3, 5):
                        sp.dma_start(qs[j][r * HD:(r + 1) * HD, :], part("qs", 1)).then_inc(q_in, 16)
                    sp.dma_start(qs[j][5 * HD:6 * HD, :], part("qs", 2)).then_inc(q_in, 16)
                    for r, s in enumerate((0, 1, 2, 0, 1, 0)):
                        sp.dma_start(ks[j][r * HD:(r + 1) * HD, :], part("ks", s)).then_inc(q_in, 16)
                sp.dma_start(vs[:], scr["v"][b * L:(b + 1) * L, bass.ds(head, HQ), :]
                             .rearrange("(t p) h c -> p t h c", p=P)).then_inc(q_in, 16)
            groups(sp, body)

        @block.gpsimd
        def _(pool):
            for j in range(HQ):
                pool.memset(ks[j][P - 32:P, :], 1.0).then_inc(ready, 1)
            for j in range(HQ):
                pool.memset(qs[j][P - 32:P, :], 0.0).then_inc(ready, 1)

            def body(b, hq, g):
                row = hq * (HQ * HD)
                for qb in range(QB):
                    pool.wait_ge(on_done, g * QB + qb + 1)
                    for j in range(HQ):
                        pool.dma_start(scr["at"][bass.ds(row + j * HD, HD), b * L + qb * BLK:b * L + (qb + 1) * BLK],
                                       on[qb % 2][32 * j:32 * j + HD, :]).then_inc(on_st[qb % 2], 16)
            groups(pool, body)
            for u in range(2):
                pool.wait_ge(on_st[u], G * QB // 2 * HQ * 16)

        @block.tensor
        def _(pe):
            def scores(g, qb, x, item):
                a, kc, j = item
                k = s1_before[qb] + x
                q0, width = (SUB * qb + a) * P, BLK if kc < qb else (a + 1) * P
                pe.wait_ge(mx_done, g * s1_before[QB] + k + 1)
                last = pe.matmul(p1[k % 2][:, 0:width], qs[j][0:6 * HD, q0:q0 + P],
                                 ks[j][0:6 * HD, kc * BLK:kc * BLK + width], start=True, stop=kc < qb)
                if kc == qb:
                    last = pe.matmul(p1[k % 2][:, a * P:width], idb[:], later[:, 0, :], start=False, stop=True)
                last.then_inc(s1_mm, 1)

            def maxima(g, qb):
                pe.wait_ge(s_lo, g * QB + qb + 1)
                for j in range(HQ):
                    pe.wait_ge(t_out, g * (QB * HQ) + qb * HQ + j)
                    for a in range(SUB):
                        last = pe.matmul(pr[6 * HD:6 * HD + 3, a * P:(a + 1) * P], msp[:, qb % 2, a, j, :], idb[:],
                                         start=True, stop=True)
                    last.then_inc(t_mm, 1)

            def values(g, n):
                qb, kt = units[n]
                dk = max(kt - SUB * qb, 0)
                pe.wait_ge(e_done, g * 2 * NU + 2 * n + 2 + E_AHEAD)
                if kt == 0:
                    pe.wait_ge(ob_done, g * QB + qb)
                for j in range(HQ):
                    last = pe.matmul(po[32 * j:32 * j + 32, dk * P:], vs[:, kt, j, :], pt[n % 2][:, j, dk * P:],
                                     start=kt == 0, stop=units[n] in last_of)
                last.then_inc(pv_mm, 1)

            def sums(g, qb):
                pe.wait_ge(ob_done, g * QB + qb + 1)
                pe.matmul(pr[:], dsel[:], ob[:], start=True, stop=True).then_inc(b_mm, 1)

            pe.sem_inc(pv_mm, PV_AHEAD)
            pe.wait_ge(consts, 48)

            def body(b, hq, g):
                pe.wait_ge(q_in, (g + 1) * (LOADS_ * 16))
                for x, item in enumerate(s1_of[0]):
                    scores(g, 0, x, item)
                pe.wait_ge(rec_done, g * QB)
                maxima(g, 0)
                for n, (qb, kt) in enumerate(units):
                    if units[n] in last_of and qb + 1 < QB:
                        maxima(g, qb + 1)
                    if kt == 0:
                        pe.wait_ge(t_out, g * (QB * HQ) + (qb + 1) * HQ)
                    dk = max(kt - SUB * qb, 0)
                    for s in range(2):
                        pe.wait_ge(e_done, g * 2 * NU + 2 * n + s + 1)
                        for j in range(2 * s, 2 * s + 2):
                            last = pe.matmul(p2[s][:, j % 2, dk * P:], ks[j][:, kt * P:(kt + 1) * P],
                                             qs[j][:, qb * BLK + dk * P:(qb + 1) * BLK], start=True, stop=kt < SUB * qb)
                            if kt >= SUB * qb:
                                last = pe.matmul(p2[s][:, j % 2, dk * P:(dk + 1) * P], idb[:], later[:, 1, :],
                                                 start=False, stop=True)
                        last.then_inc(s2_mm, 1)
                    if n >= 1:
                        values(g, n - 1)
                    if n >= 2 and units[n - 2] in last_of:
                        sums(g, last_of[units[n - 2]])
                    for x, item in s1_at(n):
                        scores(g, qb + 1, x, item)
                values(g, NU - 1)
                sums(g, QB - 1)
            groups(pe, body)

        @block.scalar
        def _(act):
            def maxima(g, qb):
                for j in range(HQ):
                    act.wait_ge(t_mm, g * (QB * HQ) + qb * HQ + j + 1)
                    act.activation(qs[j][6 * HD:6 * HD + 3, qb * BLK:(qb + 1) * BLK], pr[6 * HD:6 * HD + 3, :], ACT.Copy)\
                       .then_inc(t_out, 1)

            def take(g, qb, n):
                act.wait_ge(pv_mm, g * NU + n + 1 + PV_AHEAD)
                act.wait_ge(on_done, g * QB + qb)
                act.activation(ob[:], po[:], ACT.Copy).then_inc(ob_done, 1)

            act.preload_act_table_set(LN_EXP)
            act.sem_inc(e_done, E_AHEAD)

            def body(b, hq, g):
                maxima(g, 0)
                for n, (qb, kt) in enumerate(units):
                    if units[n] in last_of and qb + 1 < QB:
                        maxima(g, qb + 1)
                    dk = max(kt - SUB * qb, 0)
                    for s in range(2):
                        act.wait_ge(s2_mm, g * 2 * NU + 2 * n + s + 1)
                        act.wait_ge(pv_mm, g * NU + n)
                        act.activation(pt[n % 2][:, 2 * s:2 * s + 2, dk * P:], p2[s][:, :, dk * P:], ACT.Exp,
                                       scale=float(HD) ** -0.5).then_inc(e_done, 1)
                    if n >= 1 and units[n - 1] in last_of:
                        take(g, last_of[units[n - 1]], n - 1)
                take(g, QB - 1, NU - 1)
            groups(act, body)

        @block.vector
        def _(dve):
            def largest(g, qb, x, item):
                a, kc, j = item
                k = s1_before[qb] + x
                dve.wait_ge(s1_mm, g * s1_before[QB] + k + 1)
                own = pmx[:, qb % 2, a, j, kc:kc + 1]
                width = BLK if kc < qb else (a + 1) * P
                dve.tensor_reduce(own, p1[k % 2][:, 0:width], AX.X, ALU.max).then_inc(mx_done, 1)

            def split(g, qb):
                u, k = qb % 2, (g * QB + qb) * 4
                dve.wait_ge(mx_done, g * s1_before[QB] + s1_before[qb + 1] + S1_AHEAD)
                dve.tensor_reduce(neg[:, u], pmx[:, u, :, :, 0:qb + 1], AX.X, ALU.max, negate=True).then_inc(cut, 1)
                dve.wait_ge(cut, k + 1)
                dve.tensor_copy(msp[:, u, :, :, 0], neg[:, u]).then_inc(cut, 1)
                dve.wait_ge(cut, k + 2)
                dve.tensor_tensor(res[:, u], neg[:, u], msp[:, u, :, :, 0], ALU.subtract).then_inc(cut, 1)
                dve.wait_ge(cut, k + 3)
                dve.tensor_copy(msp[:, u, :, :, 1], res[:, u]).then_inc(cut, 1)
                dve.wait_ge(cut, k + 4)
                dve.tensor_tensor(msp[:, u, :, :, 2], res[:, u], msp[:, u, :, :, 1], ALU.subtract).then_inc(s_lo, 1)

            def norm(g, qb):
                dve.wait_ge(b_mm, g * QB + qb + 1)
                dve.wait_ge(on_done, g * QB + qb)
                dve.reciprocal(rec[:], pr[:]).then_inc(rec_done, 1)
                dve.wait_ge(rec_done, g * QB + qb + 1)
                dve.wait_ge(on_st[qb % 2], (g * (QB // 2) + qb // 2) * (HQ * 16))
                dve.tensor_tensor(on[qb % 2][:], ob[:], rec[:], ALU.mult).then_inc(on_done, 1)

            dve.sem_inc(mx_done, S1_AHEAD)
            dve.wait_ge(consts, 48)

            def body(b, hq, g):
                for x, item in enumerate(s1_of[0]):
                    largest(g, 0, x, item)
                split(g, 0)
                for n, (qb, kt) in enumerate(units):
                    if n >= 2 and units[n - 2] in last_of:
                        norm(g, last_of[units[n - 2]])
                    todo = s1_at(n)
                    for x, item in todo:
                        largest(g, qb + 1, x, item)
                    if todo and todo[-1][0] == len(s1_of[qb + 1]) - 1:
                        split(g, qb + 1)
                norm(g, QB - 1)
            groups(dve, body)


def attention_out(nc, alloc, w, scr, x1, mean3, rstd3, out, scale4):
    sb, ps, sem = alloc
    wo = sb("ao_w", [P, KD, D])
    yt = [sb(f"ao_y{b}", [P, KD, BLK]) for b in range(B)]
    r1 = sb("ao_r1", [P, 2, D])
    raw, mv, tmp = sb("ao_raw", [P, NT, 6]), sb("ao_mv", [P, NT, 2]), sb("ao_tmp", [P, 2, NT])
    po = [ps(f"ao_ps{j}", [P, BLK])[:, 0:D] for j in range(2)]
    weights, mm, res, summed, raw_done, mv_done, step, root_in, root = (
        sem(f"ao_{n}") for n in ("weights", "mm", "res", "summed", "raw", "mv", "step", "root_in", "root"))
    y_in = [sem(f"ao_y_in{b}") for b in range(B)]
    M = B * SUB
    with nc.Block() as block:

        @block.sync
        def _(sp):
            sp.dma_start(wo[:], w["wo"]).then_inc(weights, 16)
            with sp.Fori(0, NB) as i:
                for b in range(B):
                    sp.wait_ge(mm, i * M)
                    sp.dma_start(yt[b][:], scr["at"][:, bass.ds(b * L + i * BLK, BLK)].rearrange("(k p) t -> p k t", p=P))\
                      .then_inc(y_in[b], 16)

        @block.tensor
        def _(pe):
            pe.wait_ge(weights, 16)
            with pe.Fori(0, NB) as i:
                for b in range(B):
                    pe.wait_ge(y_in[b], 16 * (i + 1))
                    for a in range(SUB):
                        pe.wait_ge(summed, i * M + SUB * b + a + 1)
                        for k in range(KD):
                            last = pe.matmul(po[a % 2], yt[b][:, k, a * P:(a + 1) * P], wo[:, k, :],
                                             start=k == 0, stop=k == KD - 1)
                        last.then_inc(mm, 1)

        @block.vector
        def _(dve):
            dve.sem_inc(summed, 2)
            with dve.Fori(0, NB) as i:
                for b in range(B):
                    for a in range(SUB):
                        n = i * M + SUB * b + a
                        t = b * (NT // B) + i * SUB + a
                        at = lambda v: v[:, bass.ds(t, 1)]
                        tok = lambda v: v[:, bass.ds(t, 1), :].rearrange("p a d -> p (a d)")
                        dve.wait_ge(summed, n + 2)
                        dve.tensor_scalar(r1[:, a % 2, :], tok(x1), at(mean3), at(rstd3), ALU.subtract, ALU.mult)\
                           .then_inc(res, 1)
                        dve.wait_ge(res, n + 1)
                        dve.wait_ge(mm, n + 1)
                        dve.tensor_tensor(tok(out), po[a % 2], r1[:, a % 2, :], ALU.add).then_inc(summed, 1)
            dve.wait_ge(summed, NT + 2)
            for t in range(NT):
                dve.bn_stats(raw[:, t, :], out[:, t, :]).then_inc(raw_done, 1)
            for t in range(NT):
                dve.wait_ge(raw_done, t + 1)
                dve.bn_aggr(mv[:, t, :], raw[:, t, :]).then_inc(mv_done, 1)
            dve.wait_ge(mv_done, NT)
            dve.tensor_tensor(tmp[:, 0, :], mv[:, :, 0], mv[:, :, 0], ALU.mult).then_inc(step, 1)
            dve.wait_ge(step, 1)
            dve.tensor_tensor(tmp[:, 1, :], tmp[:, 0, :], mv[:, :, 1], ALU.add).then_inc(step, 1)
            dve.wait_ge(step, 2)
            dve.tensor_scalar(tmp[:, 0, :], tmp[:, 1, :], STD_EPS, None, ALU.add).then_inc(root_in, 1)
            dve.wait_ge(root, 1)
            dve.reciprocal(scale4[:], tmp[:, 1, :]).then_inc(step, 1)

        @block.scalar
        def _(act):
            act.wait_ge(root_in, 1)
            act.activation(tmp[:, 1, :], tmp[:, 0, :], ACT.Sqrt).then_inc(root, 1)


def experts(nc, alloc, w, h_t, x1, acc, out):
    sb, ps, sem = alloc
    gw, gb = sb("ex_gw", [P, KD, NE]), sb("ex_gb", [P, NE])
    w1 = [sb(f"ex_w1{e}", [P, KD, DHID]) for e in range(NE)]
    w2 = [sb(f"ex_w2{e}", [P, DHID // P, D]) for e in range(NE)]
    b1, b2, ones = sb("ex_b1", [P, NE, DHID // P]), sb("ex_b2", [1, NE, D]), sb("ex_ones", [1, P])
    lgt, top, eq, oh, left = (sb("ex_lgt", [P, NT, NE]), sb("ex_top", [P, NT]), sb("ex_eq", [P, NT, NE]),
                              sb("ex_oh", [P, NT, NE]), sb("ex_left", [P, 2, NT]))
    HM = DHID // P
    hid = [sb(f"ex_hid{u}", [P, HM, BLK]) for u in range(2)]
    pg = ps("ex_pg", [P, BLK])
    ph = [ps(f"ex_ph{j}", [P, BLK]) for j in range(4)]
    py = [ps(f"ex_py{j}", [P, BLK])[:, 0:D] for j in range(2)]
    weights, w_in, g_mm, gate, h_mm, relu, y_mm, acc_done, added = (
        sem(f"ex_{n}") for n in ("weights", "w_in", "g_mm", "gate", "h_mm", "relu", "y_mm", "acc", "added"))
    written = sem("ex_written")
    small = [(gw, "gate_w"), (gb, "gate_b"), (b1, "b1"), (b2, "b2"), (ones, "ones")]
    with nc.Block() as block:

        @block.sync
        def _(sp):
            for tile, name in small:
                sp.dma_start(tile[:], w[name]).then_inc(weights, 16)
            for e in range(NE):
                sp.dma_start(w1[e][:], w["w1"][e]).then_inc(w_in, 16)
                sp.dma_start(w2[e][:], w["w2"][e]).then_inc(w_in, 16)
            for b in range(B):
                with sp.Fori(0, NB) as i:
                    sp.wait_ge(acc_done, (b * NB + i + 1) * (NE * SUB) + 2)
                    sp.dma_start(out[b, bass.ds(i * BLK, BLK), :].rearrange("(a p) d -> p a d", p=P),
                                 acc[:, bass.ds(b * (NT // B) + i * SUB, SUB), :]).then_inc(written, 16)
            sp.wait_ge(written, B * NB * 16)

        @block.gpsimd
        def _(pool):
            with pool.Fori(0, NT) as t:
                tok = lambda v: v[:, bass.ds(t, 1), :].rearrange("p a d -> p (a d)")
                pool.tensor_tensor(tok(acc), tok(acc), tok(x1), ALU.add).then_inc(added, 1)

        @block.tensor
        def _(pe):
            pe.wait_ge(weights, 16 * len(small))
            for t in range(NT):
                for k in range(KD):
                    last = pe.matmul(pg[:, t * NE:(t + 1) * NE], h_t[:, k, t * P:(t + 1) * P], gw[:, k, :],
                                     start=k == 0, stop=k == KD - 1)
            last.then_inc(g_mm, 1)
            pe.wait_ge(w_in, 2 * NE * 16)
            for b in range(B):
                with pe.Fori(0, NB) as i:
                    for e in range(NE):
                        x = (b * NB + i) * NE + e
                        for m in range(HM):
                            pe.wait_ge(relu, x * HM + m + 1)
                            for k in range(KD):
                                last = pe.matmul(ph[m % 4][:], w1[e][:, k, m * P:(m + 1) * P],
                                                 h_t[:, k, bass.ds(b * L + i * BLK, BLK)], start=k == 0, stop=k == KD - 1)
                            last.then_inc(h_mm, 1)
                        pe.wait_ge(relu, (x + 1) * HM + 4)
                        for a in range(SUB):
                            pe.wait_ge(acc_done, x * SUB + a + 1)
                            for m in range(HM):
                                pe.matmul(py[a % 2], hid[e % 2][:, m, a * P:(a + 1) * P], w2[e][:, m, :],
                                          start=m == 0, stop=False)
                            pe.matmul(py[a % 2], ones[:], b2[:, e, :], start=False, stop=True).then_inc(y_mm, 1)

        @block.scalar
        def _(act):
            act.sem_inc(relu, 4)
            act.wait_ge(weights, 16 * len(small))
            for b in range(B):
                with act.Fori(0, NB) as i:
                    for e in range(NE):
                        x = (b * NB + i) * NE + e
                        act.wait_ge(y_mm, x * SUB)
                        for m in range(HM):
                            act.wait_ge(h_mm, x * HM + m + 1)
                            act.activation(hid[e % 2][:, m, :], ph[m % 4][:], ACT.Relu, bias=b1[:, e, m:m + 1])\
                               .then_inc(relu, 1)

        @block.vector
        def _(dve):
            dve.wait_ge(g_mm, 1)
            n = 0

            def step(ins):
                nonlocal n
                n += 1
                ins.then_inc(gate, 1)
                dve.wait_ge(gate, n)

            step(dve.tensor_tensor(lgt[:], pg[:, 0:NT * NE].rearrange("p (t e) -> p t e", e=NE),
                                   gb[:].unsqueeze(1).broadcast_to([P, NT, NE]), ALU.add))
            step(dve.tensor_reduce(top[:], lgt[:], AX.X, ALU.max))
            step(dve.tensor_tensor(eq[:], lgt[:], top[:].unsqueeze(2).broadcast_to([P, NT, NE]), ALU.is_equal))
            step(dve.memset(left[:, 0, :], 1.0))
            for e in range(NE):
                step(dve.tensor_tensor(oh[:, :, e], eq[:, :, e], left[:, e % 2, :], ALU.mult))
                step(dve.tensor_tensor(left[:, (e + 1) % 2, :], left[:, e % 2, :], oh[:, :, e], ALU.subtract))
            dve.sem_inc(acc_done, 2)
            dve.wait_ge(added, NT)
            for b in range(B):
                with dve.Fori(0, NB) as i:
                    for e in range(NE):
                        for a in range(SUB):
                            k = ((b * NB + i) * NE + e) * SUB + a
                            t = b * (NT // B) + i * SUB + a
                            tok = lambda v: v[:, bass.ds(t, 1), :].rearrange("p a d -> p (a d)")
                            dve.wait_ge(y_mm, k + 1)
                            if e >= 1:
                                dve.wait_ge(acc_done, k - SUB + 1 + 2)
                            dve.scalar_tensor_tensor(tok(acc), py[a % 2],
                                                     oh[:, bass.ds(t, 1), e:e + 1].rearrange("p a b -> p (a b)"), tok(acc),
                                                     ALU.mult, ALU.add).then_inc(acc_done, 1)


def program(nc, a, out):
    ctx = ExitStack()
    with ctx:
        def scope(stack):
            def sb(name, shape, dt=F32):
                return stack.enter_context(nc.sbuf_tensor(name, shape, dt))

            def ps(name, shape, dt=F32):
                return stack.enter_context(nc.psum_tensor(name, shape, dt))

            def sem(name):
                return ctx.enter_context(nc.semaphore(name))
            return sb, ps, sem

        sb, ps, sem = scope(ctx)
        scr = {n: nc.dram_tensor(f"scr_{n}", s, F32, kind="Internal").ap() for n, s in
               {n: (HP, SB_, P, DH, B, TB) for n in ("zs", "xc", "dl", "ux", "bc", "yg")}.items()}
        scr.update({n: nc.dram_tensor(f"scr_{n}", sh, dt, kind="Internal").ap() for n, sh, dt in
                    (("qs", (3, D, TOK), BF16), ("ks", (3, D, TOK), BF16), ("v", (TOK, NH, VW), F32),
                     ("at", (D, TOK), F32))})
        ident = sb("ident", [P, P])
        mean, rstd = sb("mean", [P, NT]), sb("rstd", [P, NT])
        mean3, rstd3, scale3, scale4 = (sb(n, [P, NT]) for n in ("mean3", "rstd3", "scale3", "scale4"))
        with nc.Block() as block:
            ident_in = sem("ident_in")

            @block.sync
            def _(sp):
                sp.dma_start(ident[:], a["ident"]).then_inc(ident_in, 16)
                sp.wait_ge(ident_in, 16)
        with ExitStack() as phase:
            xn_t = scope(phase)[0]("xn_t", [P, KD, TOK])
            with ExitStack() as part:
                xs, scale = scope(part)[0]("in_tokens", [P, NT, D]), scope(part)[0]("in_scale", [P, NT])
                input_stats(nc, scope(part), a["x"], xs, mean, rstd, scale)
                to_features(nc, scope(part), "f1", xs, mean, scale, a["in_alpha"], a["in_beta"], ident, xn_t)
            with ExitStack() as part:
                projections(nc, scope(part), a, xn_t, scr)
        with ExitStack() as part:
            selective_scan(nc, scope(part), a, scr)
        x1 = sb("x1", [P, NT, D])
        with ExitStack() as part:
            back_to_tokens(nc, scope(part), a, scr, a["x"], mean, rstd, x1, mean3, scale3, rstd3)
        with ExitStack() as phase:
            h_t = scope(phase)[0]("h1_t", [P, KD, TOK])
            with ExitStack() as part:
                to_features(nc, scope(part), "f2", x1, mean3, scale3, a["norm1"], None, ident, h_t)
            with ExitStack() as part:
                latents(nc, scope(part), a, h_t, scr)
        with ExitStack() as part:
            attention(nc, scope(part), a, scr)
        acc = sb("acc", [P, NT, D])
        with ExitStack() as part:
            attention_out(nc, scope(part), a, scr, x1, mean3, rstd3, acc, scale4)
        with ExitStack() as phase:
            h_t = scope(phase)[0]("h2_t", [P, KD, TOK])
            with ExitStack() as part:
                to_features(nc, scope(part), "f3", acc, None, scale4, a["norm2"], None, ident, h_t)
            with ExitStack() as part:
                experts(nc, scope(part), a, h_t, x1, acc, out)


def host_layouts(inputs):
    g = lambda n: np.ascontiguousarray(inputs[n])
    cols = lambda v, n: np.ascontiguousarray(v.reshape(n, P).T)
    rows_t = lambda w: np.ascontiguousarray(w.T.reshape(w.shape[1] // P, P, w.shape[0]).transpose(1, 0, 2))
    a = {"x": g("L0_attn_x"), "ident": np.eye(P, dtype=np.float32)}
    a["in_alpha"], a["in_beta"] = cols(g("L0_attn_in_norm_alpha"), KD), cols(g("L0_attn_in_norm_bias"), KD)
    a["in_w"], a["in_b"] = rows_t(g("L0_attn_in_proj_w")), cols(g("L0_attn_in_proj_b"), 2 * MI)
    a["cv_w"] = np.ascontiguousarray(g("L0_attn_conv_w").reshape(MI, P, KC).transpose(1, 0, 2))
    a["cv_b"] = cols(g("L0_attn_conv_b"), MI)
    a["dt_w"], a["dt_b"] = rows_t(g("L0_attn_dt_proj_w")), cols(g("L0_attn_dt_proj_b"), MI)
    bc = g("L0_attn_x_proj_w").reshape(2, NS, DI)
    rep = np.tile(bc, (1, P // NS, 1))
    a["bc_w"] = np.ascontiguousarray(rep.reshape(2, P, MI, P).transpose(3, 2, 0, 1))
    a["bc_b"] = np.ascontiguousarray(np.tile(g("L0_attn_x_proj_b").reshape(2, NS), (1, P // NS)).T)
    wide = lambda v: np.ascontiguousarray(np.broadcast_to(v, (P,) + v.shape))
    a["out_w"], a["out_b"] = rows_t(g("L0_attn_out_proj_w")), wide(g("L0_attn_out_proj_b"))
    a["gamma"], a["beta"] = wide(g("L0_attn_norm_alpha")), wide(g("L0_attn_norm_bias"))
    a["norm1"], a["norm2"] = cols(g("L0_ffn_norm1_w"), KD), cols(g("L0_ffn_norm2_w"), KD)
    half = lambda v: np.ascontiguousarray(v.reshape(NH, 2, HD // 2, -1)[:, ::-1].reshape(D, -1))
    both = lambda v: np.concatenate([v, half(v)], 0)
    a["wq"] = rows_t(both(g("L0_ffn_Wq")))
    a["wk"] = np.ascontiguousarray(both(g("L0_ffn_Wuk")).T)
    a["wl"] = rows_t(g("L0_ffn_Wdkv"))
    a["wv"] = np.ascontiguousarray(g("L0_ffn_Wuv").T)
    a["wo"] = rows_t(g("L0_ffn_Wo"))
    a["ln_g"], a["ln_b"] = cols(g("L0_ffn_ln_g"), 1), cols(g("L0_ffn_ln_b"), 1)
    inv = (1.0 / np.float32(10000.0) ** (np.arange(HD // 2, dtype=np.float32) / np.float32(HD // 2))).astype(np.float32)
    ang = inv[np.arange(P) % (HD // 2)][:, None] * np.arange(L, dtype=np.float32)[None]
    sign = np.where(np.arange(P) % HD < HD // 2, -1.0, 1.0).astype(np.float32)[:, None]
    a["cos"], a["sin"] = np.cos(ang).astype(np.float32), (np.sin(ang) * sign).astype(np.float32)
    a["avg"] = np.full((P, P), 1.0 / LAT, np.float32)
    a["idb"] = np.eye(P).astype(mybir.dt.np(BF16))
    later = np.where(np.arange(P)[None] > np.arange(P)[:, None], -1.0e30, 0.0)
    a["later"] = np.ascontiguousarray(np.stack([later, later.T], 1).astype(mybir.dt.np(BF16)))
    a["dsel"] = np.ascontiguousarray((np.arange(P)[:, None] == 32 * (np.arange(P)[None] // 32) + HD).astype(np.float32))
    a["gate_w"], a["gate_b"] = rows_t(g("L0_ffn_gate_w")), wide(g("L0_ffn_gate_b"))
    a["w1"] = np.stack([rows_t(v) for v in g("L0_ffn_W1")])
    a["w2"] = np.stack([rows_t(v) for v in g("L0_ffn_W2")])
    a["b1"] = np.ascontiguousarray(g("L0_ffn_b1").reshape(NE, DHID // P, P).transpose(2, 0, 1))
    a["b2"], a["ones"] = g("L0_ffn_b2")[None], np.ones((1, P), np.float32)
    p, eye = np.arange(P), np.eye(P, dtype=np.float32)
    pick = np.stack([eye[:, 8 * i + p // NS] for i in range(4)], 1)
    a["sel"] = np.ascontiguousarray(np.tile(pick[:32], (4, 1, 1)))
    a["ysel"] = np.ascontiguousarray(np.stack([(np.arange(32)[None] == 8 * i + p[:, None] // NS) for i in range(4)], 1)
                                     .astype(np.float32))
    a["pool16"] = np.ascontiguousarray((p[:, None] // NS == p[None] // NS).astype(np.float32))
    a_log = g("L0_attn_A_log").reshape(HP, DH, 4, 4, GD * NS)
    order = np.array([tile_place(s) for s in range(TL)])
    par = np.zeros((P, HP, SB_, TL + DH + 1), np.float32)
    for h in range(HP):
        par[:, h, :, :TL] = a_log[h, order[:, 0], order[:, 1], order[:, 2]].T[:, None]
        par[:, h, :, TL:TL + DH] = g("L0_attn_D").reshape(HP, DH, P)[h].T[:, None]
    par[:, :, 1:, TL + DH] = 1.0
    a["par"] = np.ascontiguousarray(par.reshape(P, HP * SB_, TL + DH + 1))
    return a


def kernel(**inputs):
    import concourse.bacc as _bacc
    from concourse.bass_utils import run_bass_kernel_spmd as _run

    nc = _bacc.Bacc("TRN2", target_bir_lowering=False, num_devices=1)
    arrays, aps = {}, {}
    for name, v in host_layouts(inputs).items():
        arrays[f"in_{name}"] = v
        aps[name] = nc.dram_tensor(f"in_{name}", v.shape, mybir.dt.from_np(v.dtype), kind="ExternalInput").ap()
    out = nc.dram_tensor("out_0_dram", (B, L, D), F32, kind="ExternalOutput").ap()
    program(nc, aps, out)
    r = _run(nc, [arrays], core_ids=[0])
    return r.results[0]["out_0_dram"]
```

```python
from contextlib import ExitStack

import numpy as np

import concourse.bass as bass
from concourse import mybir

F32 = mybir.dt.float32
BF16 = mybir.dt.bfloat16
ALU = mybir.AluOpType
ACT = mybir.ActivationFunctionType
AX = mybir.AxisListType

P = 128
B, L, D = 2, 2048, 256
DI, NS, KC = 512, 16, 4
TOK = B * L
NT = TOK // P
KD = D // P
MI = DI // P
BLK = 512
NB = L // BLK
HP = 2
DH = MI // HP
TB = 128
SB_ = L // TB
SUB = BLK // TB
CH = 16
NC_ = TB // CH
GD = P // NS
TL = DH * P // GD
ST = TL * B
W1 = CH + 1
IT = 8
TI = TL // IT
NH, HD, LAT = 16, 16, 128
VW = 32
NE, DHID = 4, 1024
H_MAX = 10.0
INP_AT = [(), (0,), (1,), (2,), (3,), (4,), (5,), (6, 7)]
SUMS_AT = [(0, 1, 2, 3), (4, 5), (6, 7), (), (), (), (), ()]
SPREAD_AT = [(0,), (1,), (2,), (3,), (4,), (5,), (6,), (7,)]
DA_MIN = float(np.exp(np.float32(-10.0)))
LN_EPS = 1e-5
STD_EPS = 1e-6
BESSEL = D / (D - 1)
DT_MIN, DT_MAX = 1e-4, 10.0
LN_EXP, SQRT_SET = "natural_log_exp_and_others", "sqrt_and_others"


def sliced(ap, start, size):
    return ap[bass.ds(start, size)]


def token_rows(t, j, n, per=1):
    return t[:, bass.ds(j, n)]


def input_stats(nc, alloc, x, xs, mean, rstd, scale):
    sb, ps, sem = alloc
    raw = sb("in_bn_raw", [P, NT, 6])
    mv = sb("in_mean_var", [P, NT, 2])
    tmp = sb("in_tmp", [P, 4, NT])
    LOADS = 4
    per = NT // LOADS
    x_in = [sem(f"in_x_in{j}") for j in range(LOADS)]
    raw_done, mv_done, var_eps, roots, step = (sem(f"in_{n}") for n in ("raw", "mv", "var_eps", "roots", "step"))
    xt = x.rearrange("b (t p) d -> p (b t) d", p=P)
    with nc.Block() as block:

        @block.sync
        def _(sp):
            for j in range(LOADS):
                sp.dma_start(xs[:, j * per:(j + 1) * per, :], xt[:, j * per:(j + 1) * per, :]).then_inc(x_in[j], 16)

        @block.vector
        def _(dve):
            for j in range(LOADS):
                dve.wait_ge(x_in[j], 16)
                for t in range(j * per, (j + 1) * per):
                    dve.bn_stats(raw[:, t, :], xs[:, t, :]).then_inc(raw_done, 1)
            for t in range(NT):
                dve.wait_ge(raw_done, t + 1)
                dve.bn_aggr(mv[:, t, :], raw[:, t, :]).then_inc(mv_done, 1)
            dve.wait_ge(mv_done, NT)
            dve.tensor_scalar(tmp[:, 0, :], mv[:, :, 1], LN_EPS, None, ALU.add).then_inc(var_eps, 1)
            dve.tensor_copy(mean[:], mv[:, :, 0]).then_inc(step, 1)
            dve.wait_ge(roots, 2)
            dve.reciprocal(rstd[:], tmp[:, 1, :]).then_inc(step, 1)
            dve.wait_ge(step, 2)
            dve.tensor_tensor(tmp[:, 3, :], tmp[:, 2, :], rstd[:], ALU.mult).then_inc(step, 1)
            dve.wait_ge(step, 3)
            dve.tensor_scalar(scale[:], tmp[:, 3, :], STD_EPS, None, ALU.add).then_inc(step, 1)
            dve.wait_ge(step, 4)
            dve.reciprocal(tmp[:, 3, :], scale[:]).then_inc(step, 1)
            dve.wait_ge(step, 5)
            dve.tensor_tensor(scale[:], tmp[:, 3, :], rstd[:], ALU.mult).then_inc(step, 1)

        @block.scalar
        def _(act):
            act.wait_ge(var_eps, 1)
            act.activation(tmp[:, 1, :], tmp[:, 0, :], ACT.Sqrt).then_inc(roots, 1)
            act.activation(tmp[:, 2, :], mv[:, :, 1], ACT.Sqrt, scale=BESSEL).then_inc(roots, 1)


def to_features(nc, alloc, tag, xs, mean, scale, alpha, beta, ident, out):
    sb, ps, sem = alloc
    centred = [sb(f"{tag}_centred{u}", [P, 4, D]) for u in range(2)]
    weight, bias = sb(f"{tag}_weight", [P, KD]), sb(f"{tag}_bias", [P, KD])
    tr = [[ps(f"{tag}_tr{u}{k}", [P, BLK]) for k in range(KD)] for u in range(2)]
    w_in, scaled, turned, stored = (sem(f"{tag}_{n}") for n in ("w_in", "scaled", "turned", "stored"))
    loads = [(weight, alpha)] + ([(bias, beta)] if beta is not None else [])
    with nc.Block() as block:

        @block.sync
        def _(sp):
            for tile, src in loads:
                sp.dma_start(tile[:], src).then_inc(w_in, 16)

        @block.vector
        def _(dve):
            for g in range(NT // 4):
                if g >= 2:
                    dve.wait_ge(turned, 2 * (g - 1))
                for a in range(4):
                    t = 4 * g + a
                    if mean is None:
                        dve.tensor_scalar(centred[g % 2][:, a, :], xs[:, t, :], scale[:, t:t + 1], None,
                                          ALU.mult).then_inc(scaled, 1)
                    else:
                        dve.tensor_scalar(centred[g % 2][:, a, :], xs[:, t, :], mean[:, t:t + 1], scale[:, t:t + 1],
                                          ALU.subtract, ALU.mult).then_inc(scaled, 1)

        @block.scalar
        def _(act):
            act.wait_ge(w_in, 16 * len(loads))
            for g in range(NT // 4):
                for k in range(KD):
                    act.wait_ge(turned, KD * g + k + 1)
                    act.activation(out[:, k, g * BLK:(g + 1) * BLK], tr[g % 2][k][:], ACT.Identity,
                                   bias=bias[:, k:k + 1] if beta is not None else 0.0,
                                   scale=weight[:, k:k + 1]).then_inc(stored, 1)

        @block.tensor
        def _(pe):
            for g in range(NT // 4):
                pe.wait_ge(scaled, 4 * g + 4)
                for k in range(KD):
                    if g >= 2:
                        pe.wait_ge(stored, KD * (g - 2) + k + 1)
                    for a in range(4):
                        last = pe.transpose(tr[g % 2][k][:, a * P:(a + 1) * P],
                                            centred[g % 2][:, a, k * P:(k + 1) * P], ident[:])
                    last.then_inc(turned, 1)


def projections(nc, alloc, w, xn_t, scr):
    sb, ps, sem = alloc
    w_in = sb("pj_w_in", [P, KD, 2 * DI])
    b_in = sb("pj_b_in", [P, 2 * MI])
    w_cv = sb("pj_w_cv", [P, MI, KC])
    b_cv = sb("pj_b_cv", [P, MI])
    w_dt = sb("pj_w_dt", [P, MI, DI])
    b_dt = sb("pj_b_dt", [P, MI])
    w_bc = sb("pj_w_bc", [P, MI, 2, P])
    b_bc = sb("pj_b_bc", [P, 2])
    halo = KC - 1
    xin = [sb(f"pj_xin{b}", [P, MI, halo + BLK]) for b in range(B)]
    cv = [sb(f"pj_cv{b}", [P, MI, BLK]) for b in range(B)]
    xc = [sb(f"pj_xc{b}", [P, MI, BLK]) for b in range(B)]
    zs = [sb(f"pj_zs{b}", [P, MI, BLK]) for b in range(B)]
    dl = [sb(f"pj_dl{b}", [P, MI, BLK]) for b in range(B)]
    ux = [sb(f"pj_ux{b}", [P, MI, BLK]) for b in range(B)]
    bc = [sb(f"pj_bc{b}", [P, 2, BLK]) for b in range(B)]
    cuts = [sb(f"pj_{n}_cuts", [P, 3, MI, BLK], BF16) for n in ("dl", "ux")]
    ps_x = [ps(f"pj_ps_x{j}", [P, BLK]) for j in range(2)]
    ps_z = [ps(f"pj_ps_z{j}", [P, BLK]) for j in range(2)]
    ps_d = [ps(f"pj_ps_d{j}", [P, BLK]) for j in range(2)]
    ps_b = [ps(f"pj_ps_b{j}", [P, BLK]) for j in range(2)]
    weights = sem("pj_weights")
    x_mm, z_mm, d_mm, b_mm = (sem(f"pj_{n}_mm") for n in "xzdb")
    x_out, z_out, d_out, b_out = (sem(f"pj_{n}_out") for n in "xzdb")
    zeroed, halo_ok, tap, conv_done = sem("pj_zeroed"), sem("pj_halo"), sem("pj_tap"), sem("pj_conv")
    xc_done, exp_done, ln_done = sem("pj_xc"), sem("pj_exp"), sem("pj_ln")
    dl_done, ux_done = sem("pj_dl"), sem("pj_ux")
    act_stored = [sem(f"pj_act_stored{b}") for b in range(B)]
    hi_done, rest_done, cut = sem("pj_hi"), sem("pj_rest"), sem("pj_cut")
    cut_stored = [sem(f"pj_{n}_stored") for n in ("dl", "ux")]
    ACT_ST, CUT_ST = 3 * HP * 16, 3 * HP * 16
    M2 = B * MI
    loads = [(w_in, w["in_w"]), (b_in, w["in_b"]), (w_cv, w["cv_w"]), (b_cv, w["cv_b"]), (w_dt, w["dt_w"]),
             (b_dt, w["dt_b"]), (w_bc, w["bc_w"]), (b_bc, w["bc_b"])]
    with nc.Block() as block:

        @block.gpsimd
        def _(pool):
            for tile, src in loads:
                pool.dma_start(tile[:], src).then_inc(weights, 16)
            with pool.Fori(0, NB) as i:
                for b in range(B):
                    for t, rest in enumerate((dl[b], ux[b])):
                        n = (i * B + b) * 2 + t
                        pool.wait_ge(hi_done, n + 1)
                        pool.tensor_tensor(cuts[t][:, 1], rest[:], cuts[t][:, 0], ALU.subtract).then_inc(cut, 1)
                        pool.wait_ge(cut, 2 * n + 1)
                        pool.tensor_tensor(rest[:], rest[:], cuts[t][:, 0], ALU.subtract).then_inc(cut, 1)
                        pool.wait_ge(cut, 2 * n + 2)
                        pool.tensor_tensor(cuts[t][:, 2], rest[:], cuts[t][:, 1], ALU.subtract).then_inc(rest_done, 1)

        @block.sync
        def _(sp):
            def store(name, tile, i, b, done):
                n = tile.shape[1] // (HP if name != "bc" else 1)
                for h in range(HP):
                    own = tile[:, h * n:(h + 1) * n, :] if name != "bc" else tile[:]
                    sp.dma_start(scr[name][h, bass.ds(i * SUB, SUB), :, :, b, :].rearrange("n p d t -> p d n t"),
                                 own.rearrange("p d (n t) -> p d n t", t=TB)).then_inc(done, 16)

            with sp.Fori(0, NB) as i:
                for b in range(B):
                    sp.wait_ge(z_out, i * M2 + MI * (b + 1) + 2)
                    store("zs", zs[b], i, b, act_stored[b])
                    sp.wait_ge(xc_done, i * M2 + MI * (b + 1))
                    store("xc", xc[b], i, b, act_stored[b])
                for b in range(B):
                    sp.wait_ge(b_out, i * 2 * B + 2 * (b + 1) + 2)
                    store("bc", bc[b], i, b, act_stored[b])
                    for t, name in enumerate(("dl", "ux")):
                        sp.wait_ge(rest_done, (i * B + b) * 2 + t + 1)
                        for h in range(HP):
                            for part in range(3):
                                sp.dma_start(
                                    scr[name][h, bass.ds(i * SUB, SUB), part, :, :, b, :].rearrange("n p d t -> p d n t"),
                                    cuts[t][:, part, h * DH:(h + 1) * DH, :].rearrange("p d (n t) -> p d n t", t=TB))\
                                  .then_inc(cut_stored[t], 16)
            for b in range(B):
                sp.wait_ge(act_stored[b], NB * ACT_ST)
            for t in range(2):
                sp.wait_ge(cut_stored[t], NB * B * CUT_ST)

        @block.tensor
        def _(pe):
            pe.wait_ge(weights, 16 * len(loads))
            with pe.Fori(0, NB) as i:
                for b in range(B):
                    rhs = [xn_t[:, k, bass.ds(b * L + i * BLK, BLK)] for k in range(KD)]
                    for m in range(MI):
                        pe.wait_ge(x_out, i * M2 + MI * b + m + 1)
                        for k in range(KD):
                            mm = pe.matmul(ps_x[m % 2][:], w_in[:, k, m * P:(m + 1) * P], rhs[k],
                                           start=k == 0, stop=k == KD - 1)
                        mm.then_inc(x_mm, 1)
                        pe.wait_ge(z_out, i * M2 + MI * b + m + 1)
                        for k in range(KD):
                            mm = pe.matmul(ps_z[m % 2][:], w_in[:, k, DI + m * P:DI + (m + 1) * P], rhs[k],
                                           start=k == 0, stop=k == KD - 1)
                        mm.then_inc(z_mm, 1)
                for b in range(B):
                    pe.wait_ge(xc_done, i * M2 + MI * (b + 1))
                    for c in range(2):
                        pe.wait_ge(b_out, i * 2 * B + 2 * b + c + 1)
                        for k in range(MI):
                            mm = pe.matmul(ps_b[c][:], w_bc[:, k, c, :], xc[b][:, k, :], start=k == 0, stop=k == MI - 1)
                        mm.then_inc(b_mm, 1)
                    for m in range(MI):
                        pe.wait_ge(d_out, i * M2 + MI * b + m + 1)
                        for k in range(MI):
                            mm = pe.matmul(ps_d[m % 2][:], w_dt[:, k, m * P:(m + 1) * P], xc[b][:, k, :],
                                           start=k == 0, stop=k == MI - 1)
                        mm.then_inc(d_mm, 1)

        @block.vector
        def _(dve):
            for b in range(B):
                dve.memset(xin[b][:], 0.0).then_inc(zeroed, 1)
            dve.sem_inc(x_out, 2)
            dve.sem_inc(d_out, 2)
            dve.wait_ge(weights, 16 * len(loads))
            dve.wait_ge(zeroed, B)
            with dve.Fori(0, NB) as i:
                for b in range(B):
                    dve.wait_ge(conv_done, i * M2)
                    dve.tensor_copy(xin[b][:, :, 0:halo], xin[b][:, :, BLK:BLK + halo]).then_inc(halo_ok, 1)
                    dve.wait_ge(halo_ok, i * B + b + 1)
                    dve.wait_ge(xc_done, i * M2)
                    for m in range(MI):
                        n = i * M2 + MI * b + m
                        dve.wait_ge(x_mm, n + 1)
                        dve.tensor_scalar(xin[b][:, m, halo:], ps_x[m % 2][:], b_in[:, m:m + 1], None,
                                          ALU.add).then_inc(x_out, 1)
                        dve.wait_ge(x_out, n + 3)
                        dve.tensor_scalar(cv[b][:, m, :], xin[b][:, m, 0:BLK], w_cv[:, m, 0:1], b_cv[:, m:m + 1],
                                          ALU.mult, ALU.add).then_inc(tap, 1)
                        for j in range(1, KC):
                            dve.wait_ge(tap, n * (KC - 1) + j)
                            dve.scalar_tensor_tensor(cv[b][:, m, :], xin[b][:, m, j:j + BLK], w_cv[:, m, j:j + 1],
                                                     cv[b][:, m, :], ALU.mult, ALU.add)\
                               .then_inc(tap if j < KC - 1 else conv_done, 1)
                for b in range(B):
                    dve.wait_ge(rest_done, i * 2 * B)
                    for m in range(MI):
                        n = i * M2 + MI * b + m
                        dve.wait_ge(d_mm, n + 1)
                        dve.tensor_scalar(dl[b][:, m, :], ps_d[m % 2][:], b_dt[:, m:m + 1], 20.0,
                                          ALU.add, ALU.min).then_inc(d_out, 1)
                    for m in range(MI):
                        n = i * M2 + MI * b + m
                        dve.wait_ge(ln_done, n + 1)
                        dve.tensor_scalar(dl[b][:, m, :], dl[b][:, m, :], DT_MIN, DT_MAX,
                                          ALU.max, ALU.min).then_inc(dl_done, 1)
                        dve.wait_ge(dl_done, n + 1)
                        dve.tensor_tensor(ux[b][:, m, :], dl[b][:, m, :], xc[b][:, m, :], ALU.mult).then_inc(ux_done, 1)
                    dve.wait_ge(ux_done, i * M2 + MI * (b + 1))
                    for t, whole in enumerate((dl[b], ux[b])):
                        dve.wait_ge(cut_stored[t], (i * B + b) * CUT_ST)
                        dve.tensor_copy(cuts[t][:, 0], whole[:]).then_inc(hi_done, 1)

        @block.scalar
        def _(act):
            act.sem_inc(z_out, 2)
            act.sem_inc(b_out, 2)
            act.wait_ge(weights, 16 * len(loads))
            with act.Fori(0, NB) as i:
                for b in range(B):
                    act.wait_ge(act_stored[b], i * ACT_ST)
                    for m in range(MI):
                        n = i * M2 + MI * b + m
                        act.wait_ge(z_mm, n + 1)
                        act.activation(zs[b][:, m, :], ps_z[m % 2][:], ACT.Silu,
                                       bias=b_in[:, MI + m:MI + m + 1]).then_inc(z_out, 1)
                        act.wait_ge(conv_done, n + 1)
                        act.activation(xc[b][:, m, :], cv[b][:, m, :], ACT.Silu).then_inc(xc_done, 1)
                for b in range(B):
                    for c in range(2):
                        act.wait_ge(b_mm, i * 2 * B + 2 * b + c + 1)
                        act.activation(bc[b][:, c, :], ps_b[c][:], ACT.Identity, bias=b_bc[:, c:c + 1])\
                           .then_inc(b_out, 1)
                    for m in range(MI):
                        n = i * M2 + MI * b + m
                        act.wait_ge(d_out, n + 3)
                        act.activation(dl[b][:, m, :], dl[b][:, m, :], ACT.Exp).then_inc(exp_done, 1)
                        act.wait_ge(exp_done, n + 1)
                        act.activation(dl[b][:, m, :], dl[b][:, m, :], ACT.Ln, bias=1.0).then_inc(ln_done, 1)



def tile_place(st):
    item, jr, e = st // TI, (st % TI) // 2, st % 2
    d, q, r = item // 4, item // 2 % 2, item % 2
    return d, 2 * r + jr, 2 * q + e


def selective_scan(nc, alloc, w, scr):
    sb, ps, sem = alloc
    NJ = HP * SB_
    sel = sb("sc_sel", [3 * 32, 4, P], BF16)
    ysel = sb("sc_ysel", [P, 4, 32])
    pool16 = sb("sc_pool16", [P, P])
    par = sb("sc_par", [P, NJ, TL + DH + 1])
    dA = [sb(f"sc_dA{q}", [P, NC_, ST, W1]) for q in range(2)]
    hb = [sb(f"sc_h{q}", [P, NC_, ST, W1]) for q in range(2)]
    dl = [sb(f"sc_dl{q}", [3 * 32, DH, 4, B, TB], BF16) for q in range(2)]
    ux = [sb(f"sc_ux{q}", [3 * 32, DH, 4, B, TB], BF16) for q in range(2)]
    bt = [sb(f"sc_b{q}", [P, B, TB]) for q in range(2)]
    ct = [sb(f"sc_c{q}", [P, B, TB]) for q in range(2)]
    xc = [sb(f"sc_xc{q}", [P, DH, B, TB]) for q in range(2)]
    zs = [sb(f"sc_zs{q}", [P, DH, B, TB]) for q in range(2)]
    yv = [sb(f"sc_yv{q}", [P, DH, B, TB]) for q in range(2)]
    yg = [sb(f"sc_yg{q}", [P, DH, B, TB]) for q in range(2)]
    sq = sb("sc_sq", [P, ST])
    mx = sb("sc_mx", [P, ST])
    lg = sb("sc_lg", [P, ST])
    scl = [sb(f"sc_scl{q}", [P, ST]) for q in range(2)]
    ps_d = [ps(f"sc_ps_d{q}", [P, 2, 2, B * TB]) for q in range(2)]
    ps_u = ps("sc_ps_u", [P, 2, 2, B * TB])
    ps_y = ps("sc_ps_y", [P, DH, B * TB])
    ps_n = ps("sc_ps_n", [P, BLK])

    consts, decay = sem("sc_consts"), sem("sc_decay")
    cleared = sem("sc_cleared")
    in_a = [sem(f"sc_in_a{q}") for q in range(2)]
    in_c = [sem(f"sc_in_c{q}") for q in range(2)]
    in_x = [sem(f"sc_in_x{q}") for q in range(2)]
    stored = [sem(f"sc_stored{q}") for q in range(2)]
    d_mm, u_mm, n_mm, y_mm = (sem(f"sc_{n}_mm") for n in "duny")
    exp_done, clip_done, inp_done = sem("sc_exp"), sem("sc_clip"), sem("sc_inp")
    scan_done, sq_done, mx_done, lg_done, scl_done, head_done = (
        sem(f"sc_{n}") for n in ("scan", "sq", "mx", "lg", "scl", "head"))
    last_done, c_done = sem("sc_last"), sem("sc_cmul")
    y_done, gate_done = sem("sc_y"), sem("sc_gate")
    IN_A = (2 * 3 * 4 + 1) * 16
    EXP_AHEAD, LAST_AHEAD, GATE_AHEAD = 2 * TI, 1, 2

    def turns(eng, turn):
        for u in range(2):
            turn(u, u, 0, u == 0, False)
        with eng.Fori(1, NJ // 2 - 1) as m:
            for u in range(2):
                turn(2 * m + u, u, m, False, False)
        for u in range(2):
            turn(NJ - 2 + u, u, NJ // 2 - 1, False, u == 1)

    blocks = {n: scr[n].rearrange("h n p d b t -> (h n) p d b t") for n in ("xc", "zs", "yg", "bc")}
    cut_blocks = {n: scr[n].rearrange("h n s p d b t -> (h n) s p d b t") for n in ("dl", "ux")}

    def block_of(name, j):
        return blocks[name][bass.ds(j, 1)].rearrange("n p d b t -> (n p) d b t")

    with nc.Block() as block:

        @block.sync
        def _(sp):
            def load_a(j, q):
                for name, tile in (("dl", dl[q]), ("ux", ux[q])):
                    for part in range(3):
                        for quad in range(4):
                            src = cut_blocks[name][bass.ds(j, 1), part, 32 * quad:32 * quad + 32]
                            sp.dma_start(tile[32 * part:32 * part + 32, :, quad],
                                         src.rearrange("n p d b t -> (n p) d b t")).then_inc(in_a[q], 16)
                sp.dma_start(bt[q][:], block_of("bc", j)[:, 0]).then_inc(in_a[q], 16)

            def load_c(j, q):
                sp.dma_start(ct[q][:], block_of("bc", j)[:, 1]).then_inc(in_c[q], 16)

            def load_x(j, q):
                sp.dma_start(xc[q][:], block_of("xc", j)).then_inc(in_x[q], 16)
                sp.dma_start(zs[q][:], block_of("zs", j)).then_inc(in_x[q], 16)

            def turn(j, u, m, first, last):
                ahead = not (isinstance(j, int) and j + 2 >= NJ)
                if ahead:
                    sp.wait_ge(d_mm, (j + 1) * IT)
                    sp.wait_ge(inp_done, (j + 1) * 2 * IT)
                    load_a(j + 2, u)
                if not first:
                    sp.wait_ge(gate_done, j + GATE_AHEAD)
                    sp.dma_start(block_of("yg", j - 1), yg[1 - u][:]).then_inc(stored[1 - u], 16)
                if not last:
                    load_x(j + 1, 1 - u)
                if ahead:
                    sp.wait_ge(c_done, (j + 1) * NC_)
                    load_c(j + 2, u)

            for name, tile in (("sel", sel), ("ysel", ysel), ("pool16", pool16), ("par", par)):
                sp.dma_start(tile[:], w[name]).then_inc(consts, 16)
            for q in range(2):
                load_a(q, q)
                load_c(q, q)
            load_x(0, 0)
            turns(sp, turn)
            sp.wait_ge(gate_done, NJ + GATE_AHEAD)
            sp.dma_start(block_of("yg", NJ - 1), yg[1][:]).then_inc(stored[1], 16)
            for q in range(2):
                sp.wait_ge(stored[q], 16 * NJ // 2)

        @block.tensor
        def _(pe):
            def spread(out, src, item, jr_e):
                jr, e = jr_e
                d, quad, i = tile_place(item * TI + 2 * jr + e)
                return pe.matmul(out[:, jr, e, :], sel[:, i, :], src[:, d, quad].rearrange("p b t -> p (b t)"),
                                 start=True, stop=True)

            def decays(jj, q, item):
                pe.wait_ge(exp_done, (jj * IT + item) * TI + TI)
                for e in range(2):
                    for jr in range(2):
                        mm = spread(ps_d[item % 2], dl[q], item, (jr, e))
                mm.then_inc(d_mm, 1)

            def inputs(jj, q, item):
                pe.wait_ge(inp_done, (jj * IT + item) * 2)
                for e in range(2):
                    for jr in range(2):
                        mm = spread(ps_u, ux[q], item, (jr, e))
                mm.then_inc(u_mm, 1)

            def sums(j, q, part):
                for quad in range(4):
                    d, i = part // 4, part % 4
                    st = next(s for s in range(TL) if tile_place(s) == (d, quad, i))
                    h = hb[q][:, :, st * B:(st + 1) * B, 1:].rearrange("p c b t -> p b c t")
                    mm = pe.matmul(ps_y[32 * quad:32 * quad + 32, d, :].rearrange("p (b c t) -> p b c t", b=B, t=CH),
                                   ysel[:, i, :], h, start=i == 0, stop=i == 3)
                mm.then_inc(y_mm, 1)

            def turn(j, u, m, first, last):
                for c in range(NC_):
                    pe.wait_ge(sq_done, j * NC_ + c + 1)
                    pe.matmul(ps_n[:, 0:ST], pool16[:], sq[:], start=True, stop=True).then_inc(n_mm, 1)
                    if not last:
                        if c == 0:
                            pe.wait_ge(in_a[1 - u], IN_A * (m + 1 + u))
                        decays(j + 1, 1 - u, c)
                    if SUMS_AT[c] and not first:
                        if c == 0:
                            pe.wait_ge(c_done, j * NC_)
                            pe.wait_ge(y_done, (j - 1) * DH)
                        for part in SUMS_AT[c]:
                            sums(j - 1, 1 - u, part)
                    if not last:
                        for item in SPREAD_AT[c]:
                            inputs(j + 1, 1 - u, item)

            pe.wait_ge(consts, 64)
            pe.wait_ge(in_a[0], IN_A)
            for item in range(IT):
                decays(0, 0, item)
                inputs(0, 0, item)
            turns(pe, turn)
            pe.wait_ge(c_done, NJ * NC_)
            pe.wait_ge(y_done, (NJ - 1) * DH)
            for part in range(8):
                sums(NJ - 1, 1, part)

        @block.scalar
        def _(act):
            def decay_exps(jj, q, item, tiles):
                if 0 in tiles:
                    act.wait_ge(d_mm, jj * IT + item + 1)
                for n in tiles:
                    st = item * TI + n
                    out = dA[q][:, :, st * B:(st + 1) * B, 1:].rearrange("p c b t -> p b c t")
                    act.activation(out, ps_d[item % 2][:, n // 2, n % 2, :].rearrange("p (b c t) -> p b c t", b=B, t=CH),
                                   ACT.Exp, scale=par[:, jj, st:st + 1] if isinstance(jj, int)
                                   else par[:, bass.ds(jj, 1), st:st + 1].rearrange("p a b -> p (a b)"))\
                       .then_inc(exp_done, 1)

            def turn(j, u, m, first, last):
                for c in range(NC_):
                    s = j * NC_ + c
                    act.wait_ge(scan_done, s + 1)
                    act.activation(sq[:], hb[u][:, c, :, CH], ACT.Square).then_inc(sq_done, 1)
                    act.wait_ge(mx_done, s + 1)
                    act.activation(lg[:], mx[:], ACT.Ln, scale=1.0 / (H_MAX * H_MAX)).then_inc(lg_done, 1)
                    act.wait_ge(lg_done, s + 1)
                    act.wait_ge(last_done, s)
                    act.activation(scl[c % 2][:], lg[:], ACT.Exp, scale=-0.5).then_inc(scl_done, 1)
                    if not last:
                        decay_exps(j + 1, 1 - u, c, range(TI))

            act.preload_act_table_set(LN_EXP)
            act.sem_inc(exp_done, EXP_AHEAD)
            act.wait_ge(consts, 64)
            act.activation(par[:, :, 0:TL], par[:, :, 0:TL], ACT.Exp).then_inc(decay, 1)
            act.wait_ge(decay, 2)
            act.wait_ge(cleared, 2)
            for item in range(IT):
                decay_exps(0, 0, item, range(TI))
            turns(act, turn)

        @block.vector
        def _(dve):
            def clip(jj, q, item):
                dve.wait_ge(exp_done, (jj * IT + item) * TI + TI + EXP_AHEAD)
                own = dA[q][:, :, item * TI * B:(item + 1) * TI * B, 1:]
                dve.tensor_scalar(own, own, DA_MIN, None, ALU.max).then_inc(clip_done, 1)

            def inputs(jj, q, item):
                dve.wait_ge(u_mm, jj * IT + item + 1)
                for b in range(B):
                    streams = slice(item * TI * B + b, (item + 1) * TI * B, B)
                    out = hb[q][:, :, streams, 1:].rearrange("p c s t -> p s c t")
                    rep = bt[q][:, b, :].rearrange("p (c t) -> p c t", t=CH).unsqueeze(1).broadcast_to([P, TI, NC_, CH])
                    dve.tensor_tensor(out, ps_u[:, :, :, b * TB:(b + 1) * TB].rearrange("p k e (c t) -> p (k e) c t", t=CH),
                                      rep, ALU.mult).then_inc(inp_done, 1)

            def outputs(j, q, count):
                dve.wait_ge(y_mm, (j + 1) * 8)
                dve.wait_ge(in_x[q], count)
                dve.wait_ge(gate_done, j + 1)
                for d in range(DH):
                    dve.scalar_tensor_tensor(
                        yv[q][:, d].rearrange("p b t -> p (b t)"), xc[q][:, d].rearrange("p b t -> p (b t)"),
                        par[:, j, TL + d:TL + d + 1] if isinstance(j, int)
                        else par[:, bass.ds(j, 1), TL + d:TL + d + 1].rearrange("p a b -> p (a b)"),
                        ps_y[:, d, :], ALU.mult, ALU.add).then_inc(y_done, 1)

            def turn(j, u, m, first, last):
                for c in range(NC_):
                    s = j * NC_ + c
                    if c == 0:
                        dve.wait_ge(clip_done, (j + 1) * IT)
                        dve.wait_ge(inp_done, (j + 1) * 2 * IT)
                    dve.wait_ge(head_done, s + 1)
                    flat = lambda t: t[:, c].rearrange("p s w -> p (s w)")
                    dve.tensor_tensor_scan(flat(hb[u]), flat(dA[u]), flat(hb[u]), 0.0, ALU.mult, ALU.add)\
                       .then_inc(scan_done, 1)
                    if c >= 1 and not last:
                        clip(j + 1, 1 - u, c - 1)
                    dve.wait_ge(n_mm, s + 1)
                    dve.tensor_scalar(mx[:], ps_n[:, 0:ST], H_MAX * H_MAX, None, ALU.max).then_inc(mx_done, 1)
                    if c == 1 and not first:
                        dve.wait_ge(y_mm, (j - 1) * 8 + 4)
                    if c == 3 and not first:
                        outputs(j - 1, 1 - u, 32 * (m + u))
                    if not last:
                        for item in INP_AT[c][:1]:
                            inputs(j + 1, 1 - u, item)
                    dve.wait_ge(scl_done, s + 1)
                    if c < NC_ - 1:
                        dve.tensor_tensor(hb[u][:, c + 1, :, 0], hb[u][:, c, :, CH], scl[c % 2][:], ALU.mult)\
                           .then_inc(head_done, 1)
                    elif not last:
                        keep = par[:, j + 1, TL + DH:] if isinstance(j, int) else \
                            par[:, bass.ds(j + 1, 1), TL + DH:].rearrange("p a b -> p (a b)")
                        dve.scalar_tensor_tensor(hb[1 - u][:, 0, :, 0], hb[u][:, c, :, CH], keep, scl[c % 2][:],
                                                 ALU.mult, ALU.mult).then_inc(head_done, 1)
                    if not last:
                        for item in INP_AT[c][1:]:
                            inputs(j + 1, 1 - u, item)
                        if c == NC_ - 1:
                            clip(j + 1, 1 - u, c)

            for q in range(2):
                dve.memset(dA[q][:, :, :, 0], 0.0).then_inc(cleared, 1)
            dve.memset(hb[0][:, 0, :, 0], 0.0).then_inc(head_done, 1)
            dve.wait_ge(decay, 1)
            dve.tensor_scalar(par[:, :, 0:TL], par[:, :, 0:TL], -1.0, None, ALU.mult).then_inc(decay, 1)
            for item in range(IT):
                clip(0, 0, item)
                inputs(0, 0, item)
            turns(dve, turn)
            outputs(NJ - 1, 1, 32 * (NJ // 2))

        @block.gpsimd
        def _(pool):
            def gate(j, q, count):
                pool.wait_ge(y_done, (j + 1) * DH)
                pool.wait_ge(stored[q], count)
                pool.tensor_tensor(yg[q][:], yv[q][:], zs[q][:], ALU.mult).then_inc(gate_done, 1)

            def turn(j, u, m, first, last):
                for c in range(NC_):
                    s = j * NC_ + c
                    pool.wait_ge(scl_done, s + 1)
                    if not (last and c == NC_ - 1):
                        pool.wait_ge(head_done, s + 2)
                    pool.tensor_tensor(hb[u][:, c, :, CH], hb[u][:, c, :, CH], scl[c % 2][:], ALU.mult)\
                        .then_inc(last_done, 1)
                    pool.wait_ge(last_done, s + 1 + LAST_AHEAD)
                    if c == 0:
                        pool.wait_ge(in_c[u], 16 * (m + 1))
                    h = hb[u][:, c, :, 1:].rearrange("p (s b) t -> p s b t", b=B)
                    rep = ct[u][:, :, c * CH:(c + 1) * CH].unsqueeze(1).broadcast_to([P, TL, B, CH])
                    pool.tensor_tensor(h, h, rep, ALU.mult).then_inc(c_done, 1)
                    if c == 5 and not first:
                        gate(j - 1, 1 - u, 16 * (m + u - 1))

            pool.sem_inc(last_done, LAST_AHEAD)
            pool.sem_inc(gate_done, GATE_AHEAD)
            turns(pool, turn)
            gate(NJ - 1, 1, 16 * (NJ // 2 - 1))


def back_to_tokens(nc, alloc, w, scr, x, mean, rstd, out, mean3, scale3, rstd3):
    sb, ps, sem = alloc
    wo, wb = sb("bt_w", [P, MI, D]), sb("bt_b", [P, D])
    ga, be = sb("bt_gamma", [P, D]), sb("bt_beta", [P, D])
    xb = sb("bt_x_beta", [P, NT, D])
    yt = [sb(f"bt_y{b}", [P, MI, BLK]) for b in range(B)]
    xt = [sb(f"bt_x{b}", [P, SUB, D]) for b in range(B)]
    r1, r2 = sb("bt_r1", [P, 2, D]), sb("bt_r2", [P, 2, D])
    raw, mv = sb("bt_raw", [P, NT, 6]), sb("bt_mv", [P, NT, 2])
    tmp = sb("bt_tmp", [P, 4, NT])
    po = [ps(f"bt_ps{j}", [P, BLK])[:, 0:D] for j in range(2)]
    weights, mm, res, own, summed, raw_done, xb_done = (
        sem(f"bt_{n}") for n in ("weights", "mm", "res", "own", "summed", "raw", "xb"))
    y_in = [sem(f"bt_y_in{b}") for b in range(B)]
    x_in = [sem(f"bt_x_in{b}") for b in range(B)]
    mv_done, roots, root_in, step, normed, raw2, mv2 = (
        sem(f"bt_{n}") for n in ("mv", "roots", "root_in", "step", "normed", "raw2", "mv2"))
    M = B * SUB
    with nc.Block() as block:

        @block.sync
        def _(sp):
            for tile, name in ((wo, "out_w"), (wb, "out_b"), (ga, "gamma"), (be, "beta")):
                sp.dma_start(tile[:], w[name]).then_inc(weights, 16)
            with sp.Fori(0, NB) as i:
                for b in range(B):
                    sp.wait_ge(mm, i * M)
                    for h in range(HP):
                        sp.dma_start(yt[b][:, h * DH:(h + 1) * DH, :].rearrange("p d (n t) -> p d n t", t=TB),
                                     scr["yg"][h, bass.ds(i * SUB, SUB), :, :, b, :].rearrange("n p d t -> p d n t"))\
                          .then_inc(y_in[b], 16)
                    sp.wait_ge(res, i * M)
                    sp.dma_start(xt[b][:], x[b, bass.ds(i * BLK, BLK), :].rearrange("(a p) d -> p a d", p=P))\
                      .then_inc(x_in[b], 16)

        @block.tensor
        def _(pe):
            pe.wait_ge(weights, 64)
            with pe.Fori(0, NB) as i:
                for b in range(B):
                    pe.wait_ge(y_in[b], 32 * (i + 1))
                    for a in range(SUB):
                        pe.wait_ge(own, i * M + SUB * b + a + 1)
                        for k in range(MI):
                            last = pe.matmul(po[a % 2], yt[b][:, k, a * P:(a + 1) * P], wo[:, k, :],
                                             start=k == 0, stop=k == MI - 1)
                        last.then_inc(mm, 1)

        @block.gpsimd
        def _(pool):
            pool.wait_ge(weights, 64)
            with pool.Fori(0, NB) as i:
                for b in range(B):
                    pool.wait_ge(x_in[b], 16 * (i + 1))
                    pool.tensor_tensor(xb[:, bass.ds(b * (NT // B) + i * SUB, SUB), :], xt[b][:],
                                       be[:].unsqueeze(1).broadcast_to([P, SUB, D]), ALU.add).then_inc(xb_done, 1)

        @block.vector
        def _(dve):
            dve.sem_inc(own, 2)
            dve.wait_ge(weights, 64)
            with dve.Fori(0, NB) as i:
                for b in range(B):
                    dve.wait_ge(x_in[b], 16 * (i + 1))
                    for a in range(SUB):
                        n = i * M + SUB * b + a
                        t = b * (NT // B) + i * SUB + a
                        at = lambda v: v[:, bass.ds(t, 1)]
                        dve.wait_ge(summed, n)
                        if a == SUB - 1:
                            dve.wait_ge(xb_done, i * B + b + 1)
                        dve.tensor_scalar(r1[:, a % 2, :], xt[b][:, a, :], at(mean), at(rstd),
                                          ALU.subtract, ALU.mult).then_inc(res, 1)
                        dve.wait_ge(res, n + 1)
                        dve.wait_ge(mm, n + 1)
                        dve.tensor_tensor(r2[:, a % 2, :], po[a % 2], r1[:, a % 2, :], ALU.add).then_inc(own, 1)
                        dve.wait_ge(own, n + 3)
                        dve.tensor_tensor(out[:, bass.ds(t, 1), :].rearrange("p a d -> p (a d)"), r2[:, a % 2, :], wb[:],
                                          ALU.add).then_inc(summed, 1)
            dve.wait_ge(summed, NT)
            for t in range(NT):
                dve.bn_stats(raw[:, t, :], out[:, t, :]).then_inc(raw_done, 1)
            for t in range(NT):
                dve.wait_ge(raw_done, t + 1)
                dve.bn_aggr(mv[:, t, :], raw[:, t, :]).then_inc(mv_done, 1)
            dve.wait_ge(mv_done, NT)
            dve.wait_ge(roots, 1)
            dve.tensor_scalar(tmp[:, 1, :], tmp[:, 0, :], STD_EPS, None, ALU.add).then_inc(step, 1)
            dve.wait_ge(step, 1)
            dve.reciprocal(tmp[:, 2, :], tmp[:, 1, :]).then_inc(step, 1)
            dve.wait_ge(step, 2)
            dve.wait_ge(xb_done, NB * B)
            for t in range(NT):
                dve.tensor_scalar(r1[:, t % 2, :], out[:, t, :], mv[:, t, 0:1], tmp[:, 2, t:t + 1],
                                  ALU.subtract, ALU.mult).then_inc(normed, 1)
                dve.wait_ge(normed, 3 * t + 1)
                dve.tensor_tensor(r2[:, t % 2, :], r1[:, t % 2, :], ga[:], ALU.mult).then_inc(normed, 1)
                dve.wait_ge(normed, 3 * t + 2)
                dve.tensor_tensor(out[:, t, :], r2[:, t % 2, :], xb[:, t, :], ALU.add).then_inc(normed, 1)
                dve.wait_ge(normed, 3 * t + 3)
                dve.bn_stats(raw[:, t, :], out[:, t, :]).then_inc(raw2, 1)
            dve.wait_ge(raw2, NT)
            for t in range(NT):
                dve.bn_aggr(mv[:, t, :], raw[:, t, :]).then_inc(mv2, 1)
            dve.wait_ge(mv2, NT)
            dve.tensor_copy(mean3[:], mv[:, :, 0]).then_inc(step, 1)
            dve.tensor_scalar(tmp[:, 0, :], mv[:, :, 1], LN_EPS, None, ALU.add).then_inc(root_in, 1)
            dve.wait_ge(roots, 2)
            dve.reciprocal(rstd3[:], tmp[:, 1, :]).then_inc(step, 1)
            dve.wait_ge(root_in, 1)
            dve.reciprocal(tmp[:, 2, :], tmp[:, 0, :]).then_inc(step, 1)
            dve.wait_ge(step, 5)
            dve.tensor_tensor(tmp[:, 3, :], tmp[:, 2, :], mv[:, :, 1], ALU.mult).then_inc(step, 1)
            dve.wait_ge(step, 6)
            dve.tensor_scalar(tmp[:, 2, :], tmp[:, 3, :], STD_EPS, None, ALU.add).then_inc(root_in, 1)
            dve.wait_ge(roots, 3)
            dve.reciprocal(tmp[:, 1, :], tmp[:, 0, :]).then_inc(step, 1)
            dve.wait_ge(step, 7)
            dve.tensor_tensor(scale3[:], tmp[:, 1, :], rstd3[:], ALU.mult).then_inc(step, 1)

        @block.scalar
        def _(act):
            act.wait_ge(mv_done, NT)
            act.activation(tmp[:, 0, :], mv[:, :, 1], ACT.Sqrt, scale=BESSEL).then_inc(roots, 1)
            act.wait_ge(root_in, 1)
            act.activation(tmp[:, 1, :], tmp[:, 0, :], ACT.Sqrt).then_inc(roots, 1)
            act.wait_ge(root_in, 2)
            act.activation(tmp[:, 0, :], tmp[:, 2, :], ACT.Sqrt).then_inc(roots, 1)


def latents(nc, alloc, w, h_t, scr):
    sb, ps, sem = alloc
    wq, wk = sb("la_wq", [P, KD, 2 * D]), sb("la_wk", [P, 2 * D])
    wl, wv = sb("la_wl", [P, KD, P]), sb("la_wv", [P, D])
    lg, lb = sb("la_g", [P, 1]), sb("la_b", [P, 1])
    cos, sin = sb("la_cos", [P, L]), sb("la_sin", [P, L])
    avg = sb("la_avg", [P, P])
    eps = sb("la_eps", [P, 1])
    qa, qb = sb("la_qa", [P, 2, BLK]), sb("la_qb", [P, 2, BLK])
    qf, qr = sb("la_qf", [P, 2, BLK]), sb("la_qr", [P, 2, BLK])
    parts = sb("la_parts", [P, 2, 3, BLK], BF16)
    lat, cen, sq, sd, rec = (sb(f"la_{n}", [P, BLK]) for n in ("lat", "cen", "sq", "sd", "rec"))
    ln = sb("la_ln", [P, BLK])
    vt = sb("la_vt", [P, SUB, NH, VW])
    pq = [ps(f"la_pq{j}", [P, BLK]) for j in range(4)]
    pl, pm, pv = ps("la_pl", [P, BLK]), ps("la_pm", [P, BLK]), ps("la_pv", [P, BLK])
    po = ps("la_po", [P, BLK])[:, 0:D]
    (weights, ready, l_mm, m_mm, v_mm, q_mm, o_mm, lat_done, cen_done, sq_done, sd_done, rec_done, nrm_done,
     ln_done, turn1, turn2, q_done, cut, lo_done, v_out) = (
        sem(f"la_{n}") for n in ("weights ready l_mm m_mm v_mm q_mm o_mm lat cen sq sd rec nrm ln turn1 turn2 "
                                 "q cut lo v_out").split())
    q_st = [sem(f"la_q_st{j}") for j in range(2)]
    v_st = sem("la_v_st")
    loads = [(wq, "wq"), (wk, "wk"), (wl, "wl"), (wv, "wv"), (lg, "ln_g"), (lb, "ln_b"), (cos, "cos"), (sin, "sin"),
             (avg, "avg")]
    R = 2 * KD
    with nc.Block() as block:

        @block.gpsimd
        def _(pool):
            pool.memset(vt[:], 0.0).then_inc(ready, 1)
            pool.memset(eps[:], LN_EPS).then_inc(ready, 1)
            pool.wait_ge(ready, 2)
            pool.memset(vt[:, :, :, HD], 1.0).then_inc(ready, 1)

        @block.sync
        def _(sp):
            for tile, name in loads:
                sp.dma_start(tile[:], w[name]).then_inc(weights, 16)
            for b in range(B):
                with sp.Fori(0, NB) as i:
                    n = b * NB + i
                    col = bass.ds(b * L + i * BLK, BLK)
                    for r in range(R):
                        dst = scr["qs" if r < KD else "ks"]
                        sp.wait_ge(lo_done, n * R + r + 1)
                        sp.dma_start(dst[:, r % KD * P:(r % KD + 1) * P, col].rearrange("s p t -> p s t"),
                                     parts[:, r % 2]).then_inc(q_st[r % 2], 16)
                    sp.wait_ge(v_out, (n + 1) * SUB)
                    sp.dma_start(scr["v"][bass.ds(b * L + i * BLK, BLK)].rearrange("(a p) h c -> p a h c", p=P),
                                 vt[:]).then_inc(v_st, 16)
            for r in range(2):
                sp.wait_ge(q_st[r], B * NB * R // 2 * 16)
            sp.wait_ge(v_st, B * NB * 16)

        @block.tensor
        def _(pe):
            pe.wait_ge(weights, 16 * len(loads))
            for b in range(B):
                with pe.Fori(0, NB) as i:
                    n = b * NB + i
                    rhs = [h_t[:, k, bass.ds(b * L + i * BLK, BLK)] for k in range(KD)]
                    pe.wait_ge(lat_done, n)
                    for k in range(KD):
                        last = pe.matmul(pl[:], wl[:, k, :], rhs[k], start=k == 0, stop=k == KD - 1)
                    last.then_inc(l_mm, 1)
                    for m in range(KD):
                        pe.wait_ge(turn2, n * R + m)
                        for v in range(2):
                            for k in range(KD):
                                last = pe.matmul(pq[2 * (m % 2) + v][:], wq[:, k, v * D + m * P:v * D + (m + 1) * P],
                                                 rhs[k], start=k == 0, stop=k == KD - 1)
                        last.then_inc(q_mm, 1)
                    pe.wait_ge(lat_done, n + 1)
                    pe.matmul(pm[:], avg[:], lat[:], start=True, stop=True).then_inc(m_mm, 1)
                    pe.wait_ge(sq_done, n + 1)
                    pe.matmul(pv[:], avg[:], sq[:], start=True, stop=True).then_inc(v_mm, 1)
                    pe.wait_ge(ln_done, n + 1)
                    for m in range(KD):
                        pe.wait_ge(turn2, n * R + KD + m)
                        for v in range(2):
                            last = pe.matmul(pq[2 * (m % 2) + v][:], wk[:, v * D + m * P:v * D + (m + 1) * P], ln[:],
                                             start=True, stop=True)
                        last.then_inc(q_mm, 1)
                    for a in range(SUB):
                        pe.wait_ge(v_out, n * SUB + a)
                        pe.matmul(po, ln[:, a * P:(a + 1) * P], wv[:], start=True, stop=True)\
                          .then_inc(o_mm, 1)

        @block.scalar
        def _(act):
            act.preload_act_table_set(SQRT_SET)
            act.wait_ge(ready, 3)
            for b in range(B):
                with act.Fori(0, NB) as i:
                    n = b * NB + i
                    act.wait_ge(l_mm, n + 1)
                    act.wait_ge(cen_done, n)
                    act.activation(lat[:], pl[:], ACT.Copy).then_inc(lat_done, 1)
                    act.wait_ge(cen_done, n + 1)
                    act.activation(sq[:], cen[:], ACT.Square).then_inc(sq_done, 1)
                    act.wait_ge(v_mm, n + 1)
                    act.activation(sd[:], pv[:], ACT.Sqrt, bias=eps[:]).then_inc(sd_done, 1)
                    act.wait_ge(v_st, n * 16)
                    for a in range(SUB):
                        act.wait_ge(o_mm, n * SUB + a + 1)
                        act.activation(vt[:, a, :, 0:HD], po.rearrange("p (h c) -> p h c", c=HD), ACT.Copy)\
                           .then_inc(v_out, 1)

        @block.vector
        def _(dve):
            dve.sem_inc(turn2, 1)
            dve.wait_ge(weights, 16 * len(loads))
            for b in range(B):
                with dve.Fori(0, NB) as i:
                    n = b * NB + i

                    def rotate(r):
                        u = r % 2
                        k = n * R + r
                        col = bass.ds(i * BLK, BLK)
                        dve.wait_ge(q_mm, k + 1)
                        dve.wait_ge(q_done, k)
                        dve.tensor_tensor(qa[:, u], pq[2 * u][:], cos[:, col], ALU.mult).then_inc(turn1, 1)
                        dve.tensor_tensor(qb[:, u], pq[2 * u + 1][:], sin[:, col], ALU.mult).then_inc(turn2, 1)
                        dve.wait_ge(turn1, k + 1)
                        dve.wait_ge(turn2, k + 2)
                        dve.tensor_tensor(qf[:, u], qa[:, u], qb[:, u], ALU.add).then_inc(q_done, 1)
                        dve.wait_ge(q_done, k + 1)
                        dve.wait_ge(q_st[u], (n * (R // 2) + r // 2) * 16)
                        dve.tensor_copy(parts[:, u, 0], qf[:, u]).then_inc(cut, 1)
                        dve.wait_ge(cut, 3 * k + 1)
                        dve.tensor_tensor(qr[:, u], qf[:, u], parts[:, u, 0], ALU.subtract).then_inc(cut, 1)
                        dve.wait_ge(cut, 3 * k + 2)
                        dve.tensor_copy(parts[:, u, 1], qr[:, u]).then_inc(cut, 1)
                        dve.wait_ge(cut, 3 * k + 3)
                        dve.tensor_tensor(parts[:, u, 2], qr[:, u], parts[:, u, 1], ALU.subtract).then_inc(lo_done, 1)
                        dve.wait_ge(lo_done, k + 1)

                    dve.wait_ge(m_mm, n + 1)
                    dve.wait_ge(nrm_done, n)
                    dve.tensor_tensor(cen[:], lat[:], pm[:], ALU.subtract).then_inc(cen_done, 1)
                    for m in range(KD):
                        rotate(m)
                    dve.wait_ge(sd_done, n + 1)
                    dve.reciprocal(rec[:], sd[:]).then_inc(rec_done, 1)
                    dve.wait_ge(rec_done, n + 1)
                    dve.tensor_tensor(sq[:], cen[:], rec[:], ALU.mult).then_inc(nrm_done, 1)
                    dve.wait_ge(nrm_done, n + 1)
                    dve.wait_ge(o_mm, n * SUB)
                    dve.tensor_scalar(ln[:], sq[:], lg[:], lb[:], ALU.mult, ALU.add).then_inc(ln_done, 1)
                    for m in range(KD):
                        rotate(KD + m)


def attention(nc, alloc, w, scr):
    sb, ps, sem = alloc
    HQ, QB = 4, L // BLK
    G = B * (NH // HQ)
    ks = [[sb(f"at_k{p}{j}", [P, L], BF16) for j in range(HQ)] for p in range(2)]
    qs = [[sb(f"at_q{p}{j}", [P, L], BF16) for j in range(HQ)] for p in range(2)]
    vs = [sb(f"at_v{p}", [P, L // P, HQ, VW]) for p in range(2)]
    idb, dsel = sb("at_idb", [P, P], BF16), sb("at_dsel", [P, P])
    later = sb("at_later", [P, 2, P], BF16)
    pmx = sb("at_pmx", [P, 2, SUB, HQ, QB])
    neg, res = sb("at_neg", [P, 2, SUB, HQ]), sb("at_res", [P, 2, SUB, HQ])
    msp = sb("at_msp", [P, 2, SUB, HQ, 32], BF16)
    pt = [sb(f"at_p{u}", [P, HQ, BLK]) for u in range(2)]
    ob, rec = sb("at_ob", [P, BLK]), sb("at_rec", [P, BLK])
    on = [sb(f"at_on{u}", [P, BLK]) for u in range(2)]
    p1 = [ps(f"at_p1{j}", [P, BLK]) for j in range(2)]
    p2 = [ps(f"at_p2{j}", [P, 2, BLK]) for j in range(2)]
    po = ps("at_po", [P, BLK])
    pr = ps("at_pr", [P, BLK])
    (consts, ready, s1_mm, mx_done, cut, s_lo, t_mm, t_out, s2_mm, e_done, pv_mm, ob_done, b_mm, rec_done, on_done) = (
        sem(f"at_{n}") for n in "consts ready s1 mx cut s_lo t_mm t_out s2 e pv ob b_mm rec on".split())
    q_in = [sem(f"at_q_in{p}") for p in range(2)]
    on_st = [sem(f"at_on_st{u}") for u in range(2)]
    units = [(qb, kt) for qb in range(QB) for kt in range(SUB * (qb + 1))]
    NU = len(units)
    last_of = {qb: SUB * (qb + 1) * (qb + 2) // 2 - 1 for qb in range(QB)}
    LAG = 10
    LEAD = NU - LAG
    LOAD = (HQ * 12 + 1) * 16
    E_AHEAD, S1_AHEAD, PV_AHEAD, FREE = 2, 2, NU + 1, 1
    maxima_at = {(last_of[qb] + 2 + LAG) % NU: (qb, (last_of[qb] + 2 + LAG) // NU) for qb in range(QB)}
    maxima_at = {n: (qb, 1 - late) for n, (qb, late) in maxima_at.items()}
    sums_at = {last_of[qb] + 2: qb for qb in range(QB - 1)}

    def groups(body):
        def of(eng):
            with eng.Fori(0, G // 2 - 1) as m:
                for p in range(2):
                    body(2 * m + p, p, m, True)
            for p in range(2):
                body(G - 2 + p, p, G // 2 - 1, p == 0)
        return of

    with nc.Block() as block:

        @block.sync
        def _(sp):
            for tile, name in ((idb, "idb"), (later, "later"), (dsel, "dsel")):
                sp.dma_start(tile[:], w[name]).then_inc(consts, 16)
            sp.wait_ge(ready, 4 * HQ + 1)
            for b in range(B):
                cols = slice(b * L, (b + 1) * L)
                with sp.Fori(0, NH // HQ // 2) as m:
                    for p in range(2):
                        hq = 2 * m + p
                        g = b * (NH // HQ) + hq
                        sp.wait_ge(pv_mm, g * NU - NU + PV_AHEAD)
                        for j in range(HQ):
                            rows = bass.ds(hq * (HQ * HD) + j * HD, HD)
                            for r, s in enumerate((0, 0, 0, 1, 1, 2)):
                                sp.dma_start(qs[p][j][r * HD:(r + 1) * HD, :], scr["qs"][s, rows, cols])\
                                  .then_inc(q_in[p], 16)
                            for r, s in enumerate((0, 1, 2, 0, 1, 0)):
                                sp.dma_start(ks[p][j][r * HD:(r + 1) * HD, :], scr["ks"][s, rows, cols])\
                                  .then_inc(q_in[p], 16)
                        sp.dma_start(vs[p][:], scr["v"][b * L:(b + 1) * L, bass.ds(hq * HQ, HQ), :]
                                     .rearrange("(t p) h c -> p t h c", p=P)).then_inc(q_in[p], 16)

        @block.gpsimd
        def _(pool):
            for p in range(2):
                for j in range(HQ):
                    pool.memset(ks[p][j][P - 32:P, :], 1.0).then_inc(ready, 1)
                    pool.memset(qs[p][j][P - 32:P, :], 0.0).then_inc(ready, 1)
            for b in range(B):
                with pool.Fori(0, NH // HQ) as hq:
                    for qb in range(QB):
                        pool.wait_ge(on_done, (b * (NH // HQ) + hq) * QB + qb + 1 + FREE)
                        for j in range(HQ):
                            rows = bass.ds(hq * (HQ * HD) + j * HD, HD)
                            pool.dma_start(scr["at"][rows, b * L + qb * BLK:b * L + (qb + 1) * BLK],
                                           on[qb % 2][32 * j:32 * j + HD, :]).then_inc(on_st[qb % 2], 16)
            for u in range(2):
                pool.wait_ge(on_st[u], G * QB // 2 * HQ * 16)

        @block.tensor
        def _(pe):
            def scores(g, p, x, heads):
                qb, kt = units[x]
                a, kc = kt % SUB, kt // SUB
                q0, width = (SUB * qb + a) * P, BLK if kc < qb else (a + 1) * P
                for j in heads:
                    pe.wait_ge(mx_done, (g * NU + x) * HQ + j - 1 + S1_AHEAD)
                    last = pe.matmul(p1[j % 2][:, 0:width], qs[p][j][0:6 * HD, q0:q0 + P],
                                     ks[p][j][0:6 * HD, kc * BLK:kc * BLK + width], start=True, stop=kc < qb)
                    if kc == qb:
                        last = pe.matmul(p1[j % 2][:, a * P:width], idb[:], later[:, 0, :], start=False, stop=True)
                    last.then_inc(s1_mm, 1)

            def maxima(g, qb, spread):
                pe.wait_ge(s_lo, g * QB + qb + 1)
                if spread is not None:
                    pe.wait_ge(rec_done, spread)
                for a in range(SUB):
                    last = pe.matmul(pr[:, a * P:(a + 1) * P], msp[:, qb % 2, a].rearrange("p j c -> p (j c)"), idb[:],
                                     start=True, stop=True)
                last.then_inc(t_mm, 1)

            def values(g, p, n):
                qb, kt = units[n]
                dk = max(kt - SUB * qb, 0)
                pe.wait_ge(e_done, (g * NU + n) * 2 + 2 + E_AHEAD)
                if kt == 0:
                    pe.wait_ge(ob_done, g * QB + qb + FREE)
                for j in range(HQ):
                    last = pe.matmul(po[32 * j:32 * j + 32, dk * P:], vs[p][:, kt, j, :], pt[n % 2][:, j, dk * P:],
                                     start=kt == 0, stop=n == last_of[qb])
                last.then_inc(pv_mm, 1)

            def sums(g, qb, maxima_out):
                pe.wait_ge(ob_done, g * QB + qb + 1 + FREE)
                pe.wait_ge(t_out, maxima_out * HQ)
                pe.matmul(pr[:], dsel[:], ob[:], start=True, stop=True).then_inc(b_mm, 1)

            pe.sem_inc(pv_mm, PV_AHEAD)
            pe.wait_ge(consts, 48)
            pe.wait_ge(ready, 4 * HQ + 1)
            pe.wait_ge(q_in[0], LOAD)
            for x in range(LEAD):
                scores(0, 0, x, range(HQ))
                for qb in range(QB):
                    if x == last_of[qb] + 2:
                        if qb:
                            pe.wait_ge(t_out, qb * HQ)
                        maxima(0, qb, None)

            def body(g, p, m, more):
                done = 0
                for n, (qb, kt) in enumerate(units):
                    ahead = n < LAG or more
                    first = (g, p, n + LEAD) if n < LAG else (g + 1, 1 - p, n - LAG)
                    if n == LAG and more:
                        pe.wait_ge(q_in[1 - p], (m + p + 1) * LOAD)
                    if kt == 0:
                        pe.wait_ge(t_out, (g * QB + qb + 1) * HQ)
                    dk = max(kt - SUB * qb, 0)
                    for s in range(2):
                        if ahead:
                            scores(*first, (s,))
                        pe.wait_ge(e_done, (g * NU + n) * 2 + s - 1 + E_AHEAD)
                        for j in range(2 * s, 2 * s + 2):
                            last = pe.matmul(p2[s][:, j % 2, dk * P:], ks[p][j][:, kt * P:(kt + 1) * P],
                                             qs[p][j][:, qb * BLK + dk * P:(qb + 1) * BLK], start=True,
                                             stop=kt < SUB * qb)
                            if kt >= SUB * qb:
                                last = pe.matmul(p2[s][:, j % 2, dk * P:(dk + 1) * P], idb[:], later[:, 1, :],
                                                 start=False, stop=True)
                        last.then_inc(s2_mm, 1)
                    if ahead:
                        scores(*first, (2,))
                    if n >= 1:
                        values(g, p, n - 1)
                    if n in maxima_at:
                        mqb, mg = maxima_at[n]
                        if more or mg == 0:
                            maxima(g + mg, mqb, g * QB + done)
                    if n in sums_at:
                        out = [QB * mg + mqb + 1 for k, (mqb, mg) in maxima_at.items() if k < n and (more or mg == 0)]
                        sums(g, sums_at[n], g * QB + max(out + [QB - 1]))
                        done += 1
                    if ahead:
                        scores(*first, (3,))
                values(g, p, NU - 1)
                sums(g, QB - 1, g * QB + (2 * QB - 1 if more else QB))
            groups(body)(pe)

        @block.scalar
        def _(act):
            def maxima(g, p, qb):
                act.wait_ge(t_mm, g * QB + qb + 1)
                for j in range(HQ):
                    act.activation(qs[p][j][6 * HD:6 * HD + 3, qb * BLK:(qb + 1) * BLK], pr[32 * j:32 * j + 3, :], ACT.Copy)\
                       .then_inc(t_out, 1)

            def take(g, qb, n):
                act.wait_ge(pv_mm, g * NU + n + 1 + PV_AHEAD)
                act.wait_ge(on_done, g * QB + qb + FREE)
                act.activation(ob[:], po[:], ACT.Copy).then_inc(ob_done, 1)

            act.preload_act_table_set(LN_EXP)
            act.sem_inc(e_done, E_AHEAD)
            act.sem_inc(ob_done, FREE)
            act.wait_ge(ready, 4 * HQ + 1)
            for qb in range(QB):
                if last_of[qb] + 2 < LEAD:
                    maxima(0, 0, qb)

            def body(g, p, m, more):
                for n, (qb, kt) in enumerate(units):
                    dk = max(kt - SUB * qb, 0)
                    for s in range(2):
                        act.wait_ge(s2_mm, (g * NU + n) * 2 + s + 1)
                        act.wait_ge(pv_mm, g * NU + n - 1 + PV_AHEAD)
                        act.activation(pt[n % 2][:, 2 * s:2 * s + 2, dk * P:], p2[s][:, :, dk * P:], ACT.Exp,
                                       scale=float(HD) ** -0.5).then_inc(e_done, 1)
                    if n >= 1 and n - 1 in last_of.values():
                        take(g, qb - 1, n - 1)
                    if n in maxima_at and (more or maxima_at[n][1] == 0):
                        mqb, mg = maxima_at[n]
                        maxima(g + mg, p if mg == 0 else 1 - p, mqb)
                take(g, QB - 1, NU - 1)
            groups(body)(act)

        @block.vector
        def _(dve):
            def largest(g, x):
                qb, kt = units[x]
                a, kc = kt % SUB, kt // SUB
                width = BLK if kc < qb else (a + 1) * P
                for j in range(HQ):
                    dve.wait_ge(s1_mm, (g * NU + x) * HQ + j + 1)
                    dve.tensor_reduce(pmx[:, qb % 2, a, j, kc:kc + 1], p1[j % 2][:, 0:width], AX.X, ALU.max)\
                       .then_inc(mx_done, 1)
                if x == last_of[qb]:
                    split(g, qb, x)

            def split(g, qb, x):
                u, k = qb % 2, (g * QB + qb) * 4
                dve.wait_ge(mx_done, (g * NU + x + 1) * HQ + S1_AHEAD)
                dve.tensor_reduce(neg[:, u], pmx[:, u, :, :, 0:qb + 1], AX.X, ALU.max, negate=True).then_inc(cut, 1)
                dve.wait_ge(cut, k + 1)
                dve.tensor_copy(msp[:, u, :, :, 0], neg[:, u]).then_inc(cut, 1)
                dve.wait_ge(cut, k + 2)
                dve.tensor_tensor(res[:, u], neg[:, u], msp[:, u, :, :, 0], ALU.subtract).then_inc(cut, 1)
                dve.wait_ge(cut, k + 3)
                dve.tensor_copy(msp[:, u, :, :, 1], res[:, u]).then_inc(cut, 1)
                dve.wait_ge(cut, k + 4)
                dve.tensor_tensor(msp[:, u, :, :, 2], res[:, u], msp[:, u, :, :, 1], ALU.subtract).then_inc(s_lo, 1)

            def norm(g, qb):
                dve.wait_ge(b_mm, g * QB + qb + 1)
                dve.wait_ge(on_done, g * QB + qb + FREE)
                dve.reciprocal(rec[:], pr[:]).then_inc(rec_done, 1)
                dve.wait_ge(rec_done, g * QB + qb + 1)
                dve.wait_ge(on_st[qb % 2], (g * (QB // 2) + qb // 2) * (HQ * 16))
                dve.tensor_tensor(on[qb % 2][:], ob[:], rec[:], ALU.mult).then_inc(on_done, 1)

            dve.sem_inc(mx_done, S1_AHEAD)
            dve.sem_inc(on_done, FREE)
            dve.memset(msp[:], 0.0).then_inc(ready, 1)
            dve.wait_ge(ready, 4 * HQ + 1)
            for x in range(LEAD):
                largest(0, x)

            def body(g, p, m, more):
                for n in range(NU):
                    if n < LAG:
                        largest(g, n + LEAD)
                    elif more:
                        largest(g + 1, n - LAG)
                    if n in sums_at:
                        norm(g, sums_at[n])
                norm(g, QB - 1)
            groups(body)(dve)


def attention_out(nc, alloc, w, scr, x1, mean3, rstd3, out, scale4):
    sb, ps, sem = alloc
    wo = sb("ao_w", [P, KD, D])
    yt = [sb(f"ao_y{b}", [P, KD, BLK]) for b in range(B)]
    r1 = sb("ao_r1", [P, 2, D])
    raw, mv, tmp = sb("ao_raw", [P, NT, 6]), sb("ao_mv", [P, NT, 2]), sb("ao_tmp", [P, 2, NT])
    po = [ps(f"ao_ps{j}", [P, BLK])[:, 0:D] for j in range(2)]
    weights, mm, res, summed, raw_done, mv_done, step, root_in, root = (
        sem(f"ao_{n}") for n in ("weights", "mm", "res", "summed", "raw", "mv", "step", "root_in", "root"))
    y_in = [sem(f"ao_y_in{b}") for b in range(B)]
    M = B * SUB
    with nc.Block() as block:

        @block.sync
        def _(sp):
            sp.dma_start(wo[:], w["wo"]).then_inc(weights, 16)
            with sp.Fori(0, NB) as i:
                for b in range(B):
                    sp.wait_ge(mm, i * M)
                    sp.dma_start(yt[b][:], scr["at"][:, bass.ds(b * L + i * BLK, BLK)].rearrange("(k p) t -> p k t", p=P))\
                      .then_inc(y_in[b], 16)

        @block.tensor
        def _(pe):
            pe.wait_ge(weights, 16)
            with pe.Fori(0, NB) as i:
                for b in range(B):
                    pe.wait_ge(y_in[b], 16 * (i + 1))
                    for a in range(SUB):
                        pe.wait_ge(summed, i * M + SUB * b + a + 1)
                        for k in range(KD):
                            last = pe.matmul(po[a % 2], yt[b][:, k, a * P:(a + 1) * P], wo[:, k, :],
                                             start=k == 0, stop=k == KD - 1)
                        last.then_inc(mm, 1)

        @block.vector
        def _(dve):
            dve.sem_inc(summed, 2)
            with dve.Fori(0, NB) as i:
                for b in range(B):
                    for a in range(SUB):
                        n = i * M + SUB * b + a
                        t = b * (NT // B) + i * SUB + a
                        at = lambda v: v[:, bass.ds(t, 1)]
                        tok = lambda v: v[:, bass.ds(t, 1), :].rearrange("p a d -> p (a d)")
                        dve.wait_ge(summed, n + 2)
                        dve.tensor_scalar(r1[:, a % 2, :], tok(x1), at(mean3), at(rstd3), ALU.subtract, ALU.mult)\
                           .then_inc(res, 1)
                        dve.wait_ge(res, n + 1)
                        dve.wait_ge(mm, n + 1)
                        dve.tensor_tensor(tok(out), po[a % 2], r1[:, a % 2, :], ALU.add).then_inc(summed, 1)
            dve.wait_ge(summed, NT + 2)
            for t in range(NT):
                dve.bn_stats(raw[:, t, :], out[:, t, :]).then_inc(raw_done, 1)
            for t in range(NT):
                dve.wait_ge(raw_done, t + 1)
                dve.bn_aggr(mv[:, t, :], raw[:, t, :]).then_inc(mv_done, 1)
            dve.wait_ge(mv_done, NT)
            dve.tensor_tensor(tmp[:, 0, :], mv[:, :, 0], mv[:, :, 0], ALU.mult).then_inc(step, 1)
            dve.wait_ge(step, 1)
            dve.tensor_tensor(tmp[:, 1, :], tmp[:, 0, :], mv[:, :, 1], ALU.add).then_inc(step, 1)
            dve.wait_ge(step, 2)
            dve.tensor_scalar(tmp[:, 0, :], tmp[:, 1, :], STD_EPS, None, ALU.add).then_inc(root_in, 1)
            dve.wait_ge(root, 1)
            dve.reciprocal(scale4[:], tmp[:, 1, :]).then_inc(step, 1)

        @block.scalar
        def _(act):
            act.wait_ge(root_in, 1)
            act.activation(tmp[:, 1, :], tmp[:, 0, :], ACT.Sqrt).then_inc(root, 1)


def experts(nc, alloc, w, h_t, x1, acc, out):
    sb, ps, sem = alloc
    gw, gb = sb("ex_gw", [P, KD, NE]), sb("ex_gb", [P, NE])
    w1 = [sb(f"ex_w1{e}", [P, KD, DHID]) for e in range(NE)]
    w2 = [sb(f"ex_w2{e}", [P, DHID // P, D]) for e in range(NE)]
    b1, b2, ones = sb("ex_b1", [P, NE, DHID // P]), sb("ex_b2", [1, NE, D]), sb("ex_ones", [1, P])
    lgt, top, eq, oh, left = (sb("ex_lgt", [P, NT, NE]), sb("ex_top", [P, NT]), sb("ex_eq", [P, NT, NE]),
                              sb("ex_oh", [P, NT, NE]), sb("ex_left", [P, 2, NT]))
    HM = DHID // P
    hid = [sb(f"ex_hid{u}", [P, HM, BLK]) for u in range(2)]
    pg = ps("ex_pg", [P, BLK])
    ph = [ps(f"ex_ph{j}", [P, BLK]) for j in range(4)]
    py = [ps(f"ex_py{j}", [P, BLK])[:, 0:D] for j in range(2)]
    weights, w_in, g_mm, gate, h_mm, relu, y_mm, acc_done, added = (
        sem(f"ex_{n}") for n in ("weights", "w_in", "g_mm", "gate", "h_mm", "relu", "y_mm", "acc", "added"))
    written = sem("ex_written")
    small = [(gw, "gate_w"), (gb, "gate_b"), (b1, "b1"), (b2, "b2"), (ones, "ones")]
    with nc.Block() as block:

        @block.sync
        def _(sp):
            for tile, name in small:
                sp.dma_start(tile[:], w[name]).then_inc(weights, 16)
            for e in range(NE):
                sp.dma_start(w1[e][:], w["w1"][e]).then_inc(w_in, 16)
                sp.dma_start(w2[e][:], w["w2"][e]).then_inc(w_in, 16)
            for b in range(B):
                with sp.Fori(0, NB) as i:
                    sp.wait_ge(acc_done, (b * NB + i + 1) * (NE * SUB) + 2)
                    sp.dma_start(out[b, bass.ds(i * BLK, BLK), :].rearrange("(a p) d -> p a d", p=P),
                                 acc[:, bass.ds(b * (NT // B) + i * SUB, SUB), :]).then_inc(written, 16)
            sp.wait_ge(written, B * NB * 16)

        @block.gpsimd
        def _(pool):
            with pool.Fori(0, NT) as t:
                tok = lambda v: v[:, bass.ds(t, 1), :].rearrange("p a d -> p (a d)")
                pool.tensor_tensor(tok(acc), tok(acc), tok(x1), ALU.add).then_inc(added, 1)

        @block.tensor
        def _(pe):
            pe.wait_ge(weights, 16 * len(small))
            for t in range(NT):
                for k in range(KD):
                    last = pe.matmul(pg[:, t * NE:(t + 1) * NE], h_t[:, k, t * P:(t + 1) * P], gw[:, k, :],
                                     start=k == 0, stop=k == KD - 1)
            last.then_inc(g_mm, 1)
            pe.wait_ge(w_in, 2 * NE * 16)
            for b in range(B):
                with pe.Fori(0, NB) as i:
                    for e in range(NE):
                        x = (b * NB + i) * NE + e
                        for m in range(HM):
                            pe.wait_ge(relu, x * HM + m + 1)
                            for k in range(KD):
                                last = pe.matmul(ph[m % 4][:], w1[e][:, k, m * P:(m + 1) * P],
                                                 h_t[:, k, bass.ds(b * L + i * BLK, BLK)], start=k == 0, stop=k == KD - 1)
                            last.then_inc(h_mm, 1)
                        pe.wait_ge(relu, (x + 1) * HM + 4)
                        for a in range(SUB):
                            pe.wait_ge(acc_done, x * SUB + a + 1)
                            for m in range(HM):
                                pe.matmul(py[a % 2], hid[e % 2][:, m, a * P:(a + 1) * P], w2[e][:, m, :],
                                          start=m == 0, stop=False)
                            pe.matmul(py[a % 2], ones[:], b2[:, e, :], start=False, stop=True).then_inc(y_mm, 1)

        @block.scalar
        def _(act):
            act.sem_inc(relu, 4)
            act.wait_ge(weights, 16 * len(small))
            for b in range(B):
                with act.Fori(0, NB) as i:
                    for e in range(NE):
                        x = (b * NB + i) * NE + e
                        act.wait_ge(y_mm, x * SUB)
                        for m in range(HM):
                            act.wait_ge(h_mm, x * HM + m + 1)
                            act.activation(hid[e % 2][:, m, :], ph[m % 4][:], ACT.Relu, bias=b1[:, e, m:m + 1])\
                               .then_inc(relu, 1)

        @block.vector
        def _(dve):
            dve.wait_ge(g_mm, 1)
            n = 0

            def step(ins):
                nonlocal n
                n += 1
                ins.then_inc(gate, 1)
                dve.wait_ge(gate, n)

            step(dve.tensor_tensor(lgt[:], pg[:, 0:NT * NE].rearrange("p (t e) -> p t e", e=NE),
                                   gb[:].unsqueeze(1).broadcast_to([P, NT, NE]), ALU.add))
            step(dve.tensor_reduce(top[:], lgt[:], AX.X, ALU.max))
            step(dve.tensor_tensor(eq[:], lgt[:], top[:].unsqueeze(2).broadcast_to([P, NT, NE]), ALU.is_equal))
            step(dve.memset(left[:, 0, :], 1.0))
            for e in range(NE):
                step(dve.tensor_tensor(oh[:, :, e], eq[:, :, e], left[:, e % 2, :], ALU.mult))
                step(dve.tensor_tensor(left[:, (e + 1) % 2, :], left[:, e % 2, :], oh[:, :, e], ALU.subtract))
            dve.sem_inc(acc_done, 2)
            dve.wait_ge(added, NT)
            for b in range(B):
                with dve.Fori(0, NB) as i:
                    for e in range(NE):
                        for a in range(SUB):
                            k = ((b * NB + i) * NE + e) * SUB + a
                            t = b * (NT // B) + i * SUB + a
                            tok = lambda v: v[:, bass.ds(t, 1), :].rearrange("p a d -> p (a d)")
                            dve.wait_ge(y_mm, k + 1)
                            if e >= 1:
                                dve.wait_ge(acc_done, k - SUB + 1 + 2)
                            dve.scalar_tensor_tensor(tok(acc), py[a % 2],
                                                     oh[:, bass.ds(t, 1), e:e + 1].rearrange("p a b -> p (a b)"), tok(acc),
                                                     ALU.mult, ALU.add).then_inc(acc_done, 1)


def program(nc, a, out):
    ctx = ExitStack()
    with ctx:
        def scope(stack):
            def sb(name, shape, dt=F32):
                return stack.enter_context(nc.sbuf_tensor(name, shape, dt))

            def ps(name, shape, dt=F32):
                return stack.enter_context(nc.psum_tensor(name, shape, dt))

            def sem(name):
                return ctx.enter_context(nc.semaphore(name))
            return sb, ps, sem

        sb, ps, sem = scope(ctx)
        scr = {n: nc.dram_tensor(f"scr_{n}", s, F32, kind="Internal").ap() for n, s in
               {n: (HP, SB_, P, DH, B, TB) for n in ("zs", "xc", "bc", "yg")}.items()}
        scr.update({n: nc.dram_tensor(f"scr_{n}", (HP, SB_, 3, P, DH, B, TB), BF16, kind="Internal").ap()
                    for n in ("dl", "ux")})
        scr.update({n: nc.dram_tensor(f"scr_{n}", sh, dt, kind="Internal").ap() for n, sh, dt in
                    (("qs", (3, D, TOK), BF16), ("ks", (3, D, TOK), BF16), ("v", (TOK, NH, VW), F32),
                     ("at", (D, TOK), F32))})
        ident = sb("ident", [P, P])
        mean, rstd = sb("mean", [P, NT]), sb("rstd", [P, NT])
        mean3, rstd3, scale3, scale4 = (sb(n, [P, NT]) for n in ("mean3", "rstd3", "scale3", "scale4"))
        with nc.Block() as block:
            ident_in = sem("ident_in")

            @block.sync
            def _(sp):
                sp.dma_start(ident[:], a["ident"]).then_inc(ident_in, 16)
                sp.wait_ge(ident_in, 16)
        with ExitStack() as phase:
            xn_t = scope(phase)[0]("xn_t", [P, KD, TOK])
            with ExitStack() as part:
                xs, scale = scope(part)[0]("in_tokens", [P, NT, D]), scope(part)[0]("in_scale", [P, NT])
                input_stats(nc, scope(part), a["x"], xs, mean, rstd, scale)
                to_features(nc, scope(part), "f1", xs, mean, scale, a["in_alpha"], a["in_beta"], ident, xn_t)
            with ExitStack() as part:
                projections(nc, scope(part), a, xn_t, scr)
        with ExitStack() as part:
            selective_scan(nc, scope(part), a, scr)
        x1 = sb("x1", [P, NT, D])
        with ExitStack() as part:
            back_to_tokens(nc, scope(part), a, scr, a["x"], mean, rstd, x1, mean3, scale3, rstd3)
        with ExitStack() as phase:
            h_t = scope(phase)[0]("h1_t", [P, KD, TOK])
            with ExitStack() as part:
                to_features(nc, scope(part), "f2", x1, mean3, scale3, a["norm1"], None, ident, h_t)
            with ExitStack() as part:
                latents(nc, scope(part), a, h_t, scr)
        with ExitStack() as part:
            attention(nc, scope(part), a, scr)
        acc = sb("acc", [P, NT, D])
        with ExitStack() as part:
            attention_out(nc, scope(part), a, scr, x1, mean3, rstd3, acc, scale4)
        with ExitStack() as phase:
            h_t = scope(phase)[0]("h2_t", [P, KD, TOK])
            with ExitStack() as part:
                to_features(nc, scope(part), "f3", acc, None, scale4, a["norm2"], None, ident, h_t)
            with ExitStack() as part:
                experts(nc, scope(part), a, h_t, x1, acc, out)


def host_layouts(inputs):
    g = lambda n: np.ascontiguousarray(inputs[n])
    cols = lambda v, n: np.ascontiguousarray(v.reshape(n, P).T)
    rows_t = lambda w: np.ascontiguousarray(w.T.reshape(w.shape[1] // P, P, w.shape[0]).transpose(1, 0, 2))
    a = {"x": g("L0_attn_x"), "ident": np.eye(P, dtype=np.float32)}
    a["in_alpha"], a["in_beta"] = cols(g("L0_attn_in_norm_alpha"), KD), cols(g("L0_attn_in_norm_bias"), KD)
    a["in_w"], a["in_b"] = rows_t(g("L0_attn_in_proj_w")), cols(g("L0_attn_in_proj_b"), 2 * MI)
    a["cv_w"] = np.ascontiguousarray(g("L0_attn_conv_w").reshape(MI, P, KC).transpose(1, 0, 2))
    a["cv_b"] = cols(g("L0_attn_conv_b"), MI)
    a["dt_w"], a["dt_b"] = rows_t(g("L0_attn_dt_proj_w")), cols(g("L0_attn_dt_proj_b"), MI)
    bc = g("L0_attn_x_proj_w").reshape(2, NS, DI)
    rep = np.tile(bc, (1, P // NS, 1))
    a["bc_w"] = np.ascontiguousarray(rep.reshape(2, P, MI, P).transpose(3, 2, 0, 1))
    a["bc_b"] = np.ascontiguousarray(np.tile(g("L0_attn_x_proj_b").reshape(2, NS), (1, P // NS)).T)
    wide = lambda v: np.ascontiguousarray(np.broadcast_to(v, (P,) + v.shape))
    a["out_w"], a["out_b"] = rows_t(g("L0_attn_out_proj_w")), wide(g("L0_attn_out_proj_b"))
    a["gamma"], a["beta"] = wide(g("L0_attn_norm_alpha")), wide(g("L0_attn_norm_bias"))
    a["norm1"], a["norm2"] = cols(g("L0_ffn_norm1_w"), KD), cols(g("L0_ffn_norm2_w"), KD)
    half = lambda v: np.ascontiguousarray(v.reshape(NH, 2, HD // 2, -1)[:, ::-1].reshape(D, -1))
    both = lambda v: np.concatenate([v, half(v)], 0)
    a["wq"] = rows_t(both(g("L0_ffn_Wq")))
    a["wk"] = np.ascontiguousarray(both(g("L0_ffn_Wuk")).T)
    a["wl"] = rows_t(g("L0_ffn_Wdkv"))
    a["wv"] = np.ascontiguousarray(g("L0_ffn_Wuv").T)
    a["wo"] = rows_t(g("L0_ffn_Wo"))
    a["ln_g"], a["ln_b"] = cols(g("L0_ffn_ln_g"), 1), cols(g("L0_ffn_ln_b"), 1)
    inv = (1.0 / np.float32(10000.0) ** (np.arange(HD // 2, dtype=np.float32) / np.float32(HD // 2))).astype(np.float32)
    ang = inv[np.arange(P) % (HD // 2)][:, None] * np.arange(L, dtype=np.float32)[None]
    sign = np.where(np.arange(P) % HD < HD // 2, -1.0, 1.0).astype(np.float32)[:, None]
    a["cos"], a["sin"] = np.cos(ang).astype(np.float32), (np.sin(ang) * sign).astype(np.float32)
    a["avg"] = np.full((P, P), 1.0 / LAT, np.float32)
    a["idb"] = np.eye(P).astype(mybir.dt.np(BF16))
    later = np.where(np.arange(P)[None] > np.arange(P)[:, None], -1.0e30, 0.0)
    a["later"] = np.ascontiguousarray(np.stack([later, later.T], 1).astype(mybir.dt.np(BF16)))
    a["dsel"] = np.ascontiguousarray((np.arange(P)[:, None] == 32 * (np.arange(P)[None] // 32) + HD).astype(np.float32))
    a["gate_w"], a["gate_b"] = rows_t(g("L0_ffn_gate_w")), wide(g("L0_ffn_gate_b"))
    a["w1"] = np.stack([rows_t(v) for v in g("L0_ffn_W1")])
    a["w2"] = np.stack([rows_t(v) for v in g("L0_ffn_W2")])
    a["b1"] = np.ascontiguousarray(g("L0_ffn_b1").reshape(NE, DHID // P, P).transpose(2, 0, 1))
    a["b2"], a["ones"] = g("L0_ffn_b2")[None], np.ones((1, P), np.float32)
    p, eye = np.arange(P), np.eye(P, dtype=np.float32)
    pick = np.stack([eye[:32, GD * i + p // NS] for i in range(4)], 1)
    a["sel"] = np.ascontiguousarray(np.tile(pick, (3, 1, 1)).astype(mybir.dt.np(BF16)))
    a["ysel"] = np.ascontiguousarray(np.stack([(np.arange(32)[None] == 8 * i + p[:, None] // NS) for i in range(4)], 1)
                                     .astype(np.float32))
    a["pool16"] = np.ascontiguousarray((p[:, None] // NS == p[None] // NS).astype(np.float32))
    a_log = g("L0_attn_A_log").reshape(HP, DH, 4, 4, GD * NS)
    order = np.array([tile_place(s) for s in range(TL)])
    par = np.zeros((P, HP, SB_, TL + DH + 1), np.float32)
    for h in range(HP):
        par[:, h, :, :TL] = a_log[h, order[:, 0], order[:, 1], order[:, 2]].T[:, None]
        par[:, h, :, TL:TL + DH] = g("L0_attn_D").reshape(HP, DH, P)[h].T[:, None]
    par[:, :, 1:, TL + DH] = 1.0
    a["par"] = np.ascontiguousarray(par.reshape(P, HP * SB_, TL + DH + 1))
    return a


def kernel(**inputs):
    import concourse.bacc as _bacc
    from concourse.bass_utils import run_bass_kernel_spmd as _run

    nc = _bacc.Bacc("TRN2", target_bir_lowering=False, num_devices=1)
    arrays, aps = {}, {}
    for name, v in host_layouts(inputs).items():
        arrays[f"in_{name}"] = v
        aps[name] = nc.dram_tensor(f"in_{name}", v.shape, mybir.dt.from_np(v.dtype), kind="ExternalInput").ap()
    out = nc.dram_tensor("out_0_dram", (B, L, D), F32, kind="ExternalOutput").ap()
    program(nc, aps, out)
    r = _run(nc, [arrays], core_ids=[0])
    return r.results[0]["out_0_dram"]
```

```python
from contextlib import ExitStack

import numpy as np

import concourse.bass as bass
from concourse import mybir

F32 = mybir.dt.float32
BF16 = mybir.dt.bfloat16
ALU = mybir.AluOpType
ACT = mybir.ActivationFunctionType
AX = mybir.AxisListType

P = 128
B, L, D = 2, 2048, 256
DI, NS, KC = 512, 16, 4
TOK = B * L
NT = TOK // P
KD = D // P
MI = DI // P
BLK = 512
NB = L // BLK
HP = 2
DH = MI // HP
TB = 128
SB_ = L // TB
SUB = BLK // TB
CH = 16
NC_ = TB // CH
GD = P // NS
TL = DH * P // GD
ST = TL * B
W1 = CH + 1
IT = 8
TI = TL // IT
NH, HD, LAT = 16, 16, 128
VW = 32
NE, DHID = 4, 1024
H_MAX = 10.0
INP_AT = [(), (0,), (1,), (2,), (3,), (4,), (5,), (6, 7)]
SPREAD_AT = [(0,), (1,), (2,), (3,), (4,), (5,), (6,), (7,)]
SUMS_AT = [(0, 1), (2, 3), (4, 5), (6, 7), (), (), (), ()]
DA_MIN = float(np.exp(np.float32(-10.0)))
LN_EPS = 1e-5
STD_EPS = 1e-6
BESSEL = D / (D - 1)
DT_MIN, DT_MAX = 1e-4, 10.0
LN_EXP, SQRT_SET = "natural_log_exp_and_others", "sqrt_and_others"


def input_stats(nc, alloc, x, ident_rows, ident, xs, mean, rstd, scale):
    sb, _, sem = alloc
    raw = sb("in_bn_raw", [P, NT, 6])
    mv = sb("in_mean_var", [P, NT, 2])
    tmp = sb("in_tmp", [P, 4, NT])
    LOADS = 4
    per = NT // LOADS
    x_in = [sem(f"in_x_in{j}") for j in range(LOADS)]
    raw_done, mv_done, var_eps, roots, step = (sem(f"in_{n}") for n in ("raw", "mv", "var_eps", "roots", "step"))
    ident_in = sem("in_ident")
    xt = x.rearrange("b (t p) d -> p (b t) d", p=P)
    with nc.Block() as block:

        @block.sync
        def _(sp):
            for j in range(LOADS):
                sp.dma_start(xs[:, j * per:(j + 1) * per, :], xt[:, j * per:(j + 1) * per, :]).then_inc(x_in[j], 16)
            sp.dma_start(ident[:], ident_rows).then_inc(ident_in, 16)
            sp.wait_ge(ident_in, 16)

        @block.vector
        def _(dve):
            for j in range(LOADS):
                dve.wait_ge(x_in[j], 16)
                for t in range(j * per, (j + 1) * per):
                    dve.bn_stats(raw[:, t, :], xs[:, t, :]).then_inc(raw_done, 1)
            for t in range(NT):
                dve.wait_ge(raw_done, t + 1)
                dve.bn_aggr(mv[:, t, :], raw[:, t, :]).then_inc(mv_done, 1)
            dve.wait_ge(mv_done, NT)
            dve.tensor_scalar(tmp[:, 0, :], mv[:, :, 1], LN_EPS, None, ALU.add).then_inc(var_eps, 1)
            dve.tensor_copy(mean[:], mv[:, :, 0]).then_inc(step, 1)
            dve.wait_ge(roots, 2)
            dve.reciprocal(rstd[:], tmp[:, 1, :]).then_inc(step, 1)
            dve.wait_ge(step, 2)
            dve.tensor_tensor(tmp[:, 3, :], tmp[:, 2, :], rstd[:], ALU.mult).then_inc(step, 1)
            dve.wait_ge(step, 3)
            dve.tensor_scalar(scale[:], tmp[:, 3, :], STD_EPS, None, ALU.add).then_inc(step, 1)
            dve.wait_ge(step, 4)
            dve.reciprocal(tmp[:, 3, :], scale[:]).then_inc(step, 1)
            dve.wait_ge(step, 5)
            dve.tensor_tensor(scale[:], tmp[:, 3, :], rstd[:], ALU.mult).then_inc(step, 1)

        @block.scalar
        def _(act):
            act.wait_ge(var_eps, 1)
            act.activation(tmp[:, 1, :], tmp[:, 0, :], ACT.Sqrt).then_inc(roots, 1)
            act.activation(tmp[:, 2, :], mv[:, :, 1], ACT.Sqrt, scale=BESSEL).then_inc(roots, 1)


def to_features(nc, alloc, tag, xs, mean, scale, alpha, beta, ident, out):
    sb, ps, sem = alloc
    centred = [sb(f"{tag}_centred{u}", [P, 4, D]) for u in range(2)]
    weight, bias = sb(f"{tag}_weight", [P, KD]), sb(f"{tag}_bias", [P, KD])
    tr = [[ps(f"{tag}_tr{u}{k}", [P, BLK]) for k in range(KD)] for u in range(2)]
    w_in, scaled, turned, stored = (sem(f"{tag}_{n}") for n in ("w_in", "scaled", "turned", "stored"))
    loads = [(weight, alpha)] + ([(bias, beta)] if beta is not None else [])
    with nc.Block() as block:

        @block.sync
        def _(sp):
            for tile, src in loads:
                sp.dma_start(tile[:], src).then_inc(w_in, 16)

        @block.vector
        def _(dve):
            for g in range(NT // 4):
                if g >= 2:
                    dve.wait_ge(turned, 2 * (g - 1))
                for a in range(4):
                    t = 4 * g + a
                    if mean is None:
                        dve.tensor_scalar(centred[g % 2][:, a, :], xs[:, t, :], scale[:, t:t + 1], None,
                                          ALU.mult).then_inc(scaled, 1)
                    else:
                        dve.tensor_scalar(centred[g % 2][:, a, :], xs[:, t, :], mean[:, t:t + 1], scale[:, t:t + 1],
                                          ALU.subtract, ALU.mult).then_inc(scaled, 1)

        @block.scalar
        def _(act):
            act.wait_ge(w_in, 16 * len(loads))
            for g in range(NT // 4):
                for k in range(KD):
                    act.wait_ge(turned, KD * g + k + 1)
                    act.activation(out[:, k, g * BLK:(g + 1) * BLK], tr[g % 2][k][:], ACT.Identity,
                                   bias=bias[:, k:k + 1] if beta is not None else 0.0,
                                   scale=weight[:, k:k + 1]).then_inc(stored, 1)

        @block.tensor
        def _(pe):
            for g in range(NT // 4):
                pe.wait_ge(scaled, 4 * g + 4)
                for k in range(KD):
                    if g >= 2:
                        pe.wait_ge(stored, KD * (g - 2) + k + 1)
                    for a in range(4):
                        last = pe.transpose(tr[g % 2][k][:, a * P:(a + 1) * P],
                                            centred[g % 2][:, a, k * P:(k + 1) * P], ident[:])
                    last.then_inc(turned, 1)


def projections(nc, alloc, w, xn_t, scr):
    sb, ps, sem = alloc
    w_in = sb("pj_w_in", [P, KD, 2 * DI])
    b_in = sb("pj_b_in", [P, 2 * MI])
    w_cv = sb("pj_w_cv", [P, MI, KC])
    b_cv = sb("pj_b_cv", [P, MI])
    w_dt = sb("pj_w_dt", [P, MI, DI])
    b_dt = sb("pj_b_dt", [P, MI])
    w_bc = sb("pj_w_bc", [P, MI, 2, P])
    b_bc = sb("pj_b_bc", [P, 2])
    halo = KC - 1
    xin = [sb(f"pj_xin{b}", [P, MI, halo + BLK]) for b in range(B)]
    cv = [sb(f"pj_cv{b}", [P, MI, BLK]) for b in range(B)]
    xc = [sb(f"pj_xc{b}", [P, MI, BLK]) for b in range(B)]
    zs = [sb(f"pj_zs{b}", [P, MI, BLK]) for b in range(B)]
    dl = [sb(f"pj_dl{b}", [P, MI, BLK]) for b in range(B)]
    ux = [sb(f"pj_ux{b}", [P, MI, BLK]) for b in range(B)]
    bc = [sb(f"pj_bc{b}", [P, 2, BLK]) for b in range(B)]
    cuts = [sb(f"pj_{n}_cuts", [P, 3, MI, BLK], BF16) for n in ("dl", "ux")]
    ps_x = [ps(f"pj_ps_x{j}", [P, BLK]) for j in range(2)]
    ps_z = [ps(f"pj_ps_z{j}", [P, BLK]) for j in range(2)]
    ps_d = [ps(f"pj_ps_d{j}", [P, BLK]) for j in range(2)]
    ps_b = [ps(f"pj_ps_b{j}", [P, BLK]) for j in range(2)]
    weights, late_weights = sem("pj_weights"), sem("pj_late_weights")
    x_mm, z_mm, d_mm, b_mm = (sem(f"pj_{n}_mm") for n in "xzdb")
    x_out, z_out, d_out, b_out = (sem(f"pj_{n}_out") for n in "xzdb")
    zeroed, halo_ok, tap, conv_done = sem("pj_zeroed"), sem("pj_halo"), sem("pj_tap"), sem("pj_conv")
    xc_done, exp_done, ln_done = sem("pj_xc"), sem("pj_exp"), sem("pj_ln")
    dl_done, ux_done = sem("pj_dl"), sem("pj_ux")
    act_stored = [sem(f"pj_act_stored{b}") for b in range(B)]
    hi_done, mid_done, rest_done, cut = sem("pj_hi"), sem("pj_mid"), sem("pj_rest"), sem("pj_cut")
    cut_stored = [sem(f"pj_{n}_stored") for n in ("dl", "ux")]
    ACT_ST, CUT_ST = 3 * HP * 16, 3 * HP * 16
    M2 = B * MI
    loads = [(w_in, w["in_w"]), (b_in, w["in_b"]), (w_cv, w["cv_w"]), (b_cv, w["cv_b"])]
    late_loads = [(w_bc, w["bc_w"]), (b_bc, w["bc_b"]), (w_dt, w["dt_w"]), (b_dt, w["dt_b"])]
    with nc.Block() as block:

        @block.gpsimd
        def _(pool):
            with pool.Fori(0, NB) as i:
                for b in range(B):
                    for t, rest in enumerate((dl[b], ux[b])):
                        n = (i * B + b) * 2 + t
                        pool.wait_ge(mid_done, n + 1)
                        pool.tensor_tensor(rest[:], rest[:], cuts[t][:, 0], ALU.subtract).then_inc(cut, 1)
                        pool.wait_ge(cut, n + 1)
                        pool.tensor_tensor(cuts[t][:, 2], rest[:], cuts[t][:, 1], ALU.subtract).then_inc(rest_done, 1)

        @block.sync
        def _(sp):
            def store(name, tile, i, b, done):
                n = tile.shape[1] // (HP if name != "bc" else 1)
                for h in range(HP):
                    own = tile[:, h * n:(h + 1) * n, :] if name != "bc" else tile[:]
                    sp.dma_start(scr[name][h, bass.ds(i * SUB, SUB), :, :, b, :].rearrange("n p d t -> p d n t"),
                                 own.rearrange("p d (n t) -> p d n t", t=TB)).then_inc(done, 16)

            for tile, src in loads:
                sp.dma_start(tile[:], src).then_inc(weights, 16)
            for tile, src in late_loads:
                sp.dma_start(tile[:], src).then_inc(late_weights, 16)
            with sp.Fori(0, NB) as i:
                for b in range(B):
                    sp.wait_ge(z_out, i * M2 + MI * (b + 1) + 2)
                    store("zs", zs[b], i, b, act_stored[b])
                    sp.wait_ge(xc_done, i * M2 + MI * (b + 1))
                    store("xc", xc[b], i, b, act_stored[b])
                for b in range(B):
                    sp.wait_ge(b_out, i * 2 * B + 2 * (b + 1) + 2)
                    store("bc", bc[b], i, b, act_stored[b])
                    for t, name in enumerate(("dl", "ux")):
                        sp.wait_ge(rest_done, (i * B + b) * 2 + t + 1)
                        for h in range(HP):
                            for part in range(3):
                                sp.dma_start(
                                    scr[name][h, bass.ds(i * SUB, SUB), part, :, :, b, :].rearrange("n p d t -> p d n t"),
                                    cuts[t][:, part, h * DH:(h + 1) * DH, :].rearrange("p d (n t) -> p d n t", t=TB))\
                                  .then_inc(cut_stored[t], 16)
            for b in range(B):
                sp.wait_ge(act_stored[b], NB * ACT_ST)
            for t in range(2):
                sp.wait_ge(cut_stored[t], NB * B * CUT_ST)

        @block.tensor
        def _(pe):
            pe.wait_ge(weights, 16 * len(loads))
            with pe.Fori(0, NB) as i:
                for b in range(B):
                    rhs = [xn_t[:, k, bass.ds(b * L + i * BLK, BLK)] for k in range(KD)]
                    for m in range(MI):
                        pe.wait_ge(x_out, i * M2 + MI * b + m + 1)
                        for k in range(KD):
                            mm = pe.matmul(ps_x[m % 2][:], w_in[:, k, m * P:(m + 1) * P], rhs[k],
                                           start=k == 0, stop=k == KD - 1)
                        mm.then_inc(x_mm, 1)
                        pe.wait_ge(z_out, i * M2 + MI * b + m + 1)
                        for k in range(KD):
                            mm = pe.matmul(ps_z[m % 2][:], w_in[:, k, DI + m * P:DI + (m + 1) * P], rhs[k],
                                           start=k == 0, stop=k == KD - 1)
                        mm.then_inc(z_mm, 1)
                pe.wait_ge(late_weights, 16 * len(late_loads))
                for b in range(B):
                    pe.wait_ge(xc_done, i * M2 + MI * (b + 1))
                    for c in range(2):
                        pe.wait_ge(b_out, i * 2 * B + 2 * b + c + 1)
                        for k in range(MI):
                            mm = pe.matmul(ps_b[c][:], w_bc[:, k, c, :], xc[b][:, k, :], start=k == 0, stop=k == MI - 1)
                        mm.then_inc(b_mm, 1)
                    for m in range(MI):
                        pe.wait_ge(d_out, i * M2 + MI * b + m + 1)
                        for k in range(MI):
                            mm = pe.matmul(ps_d[m % 2][:], w_dt[:, k, m * P:(m + 1) * P], xc[b][:, k, :],
                                           start=k == 0, stop=k == MI - 1)
                        mm.then_inc(d_mm, 1)

        @block.vector
        def _(dve):
            for b in range(B):
                dve.memset(xin[b][:], 0.0).then_inc(zeroed, 1)
            dve.sem_inc(x_out, 2)
            dve.sem_inc(d_out, 2)
            dve.wait_ge(weights, 16 * len(loads))
            dve.wait_ge(zeroed, B)

            def inputs(i, b):
                dve.wait_ge(conv_done, i * M2)
                dve.tensor_copy(xin[b][:, :, 0:halo], xin[b][:, :, BLK:BLK + halo]).then_inc(halo_ok, 1)
                dve.wait_ge(halo_ok, i * B + b + 1)
                dve.wait_ge(xc_done, i * M2)
                for m in range(MI):
                    n = i * M2 + MI * b + m
                    dve.wait_ge(x_mm, n + 1)
                    dve.tensor_scalar(xin[b][:, m, halo:], ps_x[m % 2][:], b_in[:, m:m + 1], None,
                                      ALU.add).then_inc(x_out, 1)
                    dve.wait_ge(x_out, n + 3)
                    dve.tensor_scalar(cv[b][:, m, :], xin[b][:, m, 0:BLK], w_cv[:, m, 0:1], b_cv[:, m:m + 1],
                                      ALU.mult, ALU.add).then_inc(tap, 1)
                    for j in range(1, KC):
                        dve.wait_ge(tap, n * (KC - 1) + j)
                        dve.scalar_tensor_tensor(cv[b][:, m, :], xin[b][:, m, j:j + BLK], w_cv[:, m, j:j + 1],
                                                 cv[b][:, m, :], ALU.mult, ALU.add)\
                           .then_inc(tap if j < KC - 1 else conv_done, 1)

            def steps(i, b):
                for m in range(MI):
                    n = i * M2 + MI * b + m
                    dve.wait_ge(d_mm, n + 1)
                    dve.tensor_scalar(dl[b][:, m, :], ps_d[m % 2][:], b_dt[:, m:m + 1], 20.0,
                                      ALU.add, ALU.min).then_inc(d_out, 1)

            def products(i, b):
                for m in range(MI):
                    n = i * M2 + MI * b + m
                    dve.wait_ge(ln_done, n + 1)
                    dve.tensor_scalar(dl[b][:, m, :], dl[b][:, m, :], DT_MIN, DT_MAX,
                                      ALU.max, ALU.min).then_inc(dl_done, 1)
                    dve.wait_ge(dl_done, n + 1)
                    dve.tensor_tensor(ux[b][:, m, :], dl[b][:, m, :], xc[b][:, m, :], ALU.mult).then_inc(ux_done, 1)
                dve.wait_ge(ux_done, i * M2 + MI * (b + 1))
                for t, whole in enumerate((dl[b], ux[b])):
                    dve.wait_ge(cut_stored[t], (i * B + b) * CUT_ST)
                    dve.tensor_copy(cuts[t][:, 0], whole[:]).then_inc(hi_done, 1)
                for t, whole in enumerate((dl[b], ux[b])):
                    dve.wait_ge(hi_done, (i * B + b) * 2 + t + 1)
                    dve.tensor_tensor(cuts[t][:, 1], whole[:], cuts[t][:, 0], ALU.subtract).then_inc(mid_done, 1)

            def turn(i, first):
                inputs(i, 0)
                if not first:
                    products(i - 1, 1)
                inputs(i, 1)
                dve.wait_ge(late_weights, 16 * len(late_loads))
                for b in range(B):
                    if not first:
                        dve.wait_ge(rest_done, (i * B + b) * 2 - 2)
                    steps(i, b)
                    if b == 0:
                        products(i, 0)

            turn(0, True)
            with dve.Fori(1, NB) as i:
                turn(i, False)
            products(NB - 1, 1)

        @block.scalar
        def _(act):
            act.sem_inc(z_out, 2)
            act.sem_inc(b_out, 2)
            act.wait_ge(weights, 16 * len(loads))
            with act.Fori(0, NB) as i:
                for b in range(B):
                    act.wait_ge(act_stored[b], i * ACT_ST)
                    for m in range(MI):
                        n = i * M2 + MI * b + m
                        act.wait_ge(z_mm, n + 1)
                        act.activation(zs[b][:, m, :], ps_z[m % 2][:], ACT.Silu,
                                       bias=b_in[:, MI + m:MI + m + 1]).then_inc(z_out, 1)
                        act.wait_ge(conv_done, n + 1)
                        act.activation(xc[b][:, m, :], cv[b][:, m, :], ACT.Silu).then_inc(xc_done, 1)
                act.preload_act_table_set(LN_EXP)
                act.wait_ge(late_weights, 16 * len(late_loads))
                for b in range(B):
                    for c in range(2):
                        act.wait_ge(b_mm, i * 2 * B + 2 * b + c + 1)
                        act.activation(bc[b][:, c, :], ps_b[c][:], ACT.Identity, bias=b_bc[:, c:c + 1])\
                           .then_inc(b_out, 1)
                    for m in range(MI):
                        n = i * M2 + MI * b + m
                        act.wait_ge(d_out, n + 3)
                        act.activation(dl[b][:, m, :], dl[b][:, m, :], ACT.Exp).then_inc(exp_done, 1)
                    for m in range(MI):
                        n = i * M2 + MI * b + m
                        act.wait_ge(exp_done, n + 1)
                        act.activation(dl[b][:, m, :], dl[b][:, m, :], ACT.Ln, bias=1.0).then_inc(ln_done, 1)



def tile_place(st):
    item, jr, e = st // TI, (st % TI) // 2, st % 2
    d, q, r = item // 4, item // 2 % 2, item % 2
    return d, 2 * r + jr, 2 * q + e


def selective_scan(nc, alloc, w, scr):
    sb, ps, sem = alloc
    NJ = HP * SB_
    sel = sb("sc_sel", [3 * 32, 4, P], BF16)
    ysel = sb("sc_ysel", [P, 4, 32])
    pool16 = sb("sc_pool16", [P, P])
    par = sb("sc_par", [P, NJ, TL + DH + 1])
    dA = [sb(f"sc_dA{q}", [P, NC_, ST, W1]) for q in range(2)]
    hb = [sb(f"sc_h{q}", [P, NC_, ST, W1]) for q in range(2)]
    dl = [sb(f"sc_dl{q}", [3 * 32, DH, 4, B, TB], BF16) for q in range(2)]
    ux = [sb(f"sc_ux{q}", [3 * 32, DH, 4, B, TB], BF16) for q in range(2)]
    bt = [sb(f"sc_b{q}", [P, B, TB]) for q in range(2)]
    ct = [sb(f"sc_c{q}", [P, B, TB]) for q in range(2)]
    xc = [sb(f"sc_xc{q}", [P, DH, B, TB]) for q in range(2)]
    zs = [sb(f"sc_zs{q}", [P, DH, B, TB]) for q in range(2)]
    yv = [sb(f"sc_yv{q}", [P, DH, B, TB]) for q in range(2)]
    yg = [sb(f"sc_yg{q}", [P, DH, B, TB]) for q in range(2)]
    sq = sb("sc_sq", [P, ST])
    capped = sb("sc_capped", [P, ST])
    tiny = sb("sc_tiny", [P, 1])
    lg = sb("sc_lg", [P, ST])
    scl = [sb(f"sc_scl{q}", [P, ST]) for q in range(2)]
    ps_d = [ps(f"sc_ps_d{q}", [P, 2, 2, B * TB]) for q in range(2)]
    ps_u = ps("sc_ps_u", [P, 2, 2, B * TB])
    ps_y = ps("sc_ps_y", [P, DH, B * TB])
    ps_n = ps("sc_ps_n", [P, BLK])

    consts, decay = sem("sc_consts"), sem("sc_decay")
    cleared = sem("sc_cleared")
    in_a = [sem(f"sc_in_a{q}") for q in range(2)]
    in_c = [sem(f"sc_in_c{q}") for q in range(2)]
    in_x = [sem(f"sc_in_x{q}") for q in range(2)]
    stored = [sem(f"sc_stored{q}") for q in range(2)]
    d_mm, u_mm, n_mm, y_mm = (sem(f"sc_{n}_mm") for n in "duny")
    exp_done, clip_done, inp_done = sem("sc_exp"), sem("sc_clip"), sem("sc_inp")
    scan_done, sq_done, capped_done, lg_done, scl_done, head_done = (
        sem(f"sc_{n}") for n in ("scan", "sq", "capped", "lg", "scl", "head"))
    last_done, c_done, seen = sem("sc_last"), sem("sc_cmul"), sem("sc_seen")
    y_done, gate_done = sem("sc_y"), sem("sc_gate")
    IN_A = (2 * 4 + 1) * 16
    EXP_AHEAD, LAST_AHEAD, GATE_AHEAD = 2 * TI, 1, 2

    def turns(eng, turn):
        for u in range(2):
            turn(u, u, 0, u == 0, False)
        with eng.Fori(1, NJ // 2 - 1) as m:
            for u in range(2):
                turn(2 * m + u, u, m, False, False)
        for u in range(2):
            turn(NJ - 2 + u, u, NJ // 2 - 1, False, u == 1)

    blocks = {n: scr[n].rearrange("h n p d b t -> (h n) p d b t") for n in ("xc", "zs", "yg", "bc")}
    cut_blocks = {n: scr[n].rearrange("h n s p d b t -> (h n) s p d b t") for n in ("dl", "ux")}

    def block_of(name, j):
        return blocks[name][bass.ds(j, 1)].rearrange("n p d b t -> (n p) d b t")

    with nc.Block() as block:

        @block.sync
        def _(sp):
            def load_a(j, q):
                for name, tile in (("dl", dl[q]), ("ux", ux[q])):
                    for quad in range(4):
                        src = cut_blocks[name][bass.ds(j, 1), :, 32 * quad:32 * quad + 32]
                        sp.dma_start(tile[:, :, quad].rearrange("p d b t -> p d (b t)"),
                                     src.rearrange("n s p d b t -> (n s) p d (b t)")).then_inc(in_a[q], 16)
                sp.dma_start(bt[q][:], block_of("bc", j)[:, 0]).then_inc(in_a[q], 16)

            def load_c(j, q):
                sp.dma_start(ct[q][:], block_of("bc", j)[:, 1]).then_inc(in_c[q], 16)

            def load_x(j, q):
                sp.dma_start(xc[q][:], block_of("xc", j)).then_inc(in_x[q], 16)
                sp.dma_start(zs[q][:], block_of("zs", j)).then_inc(in_x[q], 16)

            def turn(j, u, m, first, last):
                ahead = not (isinstance(j, int) and j + 2 >= NJ)
                if ahead:
                    sp.wait_ge(d_mm, (j + 1) * IT)
                    sp.wait_ge(inp_done, (j + 1) * 2 * IT)
                    load_a(j + 2, u)
                if not first:
                    sp.wait_ge(gate_done, j + GATE_AHEAD)
                    sp.dma_start(block_of("yg", j - 1), yg[1 - u][:]).then_inc(stored[1 - u], 16)
                if not last:
                    load_x(j + 1, 1 - u)
                if ahead:
                    sp.wait_ge(c_done, (j + 1) * NC_)
                    load_c(j + 2, u)

            for name, tile in (("sel", sel), ("ysel", ysel), ("pool16", pool16), ("par", par)):
                sp.dma_start(tile[:], w[name]).then_inc(consts, 16)
            for q in range(2):
                load_a(q, q)
                load_c(q, q)
            load_x(0, 0)
            turns(sp, turn)
            sp.wait_ge(gate_done, NJ + GATE_AHEAD)
            sp.dma_start(block_of("yg", NJ - 1), yg[1][:]).then_inc(stored[1], 16)
            for q in range(2):
                sp.wait_ge(stored[q], 16 * NJ // 2)

        @block.tensor
        def _(pe):
            def spread(out, src, item, jr_e):
                jr, e = jr_e
                d, quad, i = tile_place(item * TI + 2 * jr + e)
                return pe.matmul(out[:, jr, e, :], sel[:, i, :], src[:, d, quad].rearrange("p b t -> p (b t)"),
                                 start=True, stop=True)

            def decays(jj, q, item):
                pe.wait_ge(exp_done, (jj * IT + item) * TI + TI)
                if item == 0 and not (isinstance(jj, int) and jj == 0):
                    pe.wait_ge(inp_done, jj * IT * 2)
                for e in range(2):
                    for jr in range(2):
                        mm = spread(ps_d[item % 2], dl[q], item, (jr, e))
                mm.then_inc(d_mm, 1)

            def inputs(jj, q, item):
                if item < IT - 1:
                    pe.wait_ge(inp_done, (jj * IT + item) * 2)
                else:
                    pe.wait_ge(exp_done, (jj * IT + item) * TI + EXP_AHEAD)
                for e in range(2):
                    for jr in range(2):
                        mm = spread(ps_u if item < IT - 1 else ps_d[item % 2 - 1], ux[q], item, (jr, e))
                mm.then_inc(u_mm, 1)

            def sums(j, q, part):
                for quad in range(4):
                    d, i = part // 4, part % 4
                    st = next(s for s in range(TL) if tile_place(s) == (d, quad, i))
                    h = hb[q][:, :, st * B:(st + 1) * B, 1:].rearrange("p c b t -> p b c t")
                    mm = pe.matmul(ps_y[32 * quad:32 * quad + 32, d, :].rearrange("p (b c t) -> p b c t", b=B, t=CH),
                                   ysel[:, i, :], h, start=i == 0, stop=i == 3)
                mm.then_inc(y_mm, 1)

            def turn(j, u, m, first, last):
                for c in range(NC_):
                    pe.wait_ge(sq_done, j * NC_ + c + 1)
                    pe.matmul(ps_n[:, 0:ST], pool16[:], sq[:], start=True, stop=True).then_inc(n_mm, 1)
                    if not last:
                        if c == 0:
                            pe.wait_ge(in_a[1 - u], IN_A * (m + 1 + u))
                        decays(j + 1, 1 - u, c)
                    if SUMS_AT[c] and not first:
                        if c == 0:
                            pe.wait_ge(c_done, j * NC_)
                            pe.wait_ge(y_done, (j - 1) * DH)
                        for part in SUMS_AT[c]:
                            sums(j - 1, 1 - u, part)
                    if not last:
                        for item in SPREAD_AT[c]:
                            inputs(j + 1, 1 - u, item)

            pe.wait_ge(consts, 64)
            pe.wait_ge(in_a[0], IN_A)
            for item in range(IT):
                decays(0, 0, item)
                inputs(0, 0, item)
            turns(pe, turn)
            pe.wait_ge(c_done, NJ * NC_)
            pe.wait_ge(y_done, (NJ - 1) * DH)
            for part in range(8):
                sums(NJ - 1, 1, part)

        @block.scalar
        def _(act):
            def decay_exps(jj, q, item, tiles):
                if 0 in tiles:
                    act.wait_ge(d_mm, jj * IT + item + 1)
                for n in tiles:
                    st = item * TI + n
                    out = dA[q][:, :, st * B:(st + 1) * B, 1:].rearrange("p c b t -> p b c t")
                    act.activation(out, ps_d[item % 2][:, n // 2, n % 2, :].rearrange("p (b c t) -> p b c t", b=B, t=CH),
                                   ACT.Exp, scale=par[:, jj, st:st + 1] if isinstance(jj, int)
                                   else par[:, bass.ds(jj, 1), st:st + 1].rearrange("p a b -> p (a b)"))\
                       .then_inc(exp_done, 1)

            def turn(j, u, m, first, last):
                for c in range(NC_):
                    s = j * NC_ + c
                    act.wait_ge(scan_done, s + 1)
                    act.activation(sq[:], hb[u][:, c, :, CH], ACT.Square).then_inc(sq_done, 1)
                    act.wait_ge(n_mm, s + 1)
                    act.activation(lg[:], ps_n[:, 0:ST], ACT.Ln, scale=1.0 / (H_MAX * H_MAX), bias=tiny[:])\
                       .then_inc(lg_done, 1)
                    act.wait_ge(lg_done, s + 1)
                    act.wait_ge(last_done, s)
                    act.activation(scl[c % 2][:], lg[:], ACT.Exp, scale=-0.5).then_inc(scl_done, 1)
                    if not last:
                        decay_exps(j + 1, 1 - u, c, range(TI))

            act.preload_act_table_set(LN_EXP)
            act.sem_inc(exp_done, EXP_AHEAD)
            act.wait_ge(consts, 64)
            act.activation(par[:, :, 0:TL], par[:, :, 0:TL], ACT.Exp).then_inc(decay, 1)
            act.wait_ge(decay, 2)
            act.wait_ge(cleared, 3)
            for item in range(IT):
                decay_exps(0, 0, item, range(TI))
            turns(act, turn)

        @block.vector
        def _(dve):
            def clip(jj, q, item):
                dve.wait_ge(exp_done, (jj * IT + item) * TI + TI + EXP_AHEAD)
                own = dA[q][:, :, item * TI * B:(item + 1) * TI * B, 1:]
                dve.tensor_scalar(own, own, DA_MIN, None, ALU.max).then_inc(clip_done, 1)

            def inputs(jj, q, item):
                if item % 2 == 0 and not (isinstance(jj, int) and jj < 2):
                    dve.wait_ge(y_mm, (jj - 2) * 8 + item + 2)
                dve.wait_ge(u_mm, jj * IT + item + 1)
                for b in range(B):
                    streams = slice(item * TI * B + b, (item + 1) * TI * B, B)
                    out = hb[q][:, :, streams, 1:].rearrange("p c s t -> p s c t")
                    rep = bt[q][:, b, :].rearrange("p (c t) -> p c t", t=CH).unsqueeze(1).broadcast_to([P, TI, NC_, CH])
                    src = ps_u if item < IT - 1 else ps_d[item % 2 - 1]
                    dve.tensor_tensor(out, src[:, :, :, b * TB:(b + 1) * TB].rearrange("p k e (c t) -> p (k e) c t", t=CH),
                                      rep, ALU.mult).then_inc(inp_done, 1)

            def outputs(j, q, count):
                dve.wait_ge(y_mm, (j + 1) * 8)
                dve.wait_ge(in_x[q], count)
                dve.wait_ge(gate_done, j + 1)
                for d in range(DH):
                    dve.scalar_tensor_tensor(
                        yv[q][:, d].rearrange("p b t -> p (b t)"), xc[q][:, d].rearrange("p b t -> p (b t)"),
                        par[:, j, TL + d:TL + d + 1] if isinstance(j, int)
                        else par[:, bass.ds(j, 1), TL + d:TL + d + 1].rearrange("p a b -> p (a b)"),
                        ps_y[:, d, :], ALU.mult, ALU.add).then_inc(y_done, 1)

            def turn(j, u, m, first, last):
                for c in range(NC_):
                    s = j * NC_ + c
                    if c == 0:
                        dve.wait_ge(clip_done, (j + 1) * IT)
                        dve.wait_ge(inp_done, (j + 1) * 2 * IT)
                    dve.wait_ge(head_done, s + 1)
                    flat = lambda t: t[:, c].rearrange("p s w -> p (s w)")
                    dve.tensor_tensor_scan(flat(hb[u]), flat(dA[u]), flat(hb[u]), 0.0, ALU.mult, ALU.add)\
                       .then_inc(scan_done, 1)
                    if c >= 1 and not last:
                        clip(j + 1, 1 - u, c - 1)
                    if c == 4 and not first:
                        outputs(j - 1, 1 - u, 32 * (m + u))
                    if not last:
                        for item in INP_AT[c][:1]:
                            inputs(j + 1, 1 - u, item)
                    dve.wait_ge(scl_done, s + 1)
                    if c < NC_ - 1:
                        dve.scalar_tensor_tensor(hb[u][:, c + 1, :, 0], scl[c % 2][:], 1.0, hb[u][:, c, :, CH],
                                                 ALU.min, ALU.mult).then_inc(head_done, 1)
                    elif not last:
                        keep = par[:, j + 1, TL + DH:] if isinstance(j, int) else \
                            par[:, bass.ds(j + 1, 1), TL + DH:].rearrange("p a b -> p (a b)")
                        dve.scalar_tensor_tensor(hb[1 - u][:, 0, :, 0], scl[c % 2][:], keep, hb[u][:, c, :, CH],
                                                 ALU.min, ALU.mult).then_inc(head_done, 1)
                    if not last:
                        for item in INP_AT[c][1:]:
                            inputs(j + 1, 1 - u, item)
                        if c == NC_ - 1:
                            clip(j + 1, 1 - u, c)

            for q in range(2):
                dve.memset(dA[q][:, :, :, 0], 0.0).then_inc(cleared, 1)
            dve.memset(tiny[:], 1e-30).then_inc(cleared, 1)
            dve.memset(hb[0][:, 0, :, 0], 0.0).then_inc(head_done, 1)
            dve.wait_ge(decay, 1)
            dve.tensor_scalar(par[:, :, 0:TL], par[:, :, 0:TL], -1.0, None, ALU.mult).then_inc(decay, 1)
            for item in range(IT):
                clip(0, 0, item)
                inputs(0, 0, item)
            turns(dve, turn)
            outputs(NJ - 1, 1, 32 * (NJ // 2))

        @block.gpsimd
        def _(pool):
            def gate(j, q, count):
                pool.wait_ge(y_done, (j + 1) * DH)
                pool.wait_ge(stored[q], count)
                pool.tensor_tensor(yg[q][:], yv[q][:], zs[q][:], ALU.mult).then_inc(gate_done, 1)

            def turn(j, u, m, first, last):
                for c in range(NC_):
                    s = j * NC_ + c
                    pool.wait_ge(scl_done, s + 1)
                    if not (last and c == NC_ - 1):
                        pool.wait_ge(head_done, s + 2)
                    pool.sem_inc(seen, 1)
                    pool.tensor_scalar(capped[:], scl[c % 2][:], 1.0, None, ALU.min).then_inc(capped_done, 1)
                    pool.wait_ge(capped_done, s + 1)
                    pool.tensor_tensor(hb[u][:, c, :, CH], hb[u][:, c, :, CH], capped[:], ALU.mult)\
                        .then_inc(last_done, 1)
                    pool.wait_ge(last_done, s + 1 + LAST_AHEAD)
                    if c == 0:
                        pool.wait_ge(in_c[u], 16 * (m + 1))
                    h = hb[u][:, c, :, 1:].rearrange("p (s b) t -> p s b t", b=B)
                    rep = ct[u][:, :, c * CH:(c + 1) * CH].unsqueeze(1).broadcast_to([P, TL, B, CH])
                    pool.tensor_tensor(h, h, rep, ALU.mult).then_inc(c_done, 1)
                    if c == 6 and not first:
                        gate(j - 1, 1 - u, 16 * (m + u - 1))

            pool.sem_inc(last_done, LAST_AHEAD)
            pool.sem_inc(gate_done, GATE_AHEAD)
            turns(pool, turn)
            gate(NJ - 1, 1, 16 * (NJ // 2 - 1))


def back_to_tokens(nc, alloc, w, scr, x, mean, rstd, out, mean3, scale3, rstd3):
    sb, ps, sem = alloc
    wo, wb = sb("bt_w", [P, MI, D]), sb("bt_b", [P, D])
    ga, be = sb("bt_gamma", [P, D]), sb("bt_beta", [P, D])
    xb = sb("bt_x_beta", [P, NT, D])
    yt = [sb(f"bt_y{b}", [P, MI, BLK]) for b in range(B)]
    xt, xh, xw, nm, sc = ([sb(f"bt_{n}{b}", [P, SUB, D]) for b in range(2)] for n in ("x", "xh", "xw", "nm", "sc"))
    raw, mv = sb("bt_raw", [P, NT, 6]), sb("bt_mv", [P, NT, 2])
    tmp, shift = sb("bt_tmp", [P, 4, NT]), sb("bt_shift", [P, 2, NT])
    po = [ps(f"bt_ps{j}", [P, BLK])[:, 0:D] for j in range(SUB)]
    (weights, mm, xhat, xw_done, xb_done, summed, raw_done, mv_done, roots, root_in, step, normed, scaled, shifted,
     raw2, mv2) = (sem(f"bt_{n}") for n in "weights mm xhat xw xb summed raw mv roots root_in step normed scaled "
                                          "shifted raw2 mv2".split())
    y_in = [sem(f"bt_y_in{b}") for b in range(B)]
    x_in = [sem(f"bt_x_in{b}") for b in range(B)]
    M = B * SUB
    G = NT // SUB
    by_tile = lambda v: v[:].unsqueeze(1).broadcast_to([P, SUB, D])
    with nc.Block() as block:

        @block.sync
        def _(sp):
            for tile, name in ((wo, "out_w"), (wb, "out_b"), (ga, "gamma"), (be, "beta")):
                sp.dma_start(tile[:], w[name]).then_inc(weights, 16)
            with sp.Fori(0, NB) as i:
                for b in range(B):
                    sp.wait_ge(mm, i * M + SUB * (b + 1))
                    for h in range(HP):
                        sp.dma_start(yt[b][:, h * DH:(h + 1) * DH, :].rearrange("p d (n t) -> p d n t", t=TB),
                                     scr["yg"][h, bass.ds(i * SUB, SUB), :, :, b, :].rearrange("n p d t -> p d n t"))\
                          .then_inc(y_in[b], 16)
                    sp.wait_ge(xw_done, i * B + b + 1)
                    sp.dma_start(xt[b][:], x[b, bass.ds(i * BLK, BLK), :].rearrange("(a p) d -> p a d", p=P))\
                      .then_inc(x_in[b], 16)

        @block.tensor
        def _(pe):
            pe.sem_inc(mm, M)
            pe.wait_ge(weights, 64)
            with pe.Fori(0, NB) as i:
                for b in range(B):
                    pe.wait_ge(y_in[b], 32 * (i + 1))
                    for a in range(SUB):
                        pe.wait_ge(summed, i * M + SUB * b + a + 1 - SUB + M)
                        for k in range(MI):
                            last = pe.matmul(po[a], yt[b][:, k, a * P:(a + 1) * P], wo[:, k, :],
                                             start=k == 0, stop=k == MI - 1)
                        last.then_inc(mm, 1)

        @block.gpsimd
        def _(pool):
            pool.sem_inc(xw_done, B)
            pool.wait_ge(weights, 64)
            with pool.Fori(0, NB) as i:
                for b in range(B):
                    n = i * B + b
                    pool.wait_ge(x_in[b], 16 * (i + 1))
                    pool.tensor_tensor(xb[:, bass.ds(b * (NT // B) + i * SUB, SUB), :], xt[b][:], by_tile(be), ALU.add)\
                        .then_inc(xb_done, 1)
                    pool.wait_ge(xb_done, n + 1)
                    pool.wait_ge(summed, i * M + SUB * (b + 1))
                    pool.wait_ge(xhat, i * M + SUB * (b + 1))
                    pool.tensor_tensor(xw[b][:], xh[b][:], by_tile(wb), ALU.add).then_inc(xw_done, 1)
            for g in range(G):
                tiles = slice(g * SUB, (g + 1) * SUB)
                pool.wait_ge(scaled, g + 1)
                pool.tensor_tensor(out[:, tiles, :], sc[g % 2][:], xb[:, tiles, :], ALU.add).then_inc(shifted, 1)

        @block.vector
        def _(dve):
            dve.sem_inc(summed, M)
            dve.tensor_tensor(shift[:, 1, :], mean[:], rstd[:], ALU.mult).then_inc(root_in, 1)
            dve.wait_ge(root_in, 1)
            dve.tensor_scalar(shift[:, 0, :], shift[:, 1, :], -1.0, None, ALU.mult).then_inc(root_in, 1)
            with dve.Fori(0, NB) as i:
                for b in range(B):
                    dve.wait_ge(xw_done, (i + 1) * B + b + 1)
                    for a in range(SUB):
                        n = i * M + SUB * b + a
                        t = b * (NT // B) + i * SUB + a
                        dve.wait_ge(mm, n + 1 + M)
                        dve.tensor_tensor(out[:, bass.ds(t, 1), :].rearrange("p a d -> p (a d)"), po[a], xw[b][:, a, :],
                                          ALU.add).then_inc(summed, 1)
            dve.wait_ge(summed, NT + M)
            for t in range(NT):
                dve.bn_stats(raw[:, t, :], out[:, t, :]).then_inc(raw_done, 1)
            for t in range(NT):
                dve.wait_ge(raw_done, t + 1)
                dve.bn_aggr(mv[:, t, :], raw[:, t, :]).then_inc(mv_done, 1)
            dve.wait_ge(mv_done, NT)
            dve.wait_ge(roots, 1)
            dve.tensor_scalar(tmp[:, 1, :], tmp[:, 0, :], STD_EPS, None, ALU.add).then_inc(step, 1)
            dve.wait_ge(step, 1)
            dve.reciprocal(tmp[:, 2, :], tmp[:, 1, :]).then_inc(step, 1)
            dve.wait_ge(step, 2)
            dve.tensor_tensor(tmp[:, 3, :], tmp[:, 2, :], mv[:, :, 0], ALU.mult).then_inc(step, 1)
            dve.wait_ge(step, 3)
            dve.tensor_scalar(shift[:, 1, :], tmp[:, 3, :], -1.0, None, ALU.mult).then_inc(step, 1)

            def statistics(g):
                dve.wait_ge(shifted, g + 1)
                for t in range(g * SUB, (g + 1) * SUB):
                    dve.bn_stats(raw[:, t, :], out[:, t, :]).then_inc(raw2, 1)

            for g in range(G):
                dve.wait_ge(normed, (g + 1) * SUB)
                if g >= 2:
                    dve.wait_ge(shifted, g - 1)
                dve.tensor_tensor(sc[g % 2][:], nm[g % 2][:], by_tile(ga), ALU.mult).then_inc(scaled, 1)
                if g >= 1:
                    statistics(g - 1)
            statistics(G - 1)
            dve.wait_ge(raw2, NT)
            for t in range(NT):
                dve.bn_aggr(mv[:, t, :], raw[:, t, :]).then_inc(mv2, 1)
            dve.wait_ge(mv2, NT)
            dve.tensor_copy(mean3[:], mv[:, :, 0]).then_inc(step, 1)
            dve.tensor_scalar(tmp[:, 0, :], mv[:, :, 1], LN_EPS, None, ALU.add).then_inc(root_in, 1)
            dve.wait_ge(roots, 2)
            dve.reciprocal(rstd3[:], tmp[:, 1, :]).then_inc(step, 1)
            dve.wait_ge(root_in, 3)
            dve.reciprocal(tmp[:, 2, :], tmp[:, 0, :]).then_inc(step, 1)
            dve.wait_ge(step, 7)
            dve.tensor_tensor(tmp[:, 3, :], tmp[:, 2, :], mv[:, :, 1], ALU.mult).then_inc(step, 1)
            dve.wait_ge(step, 8)
            dve.tensor_scalar(tmp[:, 2, :], tmp[:, 3, :], STD_EPS, None, ALU.add).then_inc(root_in, 1)
            dve.wait_ge(roots, 3)
            dve.reciprocal(tmp[:, 1, :], tmp[:, 0, :]).then_inc(step, 1)
            dve.wait_ge(step, 9)
            dve.tensor_tensor(scale3[:], tmp[:, 1, :], rstd3[:], ALU.mult).then_inc(step, 1)

        @block.scalar
        def _(act):
            act.wait_ge(root_in, 2)
            with act.Fori(0, NB) as i:
                for b in range(B):
                    act.wait_ge(x_in[b], 16 * (i + 1))
                    act.wait_ge(xw_done, i * B + b + 1)
                    for a in range(SUB):
                        t = b * (NT // B) + i * SUB + a
                        act.activation(xh[b][:, a, :], xt[b][:, a, :], ACT.Identity, bias=shift[:, 0, bass.ds(t, 1)],
                                       scale=rstd[:, bass.ds(t, 1)]).then_inc(xhat, 1)
            act.wait_ge(mv_done, NT)
            act.activation(tmp[:, 0, :], mv[:, :, 1], ACT.Sqrt, scale=BESSEL).then_inc(roots, 1)
            act.wait_ge(step, 4)
            for g in range(G):
                if g >= 2:
                    act.wait_ge(scaled, g - 1)
                for a in range(SUB):
                    t = g * SUB + a
                    act.activation(nm[g % 2][:, a, :], out[:, t, :], ACT.Identity, bias=shift[:, 1, t:t + 1],
                                   scale=tmp[:, 2, t:t + 1]).then_inc(normed, 1)
            act.wait_ge(root_in, 3)
            act.activation(tmp[:, 1, :], tmp[:, 0, :], ACT.Sqrt).then_inc(roots, 1)
            act.wait_ge(root_in, 4)
            act.activation(tmp[:, 0, :], tmp[:, 2, :], ACT.Sqrt).then_inc(roots, 1)


def latents(nc, alloc, w, h_t, scr):
    sb, ps, sem = alloc
    wq, wk = sb("la_wq", [P, KD, 2 * D]), sb("la_wk", [P, 2 * D])
    wl, wv = sb("la_wl", [P, KD, P]), sb("la_wv", [P, D])
    lg, lb = sb("la_g", [P, 1]), sb("la_b", [P, 1])
    cos, sin = sb("la_cos", [P, L]), sb("la_sin", [P, L])
    avg = sb("la_avg", [P, P])
    eps = sb("la_eps", [P, 1])
    qa, qb = sb("la_qa", [P, KD, BLK]), sb("la_qb", [P, KD, BLK])
    qf = [sb(f"la_qf{u}", [P, KD, BLK]) for u in range(2)]
    parts = [sb(f"la_parts{u}", [P, 3, KD, BLK], BF16) for u in range(2)]
    lat, cen, sq, sd, rec, nrm, ln = (sb(f"la_{n}", [P, BLK]) for n in "lat cen sq sd rec nrm ln".split())
    vt = sb("la_vt", [P, SUB, NH, VW])
    pq = ps("la_pq", [P, 2, KD, BLK])
    pl, pm, pv = ps("la_pl", [P, BLK]), ps("la_pm", [P, BLK]), ps("la_pv", [P, BLK])
    po = ps("la_po", [P, BLK])[:, 0:D]
    (weights, late_weights, ready, l_mm, m_mm, v_mm, q_mm, o_mm, lat_done, cen_done, sq_done, sd_done, rec_done, nrm_done,
     ln_done, turned, q_done, hi_done, cut, lo_done, v_out) = (
        sem(f"la_{n}") for n in ("weights late_weights ready l_mm m_mm v_mm q_mm o_mm lat cen sq sd rec nrm ln turned "
                                 "q hi cut lo v_out").split())
    q_st = [sem(f"la_q_st{u}") for u in range(2)]
    v_st = sem("la_v_st")
    loads = [(wl, "wl"), (wq, "wq"), (avg, "avg")]
    late_loads = [(cos, "cos"), (sin, "sin"), (lg, "ln_g"), (lb, "ln_b"), (wk, "wk"), (wv, "wv")]
    TURNED_AHEAD, LO_AHEAD, ST = 1, 2, 3 * 16
    with nc.Block() as block:

        @block.gpsimd
        def _(pool):
            pool.memset(vt[:], 0.0).then_inc(ready, 1)
            pool.memset(eps[:], LN_EPS).then_inc(ready, 1)
            pool.wait_ge(ready, 2)
            pool.memset(vt[:, :, :, HD], 1.0).then_inc(ready, 1)
            pool.sem_inc(lo_done, LO_AHEAD)
            for b in range(B):
                with pool.Fori(0, NB) as i:
                    for u in range(2):
                        r = (b * NB + i) * 2 + u
                        hi, mid, lo = (parts[u][:, x] for x in range(3))
                        pool.wait_ge(hi_done, r + 1)
                        pool.tensor_tensor(mid, qf[u][:], hi, ALU.subtract).then_inc(cut, 1)
                        pool.wait_ge(cut, 2 * r + 1)
                        pool.tensor_tensor(qf[u][:], qf[u][:], hi, ALU.subtract).then_inc(cut, 1)
                        pool.wait_ge(cut, 2 * r + 2)
                        pool.tensor_tensor(lo, qf[u][:], mid, ALU.subtract).then_inc(lo_done, 1)

        @block.sync
        def _(sp):
            for tile, name in loads:
                sp.dma_start(tile[:], w[name]).then_inc(weights, 16)
            for tile, name in late_loads:
                sp.dma_start(tile[:], w[name]).then_inc(late_weights, 16)
            for b in range(B):
                with sp.Fori(0, NB) as i:
                    n = b * NB + i
                    col = bass.ds(b * L + i * BLK, BLK)
                    for u, name in enumerate(("qs", "ks")):
                        sp.wait_ge(lo_done, n * 2 + u + 1 + LO_AHEAD)
                        for part in range(3):
                            sp.dma_start(scr[name][part, :, col].rearrange("(k p) t -> p k t", p=P), parts[u][:, part])\
                              .then_inc(q_st[u], 16)
                        if u == 0:
                            sp.wait_ge(v_out, (n + 1) * SUB)
                            sp.dma_start(scr["v"][bass.ds(b * L + i * BLK, BLK)].rearrange("(a p) h c -> p a h c", p=P),
                                         vt[:]).then_inc(v_st, 16)
            for u in range(2):
                sp.wait_ge(q_st[u], B * NB * ST)
            sp.wait_ge(v_st, B * NB * 16)

        @block.tensor
        def _(pe):
            pe.wait_ge(weights, 16 * len(loads))
            for b in range(B):
                with pe.Fori(0, NB) as i:
                    n = b * NB + i
                    rhs = [h_t[:, k, bass.ds(b * L + i * BLK, BLK)] for k in range(KD)]
                    pe.wait_ge(lat_done, n)
                    for k in range(KD):
                        last = pe.matmul(pl[:], wl[:, k, :], rhs[k], start=k == 0, stop=k == KD - 1)
                    last.then_inc(l_mm, 1)
                    pe.wait_ge(turned, 4 * n + TURNED_AHEAD)
                    for m in range(KD):
                        for v in range(2):
                            for k in range(KD):
                                last = pe.matmul(pq[:, v, m], wq[:, k, v * D + m * P:v * D + (m + 1) * P], rhs[k],
                                                 start=k == 0, stop=k == KD - 1)
                        if m == 0:
                            pe.wait_ge(lat_done, n + 1)
                            pe.matmul(pm[:], avg[:], lat[:], start=True, stop=True).then_inc(m_mm, 1)
                    last.then_inc(q_mm, 1)
                    pe.wait_ge(sq_done, n + 1)
                    pe.matmul(pv[:], avg[:], sq[:], start=True, stop=True).then_inc(v_mm, 1)
                    pe.wait_ge(late_weights, 16 * len(late_loads))
                    pe.wait_ge(ln_done, n + 1)
                    for a in range(SUB):
                        pe.wait_ge(v_out, n * SUB + a)
                        pe.matmul(po, ln[:, a * P:(a + 1) * P], wv[:], start=True, stop=True).then_inc(o_mm, 1)
                        if a == 0:
                            pe.wait_ge(turned, 4 * n + 2 + TURNED_AHEAD)
                        v, m = a // KD, a % KD
                        last = pe.matmul(pq[:, v, m], wk[:, v * D + m * P:v * D + (m + 1) * P], ln[:],
                                         start=True, stop=True)
                    last.then_inc(q_mm, 1)

        @block.scalar
        def _(act):
            def high(u, r, n):
                act.wait_ge(q_st[u], n * ST)
                act.wait_ge(q_done, r + 1)
                act.activation(parts[u][:, 0], qf[u][:], ACT.Copy).then_inc(hi_done, 1)

            act.preload_act_table_set(SQRT_SET)
            act.wait_ge(ready, 3)
            for b in range(B):
                with act.Fori(0, NB) as i:
                    n = b * NB + i
                    act.wait_ge(l_mm, n + 1)
                    act.wait_ge(cen_done, n)
                    act.activation(lat[:], pl[:], ACT.Copy).then_inc(lat_done, 1)
                    act.wait_ge(cen_done, n + 1)
                    act.activation(sq[:], cen[:], ACT.Square).then_inc(sq_done, 1)
                    act.wait_ge(v_mm, n + 1)
                    act.activation(sd[:], pv[:], ACT.Sqrt, bias=eps[:]).then_inc(sd_done, 1)
                    act.wait_ge(v_st, n * 16)
                    for a in range(SUB):
                        act.wait_ge(o_mm, n * SUB + a + 1)
                        act.activation(vt[:, a, :, 0:HD], po.rearrange("p (h c) -> p h c", c=HD), ACT.Copy)\
                           .then_inc(v_out, 1)
                    high(0, 2 * n, n)
                    high(1, 2 * n + 1, n)

        @block.vector
        def _(dve):
            dve.sem_inc(turned, TURNED_AHEAD)
            dve.wait_ge(late_weights, 16 * len(late_loads))
            for b in range(B):
                with dve.Fori(0, NB) as i:
                    n = b * NB + i
                    over = lambda t: t[:, bass.ds(i * BLK, BLK)].unsqueeze(1).broadcast_to([P, KD, BLK])

                    def take(r):
                        dve.wait_ge(q_mm, r + 1)
                        dve.wait_ge(q_done, r)
                        dve.tensor_tensor(qa[:], pq[:, 0], over(cos), ALU.mult).then_inc(turned, 1)
                        dve.tensor_tensor(qb[:], pq[:, 1], over(sin), ALU.mult).then_inc(turned, 1)

                    def add(u, r):
                        dve.wait_ge(lo_done, r - 1 + LO_AHEAD)
                        dve.wait_ge(turned, 2 * r + 2 + TURNED_AHEAD)
                        dve.tensor_tensor(qf[u][:], qa[:], qb[:], ALU.add).then_inc(q_done, 1)

                    dve.wait_ge(m_mm, n + 1)
                    dve.wait_ge(nrm_done, n)
                    dve.tensor_tensor(cen[:], lat[:], pm[:], ALU.subtract).then_inc(cen_done, 1)
                    take(2 * n)
                    dve.wait_ge(sd_done, n + 1)
                    dve.reciprocal(rec[:], sd[:]).then_inc(rec_done, 1)
                    dve.wait_ge(rec_done, n + 1)
                    dve.tensor_tensor(nrm[:], cen[:], rec[:], ALU.mult).then_inc(nrm_done, 1)
                    dve.wait_ge(nrm_done, n + 1)
                    dve.wait_ge(q_mm, 2 * n)
                    dve.tensor_scalar(ln[:], nrm[:], lg[:], lb[:], ALU.mult, ALU.add).then_inc(ln_done, 1)
                    add(0, 2 * n)
                    take(2 * n + 1)
                    add(1, 2 * n + 1)


def attention(nc, alloc, w, scr):
    sb, ps, sem = alloc
    HQ, QB = 4, L // BLK
    G = B * (NH // HQ)
    ks = [[sb(f"at_k{p}{j}", [P, L], BF16) for j in range(HQ)] for p in range(2)]
    qs = [[sb(f"at_q{p}{j}", [P, L], BF16) for j in range(HQ)] for p in range(2)]
    vs = [sb(f"at_v{p}", [P, L // P, HQ, VW]) for p in range(2)]
    idb, dsel = sb("at_idb", [P, P], BF16), sb("at_dsel", [P, P])
    later = sb("at_later", [P, 2, P], BF16)
    pmx = sb("at_pmx", [P, 2, SUB, HQ, QB])
    neg, res = sb("at_neg", [P, 2, SUB, HQ]), sb("at_res", [P, 2, SUB, HQ])
    msp = sb("at_msp", [P, 2, SUB, HQ, 32], BF16)
    pt = [sb(f"at_p{u}", [P, HQ, BLK]) for u in range(2)]
    ob, den, lnd, rec, first, error, lack = (sb(f"at_{n}", [P, BLK]) for n in "ob den lnd rec first error lack".split())
    on = [sb(f"at_on{u}", [P, BLK]) for u in range(2)]
    p1 = [ps(f"at_p1{j}", [P, BLK]) for j in range(2)]
    p2 = [ps(f"at_p2{j}", [P, 2, BLK]) for j in range(2)]
    po = ps("at_po", [P, BLK])
    pr = ps("at_pr", [P, BLK])
    (consts, s1_mm, mx_done, cut, s_lo, t_mm, t_out, s2_mm, e_done, pv_mm, ob_done, b_mm, den_done, rec_done,
     newton, on_done) = (
        sem(f"at_{n}") for n in "consts s1 mx cut s_lo t_mm t_out s2 e pv ob b_mm den rec newton on".split())
    ones_in, zeros_in = ([sem(f"at_{n}{p}") for p in range(2)] for n in ("ones", "zeros"))
    q_in = [sem(f"at_q_in{p}") for p in range(2)]
    on_st = [sem(f"at_on_st{u}") for u in range(2)]
    units = [(qb, kt) for qb in range(QB) for kt in range(SUB * (qb + 1))]
    NU = len(units)
    last_of = {qb: SUB * (qb + 1) * (qb + 2) // 2 - 1 for qb in range(QB)}
    LAG = 21
    LEAD = NU - LAG
    LOAD = (HQ * 6 + 1) * 16
    E_AHEAD, S1_AHEAD, PV_AHEAD, FREE = 2, 2, NU + 1, 1
    maxima_at = {(last_of[qb] + 2 + LAG) % NU: (qb, (last_of[qb] + 2 + LAG) // NU) for qb in range(QB)}
    maxima_at = {n: (qb, 1 - late) for n, (qb, late) in maxima_at.items()}
    sums_at = {last_of[qb] + 2: qb for qb in range(QB - 1)}

    def maxima_out(n, more):
        return max([QB * mg + qb + 1 for k, (qb, mg) in maxima_at.items() if k < n and (more or mg == 0)] + [1])

    def groups(body):
        def of(eng):
            with eng.Fori(0, G // 2 - 1) as m:
                for p in range(2):
                    body(2 * m + p, p, m, True)
            for p in range(2):
                body(G - 2 + p, p, G // 2 - 1, p == 0)
        return of

    with nc.Block() as block:

        @block.sync
        def _(sp):
            for tile, name in ((idb, "idb"), (later, "later"), (dsel, "dsel")):
                sp.dma_start(tile[:], w[name]).then_inc(consts, 16)
            for b in range(B):
                cols = slice(b * L, (b + 1) * L)
                with sp.Fori(0, NH // HQ // 2) as m:
                    for p in range(2):
                        hq = 2 * m + p
                        g = b * (NH // HQ) + hq
                        sp.wait_ge(pv_mm, g * NU - NU + PV_AHEAD)
                        for j in range(HQ):
                            rows = bass.ds(hq * (HQ * HD) + j * HD, HD)
                            for s, r in enumerate((0, 3, 5)):
                                part = slice(r * HD, (r + 3 - s) * HD)
                                sp.dma_start(qs[p][j][part, :],
                                             scr["qs"][s, rows, cols].unsqueeze(0).broadcast_to([3 - s, HD, L]))\
                                  .then_inc(q_in[p], 16)
                                sp.dma_start(ks[p][j][part, :],
                                             scr["ks"][0:3 - s, rows, cols]).then_inc(q_in[p], 16)
                        sp.dma_start(vs[p][:], scr["v"][b * L:(b + 1) * L, bass.ds(hq * HQ, HQ), :]
                                     .rearrange("(t p) h c -> p t h c", p=P)).then_inc(q_in[p], 16)

        @block.gpsimd
        def _(pool):
            for p in range(2):
                for j in range(HQ):
                    pool.memset(qs[p][j][P - 32:P, :], 0.0).then_inc(zeros_in[p], 1)
            pool.sem_inc(on_done, FREE)
            for b in range(B):
                with pool.Fori(0, NH // HQ) as hq:
                    for qb in range(QB):
                        k = (b * (NH // HQ) + hq) * QB + qb
                        pool.wait_ge(rec_done, k + 1)
                        pool.wait_ge(on_st[qb % 2], ((b * (NH // HQ) + hq) * (QB // 2) + qb // 2) * (HQ * 16))
                        for x, (o, i0, i1, op) in enumerate(((first, ob, rec, ALU.mult), (error, den, rec, ALU.mult),
                                                             (lack, first, error, ALU.mult),
                                                             (error, first, lack, ALU.subtract))):
                            if x >= 2:
                                pool.wait_ge(newton, 4 * k + x)
                            pool.tensor_tensor(o[:], i0[:], i1[:], op).then_inc(newton, 1)
                        pool.wait_ge(newton, 4 * k + 4)
                        pool.tensor_tensor(on[qb % 2][:], first[:], error[:], ALU.add).then_inc(on_done, 1)
                        pool.wait_ge(on_done, k + 1 + FREE)
                        for j in range(HQ):
                            rows = bass.ds(hq * (HQ * HD) + j * HD, HD)
                            pool.dma_start(scr["at"][rows, b * L + qb * BLK:b * L + (qb + 1) * BLK],
                                           on[qb % 2][32 * j:32 * j + HD, :]).then_inc(on_st[qb % 2], 16)
            for u in range(2):
                pool.wait_ge(on_st[u], G * QB // 2 * HQ * 16)

        @block.tensor
        def _(pe):
            def scores(g, p, x, heads):
                qb, kt = units[x]
                a, kc = kt % SUB, kt // SUB
                q0, width = (SUB * qb + a) * P, BLK if kc < qb else (a + 1) * P
                for j in heads:
                    pe.wait_ge(mx_done, (g * NU + x) * HQ + j - 1 + S1_AHEAD)
                    last = pe.matmul(p1[j % 2][:, 0:width], qs[p][j][0:6 * HD, q0:q0 + P],
                                     ks[p][j][0:6 * HD, kc * BLK:kc * BLK + width], start=True, stop=kc < qb)
                    if kc == qb:
                        last = pe.matmul(p1[j % 2][:, a * P:width], idb[:], later[:, 0, :], start=False, stop=True)
                    last.then_inc(s1_mm, 1)

            def maxima(g, qb, spread):
                pe.wait_ge(s_lo, g * QB + qb + 1)
                if spread is not None:
                    pe.wait_ge(den_done, spread * 2)
                for a in range(SUB):
                    last = pe.matmul(pr[:, a * P:(a + 1) * P], msp[:, qb % 2, a].rearrange("p j c -> p (j c)"), idb[:],
                                     start=True, stop=True)
                last.then_inc(t_mm, 1)

            def values(g, p, n):
                qb, kt = units[n]
                dk = max(kt - SUB * qb, 0)
                pe.wait_ge(e_done, (g * NU + n) * 2 + 2 + E_AHEAD)
                if kt == 0:
                    pe.wait_ge(ob_done, g * QB + qb + FREE)
                for j in range(HQ):
                    last = pe.matmul(po[32 * j:32 * j + 32, dk * P:], vs[p][:, kt, j, :], pt[n % 2][:, j, dk * P:],
                                     start=kt == 0, stop=n == last_of[qb])
                last.then_inc(pv_mm, 1)

            def sums(g, qb, maxima_out):
                pe.wait_ge(ob_done, g * QB + qb + 1 + FREE)
                pe.wait_ge(t_out, maxima_out * HQ)
                pe.matmul(pr[:], dsel[:], ob[:], start=True, stop=True).then_inc(b_mm, 1)

            pe.sem_inc(pv_mm, PV_AHEAD)
            pe.wait_ge(consts, 48)
            pe.wait_ge(ones_in[0], HQ + 1)
            pe.wait_ge(zeros_in[0], HQ)
            pe.wait_ge(q_in[0], LOAD)
            for x in range(LEAD):
                scores(0, 0, x, range(HQ))
                for qb in range(QB):
                    if x == last_of[qb] + 2:
                        if qb:
                            pe.wait_ge(t_out, qb * HQ)
                        maxima(0, qb, None)
            pe.wait_ge(ones_in[1], HQ)
            pe.wait_ge(zeros_in[1], HQ)

            def body(g, p, m, more):
                done = 0
                for n, (qb, kt) in enumerate(units):
                    ahead = n < LAG or more
                    first = (g, p, n + LEAD) if n < LAG else (g + 1, 1 - p, n - LAG)
                    if n == LAG and more:
                        pe.wait_ge(q_in[1 - p], (m + p + 1) * LOAD)
                    if kt == 0:
                        pe.wait_ge(t_out, (g * QB + qb + 1) * HQ)
                    dk = max(kt - SUB * qb, 0)
                    for s in range(2):
                        if ahead:
                            scores(*first, (s,))
                        pe.wait_ge(e_done, (g * NU + n) * 2 + s - 1 + E_AHEAD)
                        for j in range(2 * s, 2 * s + 2):
                            last = pe.matmul(p2[s][:, j % 2, dk * P:], ks[p][j][:, kt * P:(kt + 1) * P],
                                             qs[p][j][:, qb * BLK + dk * P:(qb + 1) * BLK], start=True,
                                             stop=kt < SUB * qb)
                            if kt >= SUB * qb:
                                last = pe.matmul(p2[s][:, j % 2, dk * P:(dk + 1) * P], idb[:], later[:, 1, :],
                                                 start=False, stop=True)
                        last.then_inc(s2_mm, 1)
                    if ahead:
                        scores(*first, (2,))
                    if n >= 1:
                        values(g, p, n - 1)
                    if n in maxima_at:
                        mqb, mg = maxima_at[n]
                        if more or mg == 0:
                            maxima(g + mg, mqb, g * QB + done)
                    if n in sums_at:
                        sums(g, sums_at[n], g * QB + maxima_out(n, more))
                        done += 1
                    if ahead:
                        scores(*first, (3,))
                values(g, p, NU - 1)
                sums(g, QB - 1, g * QB + maxima_out(NU, more))
            groups(body)(pe)

        @block.scalar
        def _(act):
            def maxima(g, p, qb):
                act.wait_ge(t_mm, g * QB + qb + 1)
                for j in range(HQ):
                    act.activation(qs[p][j][6 * HD:6 * HD + 3, qb * BLK:(qb + 1) * BLK], pr[32 * j:32 * j + 3, :], ACT.Copy)\
                       .then_inc(t_out, 1)

            def take(g, qb, n):
                act.wait_ge(pv_mm, g * NU + n + 1 + PV_AHEAD)
                act.wait_ge(on_done, g * QB + qb + FREE)
                act.activation(ob[:], po[:], ACT.Copy).then_inc(ob_done, 1)

            def reciprocals(g, qb):
                act.wait_ge(b_mm, g * QB + qb + 1)
                act.wait_ge(on_done, g * QB + qb + FREE)
                act.activation(den[:], pr[:], ACT.Copy).then_inc(den_done, 1)
                act.activation(lnd[:], pr[:], ACT.Ln).then_inc(den_done, 1)
                act.wait_ge(den_done, (g * QB + qb) * 2 + 2)
                act.activation(rec[:], lnd[:], ACT.Exp, scale=-1.0).then_inc(rec_done, 1)

            act.preload_act_table_set(LN_EXP)
            act.sem_inc(e_done, E_AHEAD)
            act.sem_inc(ob_done, FREE)
            for p in range(2):
                act.wait_ge(zeros_in[p], HQ)
            for qb in range(QB):
                if last_of[qb] + 2 < LEAD:
                    maxima(0, 0, qb)

            def body(g, p, m, more):
                for n, (qb, kt) in enumerate(units):
                    dk = max(kt - SUB * qb, 0)
                    for s in range(2):
                        act.wait_ge(s2_mm, (g * NU + n) * 2 + s + 1)
                        act.wait_ge(pv_mm, g * NU + n - 1 + PV_AHEAD)
                        act.activation(pt[n % 2][:, 2 * s:2 * s + 2, dk * P:], p2[s][:, :, dk * P:], ACT.Exp,
                                       scale=float(HD) ** -0.5).then_inc(e_done, 1)
                    if n >= 1 and n - 1 in last_of.values():
                        take(g, qb - 1, n - 1)
                    if n in maxima_at and (more or maxima_at[n][1] == 0):
                        mqb, mg = maxima_at[n]
                        maxima(g + mg, p if mg == 0 else 1 - p, mqb)
                    if n in sums_at:
                        reciprocals(g, sums_at[n])
                take(g, QB - 1, NU - 1)
                reciprocals(g, QB - 1)
            groups(body)(act)

        @block.vector
        def _(dve):
            def largest(g, x):
                qb, kt = units[x]
                a, kc = kt % SUB, kt // SUB
                width = BLK if kc < qb else (a + 1) * P
                for j in range(HQ):
                    dve.wait_ge(s1_mm, (g * NU + x) * HQ + j + 1)
                    dve.tensor_reduce(pmx[:, qb % 2, a, j, kc:kc + 1], p1[j % 2][:, 0:width], AX.X, ALU.max)\
                       .then_inc(mx_done, 1)
                if x == last_of[qb]:
                    split(g, qb, x)

            def split(g, qb, x):
                u, k = qb % 2, (g * QB + qb) * 4
                dve.wait_ge(mx_done, (g * NU + x + 1) * HQ + S1_AHEAD)
                dve.tensor_reduce(neg[:, u], pmx[:, u, :, :, 0:qb + 1], AX.X, ALU.max, negate=True).then_inc(cut, 1)
                dve.wait_ge(cut, k + 1)
                dve.tensor_copy(msp[:, u, :, :, 0], neg[:, u]).then_inc(cut, 1)
                dve.wait_ge(cut, k + 2)
                dve.tensor_tensor(res[:, u], neg[:, u], msp[:, u, :, :, 0], ALU.subtract).then_inc(cut, 1)
                dve.wait_ge(cut, k + 3)
                dve.tensor_copy(msp[:, u, :, :, 1], res[:, u]).then_inc(cut, 1)
                dve.wait_ge(cut, k + 4)
                dve.tensor_tensor(msp[:, u, :, :, 2], res[:, u], msp[:, u, :, :, 1], ALU.subtract).then_inc(s_lo, 1)

            dve.sem_inc(mx_done, S1_AHEAD)
            for p in range(2):
                for j in range(HQ):
                    dve.memset(ks[p][j][P - 32:P, :], 1.0).then_inc(ones_in[p], 1)
                if p == 0:
                    dve.memset(msp[:], 0.0).then_inc(ones_in[0], 1)
            dve.wait_ge(ones_in[0], HQ + 1)
            for x in range(LEAD):
                largest(0, x)

            def body(g, p, m, more):
                for n in range(NU):
                    if n < LAG:
                        largest(g, n + LEAD)
                    elif more:
                        largest(g + 1, n - LAG)
            groups(body)(dve)


def attention_out(nc, alloc, w, scr, x1, mean3, rstd3, out, scale4):
    sb, ps, sem = alloc
    wo = sb("ao_w", [P, KD, D])
    zero = sb("ao_zero", [P, D])
    yt = [sb(f"ao_y{b}", [P, KD, BLK]) for b in range(B)]
    xhat = [sb(f"ao_xhat{b}", [P, SUB, D]) for b in range(B)]
    shift = sb("ao_shift", [P, 2, NT])
    raw, mv, tmp = sb("ao_raw", [P, NT, 6]), sb("ao_mv", [P, NT, 2]), sb("ao_tmp", [P, 2, NT])
    po = [ps(f"ao_ps{j}", [P, BLK])[:, 0:D] for j in range(SUB)]
    weights, mm, res, summed, raw_done, mv_done, step, root_in, root = (
        sem(f"ao_{n}") for n in ("weights", "mm", "res", "summed", "raw", "mv", "step", "root_in", "root"))
    zeroed, cleared, shifted = sem("ao_zeroed"), sem("ao_cleared"), sem("ao_shifted")
    y_in = [sem(f"ao_y_in{b}") for b in range(B)]
    M = B * SUB
    with nc.Block() as block:

        @block.sync
        def _(sp):
            sp.dma_start(wo[:], w["wo"]).then_inc(weights, 16)
            with sp.Fori(0, NB) as i:
                for b in range(B):
                    sp.wait_ge(mm, i * M + SUB * (b + 1))
                    sp.dma_start(yt[b][:], scr["at"][:, bass.ds(b * L + i * BLK, BLK)].rearrange("(k p) t -> p k t", p=P))\
                      .then_inc(y_in[b], 16)

        @block.gpsimd
        def _(pool):
            pool.memset(zero[:], 0.0).then_inc(zeroed, 1)
            pool.wait_ge(zeroed, 1)
            slots = NT + NE - 1
            for s in range(slots):
                pool.dma_start(scr["sorted"][s * P:(s + 1) * P, :], zero[:]).then_inc(cleared, 16)
            pool.wait_ge(cleared, slots * 16)

        @block.tensor
        def _(pe):
            pe.sem_inc(mm, M)
            pe.wait_ge(weights, 16)
            with pe.Fori(0, NB) as i:
                for b in range(B):
                    pe.wait_ge(y_in[b], 16 * (i + 1))
                    for a in range(SUB):
                        pe.wait_ge(summed, i * M + SUB * b + a + 1 - SUB + M)
                        for k in range(KD):
                            last = pe.matmul(po[a], yt[b][:, k, a * P:(a + 1) * P], wo[:, k, :],
                                             start=k == 0, stop=k == KD - 1)
                        last.then_inc(mm, 1)

        @block.vector
        def _(dve):
            dve.sem_inc(summed, M)
            dve.tensor_tensor(shift[:, 1, :], mean3[:], rstd3[:], ALU.mult).then_inc(shifted, 1)
            dve.wait_ge(shifted, 1)
            dve.tensor_scalar(shift[:, 0, :], shift[:, 1, :], -1.0, None, ALU.mult).then_inc(shifted, 1)
            with dve.Fori(0, NB) as i:
                for b in range(B):
                    for a in range(SUB):
                        n = i * M + SUB * b + a
                        t = b * (NT // B) + i * SUB + a
                        dve.wait_ge(res, n + 1)
                        dve.wait_ge(mm, n + 1 + M)
                        dve.tensor_tensor(out[:, bass.ds(t, 1), :].rearrange("p a d -> p (a d)"), po[a], xhat[b][:, a, :],
                                          ALU.add).then_inc(summed, 1)
            dve.wait_ge(summed, NT + M)
            for t in range(NT):
                dve.bn_stats(raw[:, t, :], out[:, t, :]).then_inc(raw_done, 1)
            for t in range(NT):
                dve.wait_ge(raw_done, t + 1)
                dve.bn_aggr(mv[:, t, :], raw[:, t, :]).then_inc(mv_done, 1)
            dve.wait_ge(mv_done, NT)
            dve.tensor_tensor(tmp[:, 0, :], mv[:, :, 0], mv[:, :, 0], ALU.mult).then_inc(step, 1)
            dve.wait_ge(step, 1)
            dve.tensor_tensor(tmp[:, 1, :], tmp[:, 0, :], mv[:, :, 1], ALU.add).then_inc(step, 1)
            dve.wait_ge(step, 2)
            dve.tensor_scalar(tmp[:, 0, :], tmp[:, 1, :], STD_EPS, None, ALU.add).then_inc(root_in, 1)
            dve.wait_ge(root, 1)
            dve.reciprocal(scale4[:], tmp[:, 1, :]).then_inc(step, 1)

        @block.scalar
        def _(act):
            act.wait_ge(shifted, 2)
            with act.Fori(0, NB) as i:
                for b in range(B):
                    act.wait_ge(summed, i * M + SUB * (b + 1))
                    for a in range(SUB):
                        t = b * (NT // B) + i * SUB + a
                        act.activation(xhat[b][:, a, :], x1[:, bass.ds(t, 1), :].rearrange("p a d -> p (a d)"), ACT.Identity,
                                       bias=shift[:, 0, bass.ds(t, 1)], scale=rstd3[:, bass.ds(t, 1)]).then_inc(res, 1)
            act.wait_ge(root_in, 1)
            act.activation(tmp[:, 1, :], tmp[:, 0, :], ACT.Sqrt).then_inc(root, 1)


def experts(nc, alloc, w, h_t, x1, acc, scale4, ident, scr, out):
    sb, ps, sem = alloc
    HM, HH = DHID // P, DHID // 2
    SLOTS = NT + NE - 1
    gw, gb = sb("ex_gw", [P, KD, NE]), sb("ex_gb", [P, NE])
    w1 = sb("ex_w1", [P, KD, NE * DHID])
    rows = h_t[:].rearrange("p k t -> p (k t)").rearrange("p (t d) -> p t d", d=D)
    w2 = x1[:].rearrange("p t d -> p (t d)").rearrange("p (m n) -> p m n", m=HM)
    b1, b2, wn = sb("ex_b1", [P, NE * DHID]), sb("ex_b2", [P, NE * D]), sb("ex_norm", [P, KD])
    before, ones = sb("ex_before", [P, P]), sb("ex_ones", [P, P])
    count = sb("ex_count", [P, SLOTS])
    lgt, eq, oh = (sb(f"ex_{n}", [P, NT, NE]) for n in ("lgt", "eq", "oh"))
    top, left = sb("ex_top", [P, NT]), sb("ex_left", [P, 2, NT])
    tot, inc, exc, more = (sb(f"ex_{n}", [P, NE, NT]) for n in ("tot", "inc", "exc", "more"))
    tiles, end, base = (sb(f"ex_{n}", [P, NE]) for n in ("tiles", "end", "base"))
    place, place2 = sb("ex_place", [P, NT, NE]), sb("ex_place2", [P, NT, NE])
    slot_f, past, te_f = sb("ex_slot_f", [P, NT]), sb("ex_past", [P, SLOTS, NE - 1]), sb("ex_te_f", [P, SLOTS])
    slot, te = sb("ex_slot", [P, NT], mybir.dt.int32), sb("ex_te", [P, SLOTS], mybir.dt.int32)
    hs = [sb(f"ex_hs{u}", [P, D]) for u in range(2)]
    ht = [sb(f"ex_ht{u}", [P, KD, P]) for u in range(2)]
    hid = [sb(f"ex_hid{u}", [P, DHID]) for u in range(2)]
    hid_t = sb("ex_hid_t", [P, HM, P])
    ys = [sb(f"ex_ys{u}", [P, D]) for u in range(2)]
    BACK = 4
    back = [sb(f"ex_back{u}", [P, D]) for u in range(BACK)]
    pg, prk, pt1, py = (ps(f"ex_{n}", [P, BLK]) for n in ("pg", "prk", "pt1", "py"))
    ph = [ps(f"ex_ph{n}", [P, BLK]) for n in range(2)]
    pt2 = [ps(f"ex_pt2{n}", [P, BLK]) for n in range(2)]
    (weights, w1_in, w2_in, g_mm, r_mm, gate, slots_ready, scaled, scattered, added, t1, ht_done, h_mm, hid_done, t2,
     relu, y_mm, ys_done, summed) = (
        sem(f"ex_{n}") for n in "weights w1_in w2_in g_mm r_mm gate slots scaled scattered added t1 ht h_mm hid t2 "
                                "relu y_mm ys summed".split())
    hs_in = [sem(f"ex_hs_in{u}") for u in range(2)]
    ys_st = [sem(f"ex_ys_st{u}") for u in range(2)]
    back_in = [sem(f"ex_back_in{u}") for u in range(BACK)]
    written = sem("ex_written")
    small = [(gw, "gate_w"), (gb, "gate_b"), (wn, "norm2"), (before, "before"), (ones, "ones"), (count, "count")]
    bias_in = sem("ex_bias_in")
    HID_AHEAD, RELU_AHEAD, T2_AHEAD, Y_AHEAD, YS_AHEAD = 2, 2, 2, 1, 1

    def tiles_of(eng, first, step, last):
        first()
        with eng.Fori(0, (SLOTS - 3) // 2) as m:
            for q in range(2):
                step(2 * m + 1 + q, 1 - q, m, True, True)
        for s in range(SLOTS - 2, SLOTS):
            step(s, s % 2, (s - 1) // 2, False, s + 1 < SLOTS)
        last()

    assert SLOTS % 2 == 1

    def slot_rows(name, s):
        return scr[name][bass.ds(s * P, P), :]

    with nc.Block() as block:

        @block.sync
        def _(sp):
            for tile, name in small:
                sp.dma_start(tile[:], w[name]).then_inc(weights, 16)
            for k in range(KD):
                sp.dma_start(w1[:, k, :], w["w1"][:, k, :]).then_inc(w1_in, 16)
            for tile, name in ((b1, "b1"), (b2, "b2")):
                sp.dma_start(tile[:], w[name]).then_inc(bias_in, 16)
            sp.wait_ge(added, NT)
            for m in range(HM):
                sp.dma_start(w2[:, m, :], w["w2"][:, m, :]).then_inc(w2_in, 16)
            sp.wait_ge(scattered, NT * 16)

            def load(s, u):
                sp.dma_start(hs[u][:], slot_rows("sorted", s)).then_inc(hs_in[u], 16)

            def store(s, u):
                sp.wait_ge(ys_done, s + 1 + YS_AHEAD)
                sp.dma_start(slot_rows("chosen", s), ys[u][:]).then_inc(ys_st[u], 16)

            def first():
                load(0, 0)
                load(1, 1)
                sp.wait_ge(t1, 1)
                load(2, 0)

            def step(s, u, m, two_more, one_more):
                if two_more:
                    sp.wait_ge(t1, s + 1)
                    load(s + 2, u)
                store(s - 1, 1 - u)
            tiles_of(sp, first, step, lambda: store(SLOTS - 1, 0))
            PER = 4
            for j in range(NT // PER):
                sp.wait_ge(summed, PER * (j + 1))
                b, i = j // (NB * SUB // PER), j % (NB * SUB // PER)
                sp.dma_start(out[b, i * PER * P:(i + 1) * PER * P, :].rearrange("(a p) d -> p a d", p=P),
                             acc[:, j * PER:(j + 1) * PER, :]).then_inc(written, 16)
            sp.wait_ge(written, NT // PER * 16)

        @block.gpsimd
        def _(pool):
            pool.wait_ge(slots_ready, 1)
            for t in range(NT):
                pool.wait_ge(scaled, t + 1)
                pool.indirect_dma_start(scr["sorted"][:, :], bass.IndirectOffsetOnAxis(ap=slot[:, t:t + 1], axis=0),
                                        rows[:, t, :], None).then_inc(scattered, 16)
            for u in range(2):
                pool.wait_ge(ys_st[u], (SLOTS + 1 - u) // 2 * 16 + YS_AHEAD)
            for t in range(NT):
                if t >= BACK:
                    pool.wait_ge(summed, t - BACK + 1)
                pool.indirect_dma_start(back[t % BACK][:], None, scr["chosen"][:, :],
                                        bass.IndirectOffsetOnAxis(ap=slot[:, t:t + 1], axis=0)).then_inc(back_in[t % BACK], 16)

        @block.tensor
        def _(pe):
            pe.wait_ge(weights, 16 * len(small))
            for t in range(NT):
                for k in range(KD):
                    last = pe.matmul(pg[:, t * NE:(t + 1) * NE], h_t[:, k, t * P:(t + 1) * P], gw[:, k, :],
                                     start=k == 0, stop=k == KD - 1)
            last.then_inc(g_mm, 1)
            pe.wait_ge(gate, 4 + 2 * NE)
            own = oh[:].rearrange("p t e -> p (t e)")
            pe.matmul(prk[:, 0:NT * NE], before[:], own, start=True, stop=True)
            pe.matmul(prk[:, NT * NE:2 * NT * NE], ones[:], own, start=True, stop=True).then_inc(r_mm, 1)

            def turn_rows(s, u, count):
                pe.wait_ge(hs_in[u], count)
                for k in range(KD):
                    last = pe.transpose(pt1[:, k * P:(k + 1) * P], hs[u][:, k * P:(k + 1) * P], ident[:])
                last.then_inc(t1, 1)

            def expert_of(s):
                return pe.value_load(te[0:1, bass.ds(s, 1)], min_val=0, max_val=NE - 1)

            def hidden(s, u):
                e = expert_of(s)
                pe.wait_ge(ht_done, 2 * s + 2)
                for n in range(2):
                    pe.wait_ge(hid_done, 2 * s + n - 1 + HID_AHEAD)
                    for k in range(KD):
                        last = pe.matmul(ph[n][:], ht[u][:, k, :], w1[:, k, bass.ds(e * DHID + n * HH, HH)],
                                         start=k == 0, stop=k == KD - 1)
                    last.then_inc(h_mm, 1)

            def turn_hidden(s, u):
                for n in range(2):
                    pe.wait_ge(hid_done, 2 * s + n + 1 + HID_AHEAD)
                    pe.wait_ge(relu, 2 * s + n - 1 + RELU_AHEAD)
                    for a in range(HM // 2):
                        last = pe.transpose(pt2[n][:, a * P:(a + 1) * P], hid[u][:, n * HH + a * P:n * HH + (a + 1) * P],
                                            ident[:])
                    last.then_inc(t2, 1)

            def outputs(s):
                e = expert_of(s)
                pe.wait_ge(relu, 2 * s + 2 + RELU_AHEAD)
                pe.wait_ge(ys_done, s + YS_AHEAD)
                for m in range(HM):
                    last = pe.matmul(py[:, 0:D], hid_t[:, m, :], w2[:, m, bass.ds(e * D, D)], start=m == 0,
                                     stop=m == HM - 1)
                last.then_inc(y_mm, 1)

            def first():
                turn_rows(0, 0, 16)
                hidden(0, 0)
                turn_rows(1, 1, 16)

            def step(s, u, m, two_more, one_more):
                turn_hidden(s - 1, 1 - u)
                hidden(s, u)
                if one_more:
                    turn_rows(s + 1, 1 - u, 16 * (m + 2))
                outputs(s - 1)

            def last():
                turn_hidden(SLOTS - 1, 0)
                outputs(SLOTS - 1)
            pe.wait_ge(slots_ready, 1)
            pe.wait_ge(w1_in, KD * 16)
            pe.wait_ge(w2_in, HM * 16)
            tiles_of(pe, first, step, last)

        @block.scalar
        def _(act):
            def rows_out(s, u):
                act.wait_ge(t1, s + 1)
                for k in range(KD):
                    act.activation(ht[u][:, k, :], pt1[:, k * P:(k + 1) * P], ACT.Identity, scale=wn[:, k:k + 1])\
                       .then_inc(ht_done, 1)

            def relus(s):
                act.wait_ge(y_mm, s + Y_AHEAD)
                for n in range(2):
                    act.wait_ge(t2, 2 * s + n + 1 + T2_AHEAD)
                    act.activation(hid_t[:, n * (HM // 2):(n + 1) * (HM // 2), :].rearrange("p m t -> p (m t)"), pt2[n][:],
                                   ACT.Relu).then_inc(relu, 1)

            act.sem_inc(relu, RELU_AHEAD)
            act.sem_inc(y_mm, Y_AHEAD)
            act.wait_ge(weights, 16 * len(small))

            def step(s, u, m, two_more, one_more):
                relus(s - 1)
                if one_more:
                    act.wait_ge(h_mm, 2 * s)
                    rows_out(s + 1, 1 - u)

            def first():
                rows_out(0, 0)
                rows_out(1, 1)
            tiles_of(act, first, step, lambda: relus(SLOTS - 1))

        @block.vector
        def _(dve):
            dve.wait_ge(weights, 16 * len(small))
            dve.wait_ge(g_mm, 1)
            n = 0

            def then(ins):
                nonlocal n
                n += 1
                ins.then_inc(gate, 1)
                dve.wait_ge(gate, n)

            by_tile = lambda v: v.unsqueeze(1).broadcast_to([P, NT, NE])
            swapped = lambda v: v[:].rearrange("p e t -> p t e")
            then(dve.tensor_tensor(lgt[:], pg[:, 0:NT * NE].rearrange("p (t e) -> p t e", e=NE), by_tile(gb[:]), ALU.add))
            then(dve.tensor_reduce(top[:], lgt[:], AX.X, ALU.max))
            then(dve.tensor_tensor(eq[:], lgt[:], top[:].unsqueeze(2).broadcast_to([P, NT, NE]), ALU.is_equal))
            then(dve.memset(left[:, 0, :], 1.0))
            for e in range(NE):
                then(dve.tensor_tensor(oh[:, :, e], eq[:, :, e], left[:, e % 2, :], ALU.mult))
                then(dve.tensor_tensor(left[:, (e + 1) % 2, :], left[:, e % 2, :], oh[:, :, e], ALU.subtract))
            dve.wait_ge(r_mm, 1)
            then(dve.tensor_copy(swapped(tot), prk[:, NT * NE:2 * NT * NE].rearrange("p (t e) -> p t e", e=NE)))
            then(dve.memset(more[:], 1.0))
            for e in range(NE):
                then(dve.tensor_tensor_scan(inc[:, e, :], more[:, e, :], tot[:, e, :], 0.0, ALU.mult, ALU.add))
            then(dve.tensor_tensor(exc[:], inc[:], tot[:], ALU.subtract))
            then(dve.tensor_tensor(more[:], inc[:, :, NT - 1:NT].broadcast_to([P, NE, NT]),
                                   count[:, 0:NT].unsqueeze(1).broadcast_to([P, NE, NT]), ALU.is_gt))
            then(dve.tensor_reduce(tiles[:], more[:], AX.X, ALU.add))
            then(dve.memset(base[:], 1.0))
            then(dve.tensor_tensor_scan(end[:], base[:], tiles[:], 0.0, ALU.mult, ALU.add))
            then(dve.tensor_tensor(base[:], end[:], tiles[:], ALU.subtract))
            then(dve.tensor_scalar(base[:], base[:], float(P), None, ALU.mult))
            then(dve.tensor_tensor(place[:], prk[:, 0:NT * NE].rearrange("p (t e) -> p t e", e=NE), swapped(exc), ALU.add))
            then(dve.tensor_tensor(place2[:], place[:], by_tile(base[:]), ALU.add))
            then(dve.tensor_tensor(place[:], place2[:], oh[:], ALU.mult))
            then(dve.tensor_reduce(slot_f[:], place[:], AX.X, ALU.add))
            then(dve.tensor_copy(slot[:], slot_f[:]))
            then(dve.tensor_scalar(end[:], end[:], float(P), None, ALU.mult))
            then(dve.tensor_tensor(past[:], end[:, 0:NE - 1].unsqueeze(1).broadcast_to([P, SLOTS, NE - 1]),
                                   count[:].unsqueeze(2).broadcast_to([P, SLOTS, NE - 1]), ALU.is_le))
            then(dve.tensor_reduce(te_f[:], past[:], AX.X, ALU.add))
            dve.tensor_copy(te[:], te_f[:]).then_inc(slots_ready, 1)
            for t in range(NT):
                dve.tensor_scalar(rows[:, t, :], acc[:, t, :], scale4[:, t:t + 1], None, ALU.mult).then_inc(scaled, 1)
            for t in range(NT):
                dve.wait_ge(scaled, t + 1)
                dve.tensor_tensor(acc[:, t, :], acc[:, t, :], x1[:, t, :], ALU.add).then_inc(added, 1)

            def expert_of(s):
                return dve.value_load(te[0:1, bass.ds(s, 1)], min_val=0, max_val=NE - 1)

            def hiddens(s, u):
                e = expert_of(s)
                dve.wait_ge(t2, 2 * s - 2 + T2_AHEAD)
                for n in range(2):
                    dve.wait_ge(h_mm, 2 * s + n + 1)
                    dve.tensor_tensor(hid[u][:, n * HH:(n + 1) * HH], ph[n][:], b1[:, bass.ds(e * DHID + n * HH, HH)],
                                      ALU.add).then_inc(hid_done, 1)

            def outs(s, u, count):
                e = expert_of(s)
                dve.wait_ge(ys_st[u], count + YS_AHEAD)
                dve.wait_ge(y_mm, s + 1 + Y_AHEAD)
                dve.tensor_tensor(ys[u][:], py[:, 0:D], b2[:, bass.ds(e * D, D)], ALU.add).then_inc(ys_done, 1)

            dve.sem_inc(hid_done, HID_AHEAD)
            dve.sem_inc(t2, T2_AHEAD)
            dve.sem_inc(ys_done, YS_AHEAD)
            for u in range(2):
                dve.sem_inc(ys_st[u], YS_AHEAD)
            dve.wait_ge(slots_ready, 1)
            dve.wait_ge(bias_in, 32)

            def step(s, u, m, two_more, one_more):
                hiddens(s, u)
                outs(s - 1, 1 - u, 16 * m)
            tiles_of(dve, lambda: hiddens(0, 0), step, lambda: outs(SLOTS - 1, 0, (SLOTS - 1) // 2 * 16))
            for t in range(NT):
                dve.wait_ge(back_in[t % BACK], 16 * (t // BACK + 1))
                dve.tensor_tensor(acc[:, t, :], acc[:, t, :], back[t % BACK][:], ALU.add).then_inc(summed, 1)


def program(nc, a, out):
    with ExitStack() as ctx:
        def tensors(stack):
            def sb(name, shape, dt=F32):
                return stack.enter_context(nc.sbuf_tensor(name, shape, dt))

            def ps(name, shape, dt=F32):
                return stack.enter_context(nc.psum_tensor(name, shape, dt))
            return sb, ps

        def phase(step, *args):
            with ExitStack() as own:
                used = []

                def sem(name):
                    used.append(own.enter_context(nc.semaphore(name)))
                    return used[-1]
                step(nc, (*tensors(own), sem), *args)
                with nc.Block() as block:

                    @block.gpsimd
                    def _(pool):
                        for one in used:
                            pool.sem_clear(one)

        sb, ps = tensors(ctx)
        scr = {n: nc.dram_tensor(f"scr_{n}", sh, dt, kind="Internal").ap() for n, sh, dt in
               [(n, (HP, SB_, P, DH, B, TB), F32) for n in ("zs", "xc", "bc", "yg")]
               + [(n, (HP, SB_, 3, P, DH, B, TB), BF16) for n in ("dl", "ux")]
               + [("qs", (3, D, TOK), BF16), ("ks", (3, D, TOK), BF16), ("v", (TOK, NH, VW), F32), ("at", (D, TOK), F32)]
               + [(n, (TOK + (NE - 1) * P, D), F32) for n in ("sorted", "chosen")]}
        ident = sb("ident", [P, P])
        mean, rstd = sb("mean", [P, NT]), sb("rstd", [P, NT])
        mean3, rstd3, scale3, scale4 = (sb(n, [P, NT]) for n in ("mean3", "rstd3", "scale3", "scale4"))
        with ExitStack() as features:
            xn_t = tensors(features)[0]("xn_t", [P, KD, TOK])
            with ExitStack() as tokens:
                xs, scale = tensors(tokens)[0]("in_tokens", [P, NT, D]), tensors(tokens)[0]("in_scale", [P, NT])
                phase(input_stats, a["x"], a["ident"], ident, xs, mean, rstd, scale)
                phase(to_features, "f1", xs, mean, scale, a["in_alpha"], a["in_beta"], ident, xn_t)
            phase(projections, a, xn_t, scr)
        phase(selective_scan, a, scr)
        x1 = sb("x1", [P, NT, D])
        phase(back_to_tokens, a, scr, a["x"], mean, rstd, x1, mean3, scale3, rstd3)
        with ExitStack() as features:
            h_t = tensors(features)[0]("h1_t", [P, KD, TOK])
            phase(to_features, "f2", x1, mean3, scale3, a["norm1"], None, ident, h_t)
            phase(latents, a, h_t, scr)
        phase(attention, a, scr)
        acc = sb("acc", [P, NT, D])
        phase(attention_out, a, scr, x1, mean3, rstd3, acc, scale4)
        h_t = sb("h2_t", [P, KD, TOK])
        phase(to_features, "f3", acc, None, scale4, a["norm2"], None, ident, h_t)
        phase(experts, a, h_t, x1, acc, scale4, ident, scr, out)


def host_layouts(inputs):
    g = lambda n: np.ascontiguousarray(inputs[n])
    cols = lambda v, n: np.ascontiguousarray(v.reshape(n, P).T)
    rows_t = lambda w: np.ascontiguousarray(w.T.reshape(w.shape[1] // P, P, w.shape[0]).transpose(1, 0, 2))
    a = {"x": g("L0_attn_x"), "ident": np.eye(P, dtype=np.float32)}
    a["in_alpha"], a["in_beta"] = cols(g("L0_attn_in_norm_alpha"), KD), cols(g("L0_attn_in_norm_bias"), KD)
    a["in_w"], a["in_b"] = rows_t(g("L0_attn_in_proj_w")), cols(g("L0_attn_in_proj_b"), 2 * MI)
    a["cv_w"] = np.ascontiguousarray(g("L0_attn_conv_w").reshape(MI, P, KC).transpose(1, 0, 2))
    a["cv_b"] = cols(g("L0_attn_conv_b"), MI)
    a["dt_w"], a["dt_b"] = rows_t(g("L0_attn_dt_proj_w")), cols(g("L0_attn_dt_proj_b"), MI)
    bc = g("L0_attn_x_proj_w").reshape(2, NS, DI)
    rep = np.tile(bc, (1, P // NS, 1))
    a["bc_w"] = np.ascontiguousarray(rep.reshape(2, P, MI, P).transpose(3, 2, 0, 1))
    a["bc_b"] = np.ascontiguousarray(np.tile(g("L0_attn_x_proj_b").reshape(2, NS), (1, P // NS)).T)
    wide = lambda v: np.ascontiguousarray(np.broadcast_to(v, (P,) + v.shape))
    a["out_w"], a["out_b"] = rows_t(g("L0_attn_out_proj_w")), wide(g("L0_attn_out_proj_b"))
    a["gamma"], a["beta"] = wide(g("L0_attn_norm_alpha")), wide(g("L0_attn_norm_bias"))
    a["norm1"], a["norm2"] = cols(g("L0_ffn_norm1_w"), KD), cols(g("L0_ffn_norm2_w"), KD)
    half = lambda v: np.ascontiguousarray(v.reshape(NH, 2, HD // 2, -1)[:, ::-1].reshape(D, -1))
    both = lambda v: np.concatenate([v, half(v)], 0)
    a["wq"] = rows_t(both(g("L0_ffn_Wq")))
    a["wk"] = np.ascontiguousarray(both(g("L0_ffn_Wuk")).T)
    a["wl"] = rows_t(g("L0_ffn_Wdkv"))
    a["wv"] = np.ascontiguousarray(g("L0_ffn_Wuv").T)
    a["wo"] = rows_t(g("L0_ffn_Wo"))
    a["ln_g"], a["ln_b"] = cols(g("L0_ffn_ln_g"), 1), cols(g("L0_ffn_ln_b"), 1)
    inv = (1.0 / np.float32(10000.0) ** (np.arange(HD // 2, dtype=np.float32) / np.float32(HD // 2))).astype(np.float32)
    ang = inv[np.arange(P) % (HD // 2)][:, None] * np.arange(L, dtype=np.float32)[None]
    sign = np.where(np.arange(P) % HD < HD // 2, -1.0, 1.0).astype(np.float32)[:, None]
    a["cos"], a["sin"] = np.cos(ang).astype(np.float32), (np.sin(ang) * sign).astype(np.float32)
    a["avg"] = np.full((P, P), 1.0 / LAT, np.float32)
    a["idb"] = np.eye(P).astype(mybir.dt.np(BF16))
    later = np.where(np.arange(P)[None] > np.arange(P)[:, None], -1.0e30, 0.0)
    a["later"] = np.ascontiguousarray(np.stack([later, later.T], 1).astype(mybir.dt.np(BF16)))
    a["dsel"] = np.ascontiguousarray((np.arange(P)[:, None] == 32 * (np.arange(P)[None] // 32) + HD).astype(np.float32))
    a["gate_w"], a["gate_b"] = rows_t(g("L0_ffn_gate_w")), wide(g("L0_ffn_gate_b"))
    by_expert = lambda v: np.ascontiguousarray(np.stack([rows_t(x) for x in v], 2).reshape(P, -1, NE * v.shape[1]))
    a["w1"], a["w2"] = by_expert(g("L0_ffn_W1")), by_expert(g("L0_ffn_W2"))
    a["b1"], a["b2"] = wide(g("L0_ffn_b1").reshape(-1)), wide(g("L0_ffn_b2").reshape(-1))
    a["ones"] = np.ones((P, P), np.float32)
    a["before"] = np.triu(np.ones((P, P), np.float32), 1)
    a["count"] = wide((P * np.arange(NT + NE - 1)).astype(np.float32))
    p, eye = np.arange(P), np.eye(P, dtype=np.float32)
    pick = np.stack([eye[:32, GD * i + p // NS] for i in range(4)], 1)
    a["sel"] = np.ascontiguousarray(np.tile(pick, (3, 1, 1)).astype(mybir.dt.np(BF16)))
    a["ysel"] = np.ascontiguousarray(np.stack([(np.arange(32)[None] == 8 * i + p[:, None] // NS) for i in range(4)], 1)
                                     .astype(np.float32))
    a["pool16"] = np.ascontiguousarray((p[:, None] // NS == p[None] // NS).astype(np.float32))
    a_log = g("L0_attn_A_log").reshape(HP, DH, 4, 4, GD * NS)
    order = np.array([tile_place(s) for s in range(TL)])
    par = np.zeros((P, HP, SB_, TL + DH + 1), np.float32)
    for h in range(HP):
        par[:, h, :, :TL] = a_log[h, order[:, 0], order[:, 1], order[:, 2]].T[:, None]
        par[:, h, :, TL:TL + DH] = g("L0_attn_D").reshape(HP, DH, P)[h].T[:, None]
    par[:, :, 1:, TL + DH] = 1.0
    a["par"] = np.ascontiguousarray(par.reshape(P, HP * SB_, TL + DH + 1))
    return a


def kernel(**inputs):
    import concourse.bacc as _bacc
    from concourse.bass_utils import run_bass_kernel_spmd as _run

    nc = _bacc.Bacc("TRN2", target_bir_lowering=False, num_devices=1)
    arrays, aps = {}, {}
    for name, v in host_layouts(inputs).items():
        arrays[f"in_{name}"] = v
        aps[name] = nc.dram_tensor(f"in_{name}", v.shape, mybir.dt.from_np(v.dtype), kind="ExternalInput").ap()
    out = nc.dram_tensor("out_0_dram", (B, L, D), F32, kind="ExternalOutput").ap()
    program(nc, aps, out)
    r = _run(nc, [arrays], core_ids=[0])
    return r.results[0]["out_0_dram"]
```
